# Optimizing a Trainium2 kernel written in Bass

```python
import numpy as np
import jax
import jax.numpy as jnp

def _softmax(x, axis=-1):
    return jax.nn.softmax(x, axis=axis)

def _gelu(x):
    return jax.nn.gelu(x, approximate=True)

def _silu(x):
    return jax.nn.silu(x)

def _sigmoid(x):
    return jax.nn.sigmoid(x)

def _layernorm(x, axis=-1, eps=1e-05):
    m = jnp.mean(x, axis=axis, keepdims=True)
    v = jnp.var(x, axis=axis, keepdims=True)
    return (x - m) / jnp.sqrt(v + eps)

def _scatter_add(tgt, idx, src, axis=0):
    return tgt.at[idx].add(src)

def _segment_sum(src, seg, n):
    return jax.ops.segment_sum(src, seg, n)
kernel_name = 'mk_gnn_preln_d4_gnn_r8_9b9afd'

def setup_inputs(seed: int=0):
    np.random.seed(seed)
    _w = jnp.asarray

    def _rec_inputs():
        import jax
        import jax.numpy as jnp
        _gk = jax.random.key(seed)
        x = -0.0002117 + 1 * jax.random.normal(jax.random.fold_in(_gk, 1), (1250, 512), jnp.float32)
        src = jax.random.randint(jax.random.fold_in(_gk, 2), (20000,), 0, 1250, jnp.int32)
        dst = jax.random.randint(jax.random.fold_in(_gk, 3), (20000,), 0, 1250, jnp.int32)
        _o = jnp.argsort(dst, stable=True)
        src = src[_o]
        dst = dst[_o]
        return (x, src, dst)
    x, src, dst = _rec_inputs()

    def _L0_gnn_setup():
        import jax, jax.numpy as jnp
        import numpy as np
        N, E, D = (6250, 50000, 512)
        EPS = 1e-05
        key = jax.random.key(seed)
        ks = jax.random.split(key, 5)
        scale = 1.0 / np.sqrt(D)
        x = jax.random.normal(ks[0], (N, D), dtype=jnp.float32)
        edge_index = jax.random.randint(ks[1], (2, E), 0, N, dtype=jnp.int32)
        W_l = jax.random.normal(ks[2], (D, D), dtype=jnp.float32) * scale
        b_l = jnp.zeros((D,), dtype=jnp.float32)
        W_r = jax.random.normal(ks[3], (D, D), dtype=jnp.float32) * scale
        gamma = jnp.ones((D,), dtype=jnp.float32)
        beta = jnp.zeros((D,), dtype=jnp.float32)
        return {'x': x, 'edge_index': edge_index, 'W_l': W_l, 'b_l': b_l, 'W_r': W_r, 'gamma': gamma, 'beta': beta}
    _L0_gnn_all = _L0_gnn_setup()
    _L0_gnn_in = {k: v for k, v in _L0_gnn_all.items() if k in ('W_l', 'b_l', 'W_r', 'gamma', 'beta')}
    del _L0_gnn_all

    def _L1_gnn_setup():
        import jax, jax.numpy as jnp
        import numpy as np
        B = 32
        MAXN = 256
        HEADS = 8
        DH = 64
        M = 256
        D = 512
        EPS = 1e-05
        KEPS = 1e-06

        def _batchnorm(x, g, b):
            mu = jnp.mean(x, axis=0)
            var = jnp.mean((x - mu) ** 2, axis=0)
            return (x - mu) * jax.lax.rsqrt(var + EPS) * g + b

        def _forward(x, batch, edge_index, norm1_g, norm1_b, norm2_g, norm2_b, W_conv, b_conv, Wq, Wk, Wv, Wo, proj):
            N = x.shape[0]
            E = edge_index.shape[1]
            h = x
            xn = _batchnorm(x, norm1_g, norm1_b)
            msg = xn[edge_index[0]]
            agg = jax.ops.segment_sum(msg, edge_index[1], num_segments=N)
            deg = jax.ops.segment_sum(jnp.ones((E,), x.dtype), edge_index[1], num_segments=N)
            agg = agg / jnp.maximum(deg, 1.0)[:, None]
            conv_out = jax.nn.relu(agg @ W_conv + b_conv)
            counts = jax.ops.segment_sum(jnp.ones((N,), jnp.int32), batch, num_segments=B)
            offsets = jnp.concatenate([jnp.zeros((1,), jnp.int32), jnp.cumsum(counts)[:-1]])
            pos = jnp.arange(N, dtype=jnp.int32) - offsets[batch]
            h_dense = jnp.zeros((B, MAXN, D), x.dtype).at[batch, pos].set(h)
            mask = jnp.zeros((B, MAXN), bool).at[batch, pos].set(True)

            def heads(t, W):
                return (t @ W).reshape(B, MAXN, HEADS, DH).transpose(0, 2, 1, 3)
            q, k, v = (heads(h_dense, Wq), heads(h_dense, Wk), heads(h_dense, Wv))
            scale = DH ** (-0.25)

            def phi(t, is_query):
                t = t * scale
                u = jnp.einsum('bhnd,md->bhnm', t, proj)
                diag = 0.5 * jnp.sum(t * t, axis=-1, keepdims=True)
                if is_query:
                    m_ = jnp.max(u, axis=-1, keepdims=True)
                else:
                    m_ = jnp.max(u, axis=(-2, -1), keepdims=True)
                return jnp.exp(u - diag - jax.lax.stop_gradient(m_)) / np.sqrt(M) + KEPS
            qf = phi(q, True)
            kf = phi(k, False) * mask[:, None, :, None]
            vm = v * mask[:, None, :, None]
            kv = jnp.einsum('bhnm,bhnd->bhmd', kf, vm)
            z = 1.0 / (jnp.einsum('bhnm,bhm->bhn', qf, kf.sum(axis=2)) + KEPS)
            attn = jnp.einsum('bhnm,bhmd->bhnd', qf, kv) * z[..., None]
            attn = attn.transpose(0, 2, 1, 3).reshape(B, MAXN, D) @ Wo
            h_attn = attn[batch, pos]
            return _batchnorm(conv_out + h_attn + h, norm2_g, norm2_b)
        key = jax.random.key(seed)
        ks = jax.random.split(key, 10)
        sizes = 1024 + np.arange(B) * 131 % 1025
        N = int(sizes.sum())
        E = N * 8
        batch = jnp.asarray(np.repeat(np.arange(B), sizes), dtype=jnp.int32)
        edge_index = jax.random.randint(ks[0], (2, E), 0, N, dtype=jnp.int32)
        s = 1.0 / np.sqrt(D)
        return {'x': jax.random.normal(ks[1], (N, D), jnp.float32), 'batch': batch, 'edge_index': edge_index, 'norm1_g': jnp.ones((D,), jnp.float32), 'norm1_b': jnp.zeros((D,), jnp.float32), 'norm2_g': jnp.ones((D,), jnp.float32), 'norm2_b': jnp.zeros((D,), jnp.float32), 'W_conv': jax.random.normal(ks[2], (D, D), jnp.float32) * s, 'b_conv': jnp.zeros((D,), jnp.float32), 'Wq': jax.random.normal(ks[3], (D, D), jnp.float32) * s, 'Wk': jax.random.normal(ks[4], (D, D), jnp.float32) * s, 'Wv': jax.random.normal(ks[5], (D, D), jnp.float32) * s, 'Wo': jax.random.normal(ks[6], (D, D), jnp.float32) * s, 'proj': jax.random.normal(ks[7], (M, DH), jnp.float32)}
    _L1_gnn_all = _L1_gnn_setup()
    _L1_gnn_in = {k: v for k, v in _L1_gnn_all.items() if k in ('norm1_g', 'norm1_b', 'norm2_g', 'norm2_b', 'W_conv', 'b_conv', 'Wq', 'Wk', 'Wv', 'Wo', 'proj')}
    del _L1_gnn_all

    def _L2_gnn_setup():
        import jax, jax.numpy as jnp
        import numpy as np
        N, E, H, D_IN, D_PRIME = (6250, 100000, 8, 512, 64)

        def _segment_softmax(scores, seg, num_segments):
            smax = jax.ops.segment_max(scores, seg, num_segments=num_segments)
            ex = jnp.exp(scores - smax[seg])
            denom = jax.ops.segment_sum(ex, seg, num_segments=num_segments)
            return ex / denom[seg]
        key = jax.random.key(seed)
        ks = jax.random.split(key, 6)
        x = jax.random.normal(ks[0], (N, D_IN), dtype=jnp.float32)
        edge_index = jax.random.randint(ks[1], (2, E), 0, N)
        Ws = jax.random.normal(ks[2], (H, D_IN, D_PRIME), dtype=jnp.float32) * 0.05
        Wb = jax.random.normal(ks[3], (H, D_PRIME), dtype=jnp.float32) * 0.05
        a_w = jax.random.normal(ks[4], (H, 2 * D_PRIME), dtype=jnp.float32) * 0.05
        a_b = jax.random.normal(ks[5], (H,), dtype=jnp.float32) * 0.05
        return dict(x=x, edge_index=edge_index, Ws=Ws, Wb=Wb, a_w=a_w, a_b=a_b)
    _L2_gnn_all = _L2_gnn_setup()
    _L2_gnn_in = {k: v for k, v in _L2_gnn_all.items() if k in ('Ws', 'Wb', 'a_w', 'a_b')}
    del _L2_gnn_all

    def _L3_gnn_setup():
        import jax, jax.numpy as jnp
        import numpy as np
        N = 2500
        E = 31250
        B = 128
        Fin = 512
        Fqk = 512
        Fv = 512
        H = 8
        key = jax.random.key(seed)
        k1, k2, k3, k4 = jax.random.split(key, 4)
        x = jax.random.normal(k1, (N, Fin), dtype=jnp.float32)
        batch = jnp.sort(jax.random.randint(k2, (N,), 0, B)).astype(jnp.int32)
        ei = jax.random.randint(k3, (2, E), 0, N).astype(jnp.int32)
        W = jax.random.normal(k4, (Fin, 2 * Fqk + Fv), dtype=jnp.float32) / np.sqrt(Fin).astype(np.float32)
        return {'x': x, 'batch': batch, 'ei': ei, 'W': W}
    _L3_gnn_all = _L3_gnn_setup()
    _L3_gnn_in = {k: v for k, v in _L3_gnn_all.items() if k in ('W',)}
    del _L3_gnn_all
    return {'x': x, 'src': src, 'dst': dst, 'L0_gnn_W_l': _L0_gnn_in['W_l'], 'L0_gnn_b_l': _L0_gnn_in['b_l'], 'L0_gnn_W_r': _L0_gnn_in['W_r'], 'L0_gnn_gamma': _L0_gnn_in['gamma'], 'L0_gnn_beta': _L0_gnn_in['beta'], 'L1_gnn_norm1_g': _L1_gnn_in['norm1_g'], 'L1_gnn_norm1_b': _L1_gnn_in['norm1_b'], 'L1_gnn_norm2_g': _L1_gnn_in['norm2_g'], 'L1_gnn_norm2_b': _L1_gnn_in['norm2_b'], 'L1_gnn_W_conv': _L1_gnn_in['W_conv'], 'L1_gnn_b_conv': _L1_gnn_in['b_conv'], 'L1_gnn_Wq': _L1_gnn_in['Wq'], 'L1_gnn_Wk': _L1_gnn_in['Wk'], 'L1_gnn_Wv': _L1_gnn_in['Wv'], 'L1_gnn_Wo': _L1_gnn_in['Wo'], 'L1_gnn_proj': _L1_gnn_in['proj'], 'L2_gnn_Ws': _L2_gnn_in['Ws'], 'L2_gnn_Wb': _L2_gnn_in['Wb'], 'L2_gnn_a_w': _L2_gnn_in['a_w'], 'L2_gnn_a_b': _L2_gnn_in['a_b'], 'L3_gnn_W': _L3_gnn_in['W']}

def reference(x, src, dst, L0_gnn_W_l, L0_gnn_b_l, L0_gnn_W_r, L0_gnn_gamma, L0_gnn_beta, L1_gnn_norm1_g, L1_gnn_norm1_b, L1_gnn_norm2_g, L1_gnn_norm2_b, L1_gnn_W_conv, L1_gnn_b_conv, L1_gnn_Wq, L1_gnn_Wk, L1_gnn_Wv, L1_gnn_Wo, L1_gnn_proj, L2_gnn_Ws, L2_gnn_Wb, L2_gnn_a_w, L2_gnn_a_b, L3_gnn_W):
    import jax
    import jax.numpy as jnp

    def _L0_gnn_ref(x, edge_index, W_l, b_l, W_r, gamma, beta):
        import jax, jax.numpy as jnp
        import numpy as np
        N, E, D = (6250, 50000, 512)
        EPS = 1e-05
        n = x.shape[0]
        src, dst = (edge_index[0], edge_index[1])
        agg = jax.ops.segment_sum(x[src], dst, num_segments=n)
        cnt = jax.ops.segment_sum(jnp.ones((src.shape[0],), x.dtype), dst, num_segments=n)
        mean_agg = agg / jnp.maximum(cnt, 1.0)[:, None]
        h = mean_agg @ W_l.T + b_l + x @ W_r.T
        mu = jnp.mean(h, axis=0)
        var = jnp.var(h, axis=0)
        h = (h - mu) * jax.lax.rsqrt(var + EPS) * gamma + beta
        return jax.nn.relu(h) + x

    def _L1_gnn_ref(x, batch, edge_index, norm1_g, norm1_b, norm2_g, norm2_b, W_conv, b_conv, Wq, Wk, Wv, Wo, proj):
        import jax, jax.numpy as jnp
        import numpy as np
        B = 32
        MAXN = 256
        HEADS = 8
        DH = 64
        M = 256
        D = 512
        EPS = 1e-05
        KEPS = 1e-06

        def _batchnorm(x, g, b):
            mu = jnp.mean(x, axis=0)
            var = jnp.mean((x - mu) ** 2, axis=0)
            return (x - mu) * jax.lax.rsqrt(var + EPS) * g + b

        def _forward(x, batch, edge_index, norm1_g, norm1_b, norm2_g, norm2_b, W_conv, b_conv, Wq, Wk, Wv, Wo, proj):
            N = x.shape[0]
            E = edge_index.shape[1]
            h = x
            xn = _batchnorm(x, norm1_g, norm1_b)
            msg = xn[edge_index[0]]
            agg = jax.ops.segment_sum(msg, edge_index[1], num_segments=N)
            deg = jax.ops.segment_sum(jnp.ones((E,), x.dtype), edge_index[1], num_segments=N)
            agg = agg / jnp.maximum(deg, 1.0)[:, None]
            conv_out = jax.nn.relu(agg @ W_conv + b_conv)
            counts = jax.ops.segment_sum(jnp.ones((N,), jnp.int32), batch, num_segments=B)
            offsets = jnp.concatenate([jnp.zeros((1,), jnp.int32), jnp.cumsum(counts)[:-1]])
            pos = jnp.arange(N, dtype=jnp.int32) - offsets[batch]
            h_dense = jnp.zeros((B, MAXN, D), x.dtype).at[batch, pos].set(h)
            mask = jnp.zeros((B, MAXN), bool).at[batch, pos].set(True)

            def heads(t, W):
                return (t @ W).reshape(B, MAXN, HEADS, DH).transpose(0, 2, 1, 3)
            q, k, v = (heads(h_dense, Wq), heads(h_dense, Wk), heads(h_dense, Wv))
            scale = DH ** (-0.25)

            def phi(t, is_query):
                t = t * scale
                u = jnp.einsum('bhnd,md->bhnm', t, proj)
                diag = 0.5 * jnp.sum(t * t, axis=-1, keepdims=True)
                if is_query:
                    m_ = jnp.max(u, axis=-1, keepdims=True)
                else:
                    m_ = jnp.max(u, axis=(-2, -1), keepdims=True)
                return jnp.exp(u - diag - jax.lax.stop_gradient(m_)) / np.sqrt(M) + KEPS
            qf = phi(q, True)
            kf = phi(k, False) * mask[:, None, :, None]
            vm = v * mask[:, None, :, None]
            kv = jnp.einsum('bhnm,bhnd->bhmd', kf, vm)
            z = 1.0 / (jnp.einsum('bhnm,bhm->bhn', qf, kf.sum(axis=2)) + KEPS)
            attn = jnp.einsum('bhnm,bhmd->bhnd', qf, kv) * z[..., None]
            attn = attn.transpose(0, 2, 1, 3).reshape(B, MAXN, D) @ Wo
            h_attn = attn[batch, pos]
            return _batchnorm(conv_out + h_attn + h, norm2_g, norm2_b)
        return _forward(x, batch, edge_index, norm1_g, norm1_b, norm2_g, norm2_b, W_conv, b_conv, Wq, Wk, Wv, Wo, proj)

    def _L2_gnn_ref(x, edge_index, Ws, Wb, a_w, a_b):
        import jax, jax.numpy as jnp
        import numpy as np
        N, E, H, D_IN, D_PRIME = (6250, 100000, 8, 512, 64)

        def _segment_softmax(scores, seg, num_segments):
            smax = jax.ops.segment_max(scores, seg, num_segments=num_segments)
            ex = jnp.exp(scores - smax[seg])
            denom = jax.ops.segment_sum(ex, seg, num_segments=num_segments)
            return ex / denom[seg]
        v_src, v_tgt = (edge_index[0], edge_index[1])
        n = x.shape[0]
        outs = []
        for h in range(Ws.shape[0]):
            Wx = x @ Ws[h] + Wb[h]
            d = Wx.shape[-1]
            s = Wx[v_tgt] @ a_w[h, :d] + Wx[v_src] @ a_w[h, d:] + a_b[h]
            s = jax.nn.leaky_relu(s, negative_slope=0.2)
            alpha = _segment_softmax(s, v_tgt, n)
            outs.append(jax.ops.segment_sum(alpha[:, None] * Wx[v_src], v_tgt, num_segments=n))
        return jnp.stack(outs, axis=1).reshape(n, -1)

    def _L3_gnn_ref(x, batch, ei, W):
        import jax, jax.numpy as jnp
        import numpy as np
        N = 2500
        E = 31250
        B = 128
        Fin = 512
        Fqk = 512
        Fv = 512
        H = 8
        src, dest = (ei[0], ei[1])
        n = x.shape[0]
        Fh = Fqk // H
        Fhv = Fv // H
        scaling = float(Fh) ** (-0.5)
        qkv = x @ W
        q, k, v = jnp.split(qkv, [Fqk, 2 * Fqk], axis=-1)
        q = (q * scaling).reshape(n, H, Fh)
        k = k.reshape(n, H, Fh)
        v = v.reshape(n, H, Fhv)
        qs = q[src]
        ks = k[dest]
        vs = v[dest]
        aw = jnp.einsum('ehf,ehf->eh', qs, ks)
        m = jax.ops.segment_max(aw, src, num_segments=n)
        e = jnp.exp(aw - m[src])
        denom = jax.ops.segment_sum(e, src, num_segments=n)
        alpha = e / denom[src]
        out = jax.ops.segment_sum(alpha[:, :, None] * vs, src, num_segments=n)
        return out.reshape(n, Fv)
    edge_index = jnp.stack([src, dst])
    batch0 = jnp.zeros((1250,), jnp.int32)
    h = jnp.maximum(_layernorm(x, axis=-1), 0.0)
    x = x + _L0_gnn_ref(h, edge_index, L0_gnn_W_l, L0_gnn_b_l, L0_gnn_W_r, L0_gnn_gamma, L0_gnn_beta)
    h = jnp.maximum(_layernorm(x, axis=-1), 0.0)
    x = x + _L1_gnn_ref(h, batch0, edge_index, L1_gnn_norm1_g, L1_gnn_norm1_b, L1_gnn_norm2_g, L1_gnn_norm2_b, L1_gnn_W_conv, L1_gnn_b_conv, L1_gnn_Wq, L1_gnn_Wk, L1_gnn_Wv, L1_gnn_Wo, L1_gnn_proj)
    h = jnp.maximum(_layernorm(x, axis=-1), 0.0)
    x = x + _L2_gnn_ref(h, edge_index, L2_gnn_Ws, L2_gnn_Wb, L2_gnn_a_w, L2_gnn_a_b)
    h = jnp.maximum(_layernorm(x, axis=-1), 0.0)
    x = x + _L3_gnn_ref(h, batch0, edge_index, L3_gnn_W)
    return x

_drawn_inputs = setup_inputs


def setup_inputs(seed=0):
    import zlib

    import numpy as np

    out = dict(_drawn_inputs(seed))
    spreads = {'L0_gnn_b_l': (0.0, 2.0),
     'L0_gnn_gamma': (1.0, 0.2),
     'L0_gnn_beta': (0.0, 0.1),
     'L1_gnn_norm1_g': (1.0, 0.6),
     'L1_gnn_norm1_b': (0.0, 0.317),
     'L1_gnn_norm2_g': (1.0, 0.2),
     'L1_gnn_norm2_b': (0.0, 0.1),
     'L1_gnn_b_conv': (0.0, 0.364)}
    factors = {'L1_gnn_Wq': 26.376,
     'L1_gnn_Wk': 3.422,
     'L1_gnn_Wv': 28.504,
     'L1_gnn_Wo': 29.488,
     'L1_gnn_proj': 28.624,
     'L2_gnn_Wb': 3.352,
     'L2_gnn_a_w': 2.999,
     'L2_gnn_a_b': 59.748}
    for name, (base, spread) in spreads.items():
        noise = np.random.default_rng([zlib.crc32(name.encode()), seed]).standard_normal(out[name].shape)
        drawn = base * np.exp(spread * noise) if base else spread * noise
        out[name] = jnp.asarray(drawn.astype(out[name].dtype))
    for name, factor in factors.items():
        out[name] = (out[name] * factor).astype(out[name].dtype)
    return out
```

```python
from contextlib import ExitStack

import concourse.bass as bass
from concourse import mybir

ALU = mybir.AluOpType
ACT = mybir.ActivationFunctionType
AX = mybir.AxisListType.X
F32, BF16, F16 = mybir.dt.float32, mybir.dt.bfloat16, mybir.dt.float16
I32, I16 = mybir.dt.int32, mybir.dt.int16
RMAX = bass.bass_isa.ReduceOp.max

N, E, D = 1250, 20000, 512
TILES, ROWS = 10, 125
KD = D // 128
CHUNK = 125
PAIRS = E // (2 * CHUNK)
H, DH = 8, 64
VA = DH + 1
NPERF, MPERF = 256, 256
PB = NPERF // 128
EPS, KEPS = 1e-5, 1e-6
NEG = -1e30
CAP = 1e30
S3 = 11
TINY = 1e-30
HEAD_HALF = 5
SIZE = {F32: 4, I32: 4, BF16: 2, F16: 2, I16: 2}


def wide_matmul(pe, ps, rows, lhsT, rhs, start, stop):
    for lo, hi in ((0, 512), (512, 1024), (1024, N)):
        mm = pe.matmul(ps[0:rows, lo:hi], lhsT, rhs[:, lo:hi], start=start, stop=stop)
    return mm


def block_at(ps, rows, t):
    at = 512 * (t // 4) + ROWS * (t % 4)
    return ps[0:rows, at:at + ROWS]


def blocks_out(copy, dst, ps, rows):
    banks = ps[0:rows, :].rearrange("p (b c) -> p b c", b=3)
    copy(dst[:, 0:1000].rearrange("p (b c) -> p b c", b=2), banks[:, 0:2, 0:500])
    return copy(dst[:, 1000:N], banks[:, 2, 0:250])


def gnn_program(nc, a, out, layers=4):
    ctx = ExitStack()
    with ctx:
        def sb(name, shape, dt=F32):
            return ctx.enter_context(nc.sbuf_tensor(name, shape, dt))

        def sem(name):
            return ctx.enter_context(nc.semaphore(name))

        x_nm = sb("x_nm", [128, TILES, D])
        cnt = sb("cnt", [128, TILES, N], I16)
        cntT = sb("cntT", [128, TILES, N], I16)
        ident = sb("ident", [128, 128])
        sel = sb("sel", [TILES, TILES, 128])
        zero_bf = sb("zero_bf", [1, 512], BF16)
        deg_col = sb("deg_col", [128, TILES])
        row_sb = sb("row_sb", [TILES, 2, ROWS])
        bn6 = sb("bn6", [128, TILES, 6])
        mv = sb("mv", [128, TILES, 2])
        rstd = sb("rstd", [128, TILES])
        nbias = sb("nbias", [128, TILES])
        vec = sb("vec", [128, 8, KD])
        bl_c, ga0_c, be0_c, g1_c, b1_c, g2_c, b2_c, bc_c = [vec[:, i, :] for i in range(8)]
        bns = sb("bns", [128, KD, 3, 6])
        bnv = sb("bnv", [128, KD, 2])
        scl = sb("scl", [128, KD])
        shf = sb("shf", [128, KD])
        scl1 = sb("scl1", [128, KD])
        shf1 = sb("shf1", [128, KD])
        bounds_i = sb("bounds_i", [1, 3 * TILES], I32)
        var_eps = sb("var_eps", [128, TILES])
        root = sb("root", [128, TILES])
        half_c = sb("half_c", [128, 1])
        proj_nat = sb("proj_nat", [128, PB, 2 * DH])
        projT = sb("projT", [128, MPERF])
        qdiag = sb("qdiag", [128, H, PB])
        kdiag = sb("kdiag", [128, H, PB])
        qmax = sb("qmax", [128, H, PB])
        kmax = sb("kmax", [128, H])
        kmaxa = sb("kmaxa", [128, H])
        qbias = sb("qbias", [128, H, PB])
        kbias = sb("kbias", [128, H, PB])
        pz = sb("pz", [128, H, PB])
        tcol = sb("tcol", [128, H, TILES])
        bcol = sb("bcol", [128, H, TILES])
        b08 = sb("b08", [128, H, TILES])
        b02 = sb("b02", [128, H, TILES])
        bst = sb("bst", [128, 2, TILES])
        mcol = sb("mcol", [128, 2, TILES])
        zcol = sb("zcol", [128, 2, TILES])
        ucol = sb("ucol", [128, 2, 2, TILES])
        rden = sb("rden", [128, 2, TILES])
        head_sum = sb("head_sum", [128, 2, HEAD_HALF, DH])
        AW = 31584
        arena = sb("arena", [128, AW])

        def region(off, shape, dt=F32):
            n = 1
            for s in shape:
                n *= s
            words = (n * SIZE[dt] + 3) // 4
            assert off + words <= AW, (off, words)
            v = arena[:, off:off + words]
            if dt != F32:
                v = v.bitcast(dt)
            if len(shape) == 2:
                v = v.rearrange("p (a b) -> p a b", a=shape[0])
            if len(shape) == 3:
                v = v.rearrange("p (a b c) -> p a b c", a=shape[0], b=shape[1])
            return v

        h_nm = region(0, [TILES, D])
        hT = region(5120, [KD, N])
        rdeg_b = region(10120, [N])
        pos_b = region(11370, [N])
        G = 12620
        hot_src = [region(G + 625 * i, [N], BF16) for i in range(2)]
        hot_dst = [region(G + 1250 + 64 * i, [128], BF16) for i in range(2)]
        cnt_f = [region(G + 1400 + 1250 * i, [N]) for i in range(2)]
        iota_h = region(G + 3900, [N], F16)
        e_raw = region(G + 4530, [2, 2 * CHUNK], I32)
        e_f = region(G + 5030, [2, 2 * CHUNK])
        e_col = region(G + 5530, [2, PAIRS, 2])
        pair_mm = region(G + 5900, [2])
        pair_row = arena[0:1, G + 6000:G + 6160]
        tile_lo = arena[0:1, G + 6160:G + 6170]
        up_row = arena[0:1, G + 6200:G + 6280]
        down_row = arena[0:1, G + 6280:G + 6360]
        flag = [arena[0:1, G + 6400 + 800 * i:G + 7200 + 800 * i].rearrange("p (t q) -> p t q", t=TILES)
                for i in range(2)]
        bnd = arena[0:1, G + 8000:G + 8080].rearrange("p (r t) -> p r t", r=8)
        aggT = region(G, [KD, N])
        yT = region(G + 5000, [KD, N])
        w_nat = [region(G + 5000 + 2048 * i, [KD, D]) for i in range(2)]
        w_a = region(G + 10300, [KD, D])
        w_b = region(G + 12348, [KD, D])
        cntT_f = [region(G + 14400 + 1250 * i, [N]) for i in range(2)]
        oT = region(G + 16900, [KD, NPERF])
        wo = region(G + 14400, [KD, D])
        wv = region(G, [KD, D])
        qf = region(G, [H, PB * MPERF])
        attn = region(G, [PB, D])
        attnT = region(G + 1024, [KD, NPERF])
        sq = region(G + 4096, [2, KD * NPERF])
        kf = region(G + 4096, [H, PB * MPERF])
        qkT = region(G + 8192, [2, KD * NPERF])
        qfT = region(G + 10300, [H, PB * NPERF])
        v_perf = region(G + 17924, [PB, H, VA])
        kv_perf = region(G + 8192, [H, PB, VA])
        b_row = [region(1250 * i, [N]) for i in range(2)]
        u_row = [region(2500 + 2500 * i, [N]) for i in range(2)]
        w_row = [region(3750 + 2500 * i, [N]) for i in range(2)]
        prob = [region(7500 + 1250 * i, [N]) for i in range(2)]
        mask = region(10120, [TILES, N], BF16)
        v_aug = region(16370, [TILES, H, VA])
        score = [region(21570 + 1250 * i, [N]) for i in range(3)]
        wb_row = region(21570, [D])
        ab_row = region(22100, [H])
        ex2 = [region(25320 + 1250 * i, [N]) for i in range(2)]
        w_gat = region(27820, [KD, H, DH])
        a_mul = region(29868, [2, H, DH])
        junk = region(27820, [TILES // 2, N], BF16)
        a_rows = region(25320, [H, 2 * DH])
        q_slot = [region(1250 * i, [N]) for i in range(2)]
        k_slot = [region(2500 + 1250 * i, [N]) for i in range(2)]
        ex3 = [region(5000 + 1250 * i, [N]) for i in range(2)]
        w_k, w_q, w_v = [region(10120 + 2048 * i, [KD, D]) for i in range(3)]
        q_all = region(21570, [KD, N])
        k_all = region(26570, [KD, N])

        psW = [ctx.enter_context(nc.psum_tensor(f"wide{i}", [128, 1536], F32)) for i in range(2)]
        small = ctx.enter_context(nc.psum_tensor("small", [128, 1024], F32))
        psS = [small[:, 0:512], small[:, 512:1024]]

        def acc_view(ps):
            return ps[0:ROWS, 0:1024].rearrange("p (u c) -> p u c", u=2)[:, :, 0:HEAD_HALF * VA].rearrange(
                "p u (t d) -> p u t d", d=VA)

        names = """x_in edges_in vec_in w_in edges_f32 edges_turned edge_cols pair_bounds bounds_turned bounds_row
            pair_cols bounds_set consts_set hot0_made hot1_made hot0_free hot1_free tile_counted counts_f32
            counts_i16 counts_turning counts_turn_read deg_turned deg_row_out deg_wide deg_rows
            ln_ready h_made h_turned hT_made x_plus_h cT_f32 cT_used agg_read w_turned w_turn_read y_full y_out
            y_stats y_scaled z_turned x_updated bn1_ready qk_full qk_out v_full v_out proj_turned proj_out sq_made
            diag_full diag_out uk_full uk_max kmax_all kbias_set uk2_full kf_exp kf_made uq_full uq_max qf_exp
            qf_made qf_turned qfT_out kv_full kv_out at_full at_out at_turned atT_out o_full o_out conv_full
            conv_out sum_made wx_full wx_out wx_mul ab_cols mask_made b_picked b_turned b_rows b_wide b_out
            uw_cols uw_turned uw_rows uw_wide uw_out score_made ex_made prob_made prob_used acc_read
            proj3_full proj3_out v3_full v3_out slots_set s0_full s1_full s0_free s1_free
            waits_taken var_ready root_out m_rows ones_set dve_done stored phase_done pool_done""".split()
        S = {n: sem(n) for n in names}
        block = ctx.enter_context(nc.Block())

        class Order:

            def __init__(self, eng, semaphore):
                self.eng, self.sem, self.base, self.n = eng, semaphore, 0, 0

            def __call__(self, ins):
                self.n += 1
                ins.then_inc(self.sem, 1)
                self.eng.wait_ge(self.sem, self.base + self.n)

        def phase_end(eng, n):
            eng.drain().then_inc(S["phase_done"], 1)
            eng.wait_ge(S["phase_done"], 5 * n)

        @block.sync
        def _(sp):
            col = "(k p) -> p k"
            sp.dma_start(e_raw[0:PAIRS, 0, :], a["dst"].rearrange("(p e) -> p e", p=PAIRS)).then_inc(S["edges_in"], 16)
            sp.dma_start(e_raw[0:PAIRS, 1, :], a["src"].rearrange("(p e) -> p e", p=PAIRS)).then_inc(S["edges_in"], 16)
            for t in range(0, TILES, 5):
                sp.dma_start(x_nm[0:ROWS, t:t + 5, :], a["x"].rearrange("(t p) f -> p t f", p=ROWS)[:, t:t + 5, :]).then_inc(S["x_in"], 16)
            with nc.allow_non_contiguous_dma(reason="feature vectors as columns, 4 bytes a partition"):
                for i, name in enumerate(["L0_gnn_b_l", "L0_gnn_gamma", "L0_gnn_beta", "L1_gnn_norm1_g",
                                          "L1_gnn_norm1_b", "L1_gnn_norm2_g", "L1_gnn_norm2_b", "L1_gnn_b_conv"]):
                    sp.dma_start(vec[:, i, :], a[name].rearrange(col, p=128)).then_inc(S["vec_in"], 16)
            for r in range(2):
                sp.dma_start(proj_nat[:, :, DH * r:DH * r + DH],
                             a["L1_gnn_proj"].rearrange("(b m) d -> m b d", m=128)).then_inc(S["vec_in"], 16)
            rows = "(k p) n -> p k n"
            phase_end(sp, 1)
            sp.dma_start(w_nat[0], a["L0_gnn_W_l"].rearrange(rows, p=128)).then_inc(S["w_in"], 16)
            sp.dma_start(w_nat[1], a["L0_gnn_W_r"].rearrange(rows, p=128)).then_inc(S["w_in"], 16)
            phase_end(sp, 2)
            sp.dma_start(w_a, a["L1_gnn_Wq"].rearrange(rows, p=128)).then_inc(S["w_in"], 16)
            sp.dma_start(w_b, a["L1_gnn_Wk"].rearrange(rows, p=128)).then_inc(S["w_in"], 16)
            sp.dma_start(wv, a["L1_gnn_Wv"].rearrange(rows, p=128)).then_inc(S["w_in"], 16)
            sp.dma_start(wo, a["L1_gnn_Wo"].rearrange(rows, p=128)).then_inc(S["w_in"], 16)
            phase_end(sp, 3)
            sp.dma_start(w_a, a["L1_gnn_W_conv"].rearrange(rows, p=128)).then_inc(S["w_in"], 16)
            phase_end(sp, 4)
            for k in range(KD):
                sp.dma_start(w_gat[:, k, :, :], a["L2_gnn_Ws"][:, 128 * k:128 * k + 128, :].rearrange("h p d -> p h d")).then_inc(S["w_in"], 16)
            sp.dma_start(wb_row, a["L2_gnn_Wb"].rearrange("h d -> (h d)").partition_broadcast(128)).then_inc(S["w_in"], 16)
            sp.dma_start(a_rows.rearrange("p h d -> p (h d)"), a["L2_gnn_a_w"].rearrange("h d -> (h d)").partition_broadcast(128)).then_inc(S["w_in"], 16)
            sp.dma_start(ab_row, a["L2_gnn_a_b"].partition_broadcast(128)).then_inc(S["w_in"], 16)
            phase_end(sp, 5)
            phase_end(sp, 6)
            w3 = a["L3_gnn_W"].rearrange(rows, p=128)
            sp.dma_start(w_k, w3[:, :, D:2 * D]).then_inc(S["w_in"], 16)
            sp.dma_start(w_q, w3[:, :, 0:D]).then_inc(S["w_in"], 16)
            sp.dma_start(w_v, w3[:, :, 2 * D:3 * D]).then_inc(S["w_in"], 16)
            phase_end(sp, 7)
            phase_end(sp, 8)
            sp.dma_start(out.rearrange("(t p) f -> p t f", p=ROWS), x_nm[0:ROWS, :, :]).then_inc(S["stored"], 16)
            sp.wait_ge(S["stored"], 16)

        @block.gpsimd
        def _(pool):
            done = Order(pool, S["pool_done"])
            pool.memset(ident[:, :], 1.0)
            pool.memset(sel[:, :, :], 1.0)
            pool.memset(half_c[:, :], 0.5)
            done(pool.memset(zero_bf[:, :], 0.0))
            done(pool.affine_select(out=ident[:, :], in_=ident[:, :], compare_op=ALU.is_equal, fill=0.0, base=0,
                                    pattern=[[-1, 128]], channel_multiplier=1))
            done(pool.affine_select(out=sel[:, :, :], in_=sel[:, :, :], compare_op=ALU.is_equal, fill=0.0, base=0,
                                    pattern=[[-1, TILES], [0, 128]], channel_multiplier=1))
            many = dict(allow_small_or_imprecise_dtypes=True, channel_multiplier=0)
            done(pool.iota(tile_lo, pattern=[[ROWS, TILES]], base=0, **many))
            done(pool.iota(up_row, pattern=[[1, PAIRS]], base=1, **many))
            done(pool.iota(down_row, pattern=[[-1, PAIRS]], base=PAIRS, **many))
            pool.iota(iota_h[:, :], pattern=[[1, N]], base=0, **many).then_inc(S["consts_set"], 1)
            for t in range(TILES):
                pool.wait_ge(S["counts_f32"], t + 1)
                pool.tensor_copy(cnt[0:ROWS, t, :], cnt_f[t % 2][0:ROWS, :]).then_inc(S["counts_i16"], 1)
            phase_end(pool, 1)

            def widen(base):
                for n in range(2 * TILES):
                    if n >= 2:
                        pool.wait_ge(S["cT_used"], base + n - 1)
                    pool.tensor_copy(cntT_f[n % 2][0:ROWS, :], cntT[0:ROWS, n % TILES, :]).then_inc(S["cT_f32"], 1)

            widen(0)
            pool.wait_ge(S["hT_made"], KD)
            pool.tensor_tensor(x_nm[0:ROWS, :, :], x_nm[0:ROWS, :, :], h_nm[0:ROWS, :, :], ALU.add).then_inc(S["x_plus_h"], 1)
            phase_end(pool, 2)
            pool.wait_ge(S["uk_max"], H)
            pool.partition_all_reduce(kmaxa[:, :], kmax[:, :], 128, RMAX).then_inc(S["kmax_all"], 1)
            phase_end(pool, 3)
            widen(2 * TILES)
            phase_end(pool, 4)
            pool.memset(v_aug[0:ROWS, :, :, DH], 1.0)
            for t in range(TILES):
                pool.wait_ge(S["wx_out"], t + 1)
                if t >= 1:
                    pool.wait_ge(S["ab_cols"], t)
                for r in range(2):
                    m = pool.tensor_tensor(a_mul[0:ROWS, r, :, :], v_aug[0:ROWS, t, :, 0:DH],
                                           a_rows[0:ROWS, :, DH * r:DH * r + DH], ALU.mult)
                m.then_inc(S["wx_mul"], 1)
            phase_end(pool, 5)
            phase_end(pool, 6)
            pool.memset(v_aug[0:ROWS, :, :, DH], 1.0)
            phase_end(pool, 7)
            for b in range(2):
                o = pool.memset(k_slot[b][DH:VA, :], 1.0)
            o.then_inc(S["ones_set"], 1)
            phase_end(pool, 8)

        @block.scalar
        def _(act):
            def copy(dst, src, **k):
                return act.activation(dst, src, ACT.Copy, **k)

            for t in range(TILES + 1):
                if t < TILES:
                    act.wait_ge(S["tile_counted"], t + 1)
                    if t >= 2:
                        act.wait_ge(S["counts_i16"], t - 1)
                        act.wait_ge(S["counts_turning"], 3 * (t - 1))
                    copy(cnt_f[t % 2][0:ROWS, :], psW[t % 2][0:ROWS, 0:N], accum_out=deg_col[0:ROWS, t:t + 1]).then_inc(S["counts_f32"], 1)
                if t >= 1:
                    for r, (lo, hi) in enumerate(((0, 4), (4, 8), (8, 10))):
                        n = 3 * (t - 1) + r
                        act.wait_ge(S["counts_turning"], n + 1)
                        src = psS[n % 2][0:ROWS, 0:(hi - lo) * ROWS].rearrange("p (b c) -> p b c", b=hi - lo)
                        copy(cntT[0:ROWS, lo:hi, (t - 1) * ROWS:t * ROWS], src).then_inc(S["counts_turn_read"], 1)
            act.wait_ge(S["deg_turned"], 1)
            copy(row_sb[:, 0, :], psS[1][0:TILES, 0:ROWS]).then_inc(S["deg_row_out"], 1)

            roots = [0]

            def take_root(rows, cols):
                roots[0] += 1
                act.wait_ge(S["var_ready"], roots[0])
                act.activation(root[0:rows, 0:cols], var_eps[0:rows, 0:cols], ACT.Sqrt).then_inc(S["root_out"], 1)

            def relu_norm(l):
                take_root(ROWS, TILES)
                act.wait_ge(S["ln_ready"], l + 1)
                for t in range(TILES):
                    act.activation(h_nm[0:ROWS, t, :], x_nm[0:ROWS, t, :], ACT.Relu, bias=nbias[0:ROWS, t:t + 1],
                                   scale=rstd[0:ROWS, t:t + 1]).then_inc(S["h_made"], 1)

            phase_end(act, 1)
            relu_norm(0)
            for n in range(2 * KD):
                act.wait_ge(S["w_turned"], n + 1)
                w = (w_a, w_b)[n // KD]
                copy(w[:, n % KD, :], psS[n % 2][:, :]).then_inc(S["w_turn_read"], 1)
            for f in range(KD):
                act.wait_ge(S["y_full"], f + 1)
                act.activation(yT[:, f, :], psW[f % 2][:, 0:N], ACT.Identity, bias=bl_c[:, f:f + 1]).then_inc(S["y_out"], 1)
            take_root(128, KD)
            act.wait_ge(S["y_stats"], 1)
            for f in range(KD):
                act.activation(yT[:, f, :], yT[:, f, :], ACT.Relu, bias=shf[:, f:f + 1], scale=scl[:, f:f + 1]).then_inc(S["y_scaled"], 1)
            phase_end(act, 2)
            if layers >= 2:
                relu_norm(1)
                take_root(128, KD)
                for r in range(2):
                    act.wait_ge(S["qk_full"], r + 1)
                    act.mul(qkT[:, r, :], psW[r][:, 0:KD * NPERF], DH ** -0.25).then_inc(S["qk_out"], 1)
                act.wait_ge(S["proj_turned"], 1)
                copy(projT[:, :], psW[1][:, 1024:1024 + MPERF]).then_inc(S["proj_out"], 1)
                act.wait_ge(S["kbias_set"], 1)
                for h in range(H):
                    act.wait_ge(S["uk2_full"], h + 1)
                    for b in range(PB):
                        e = act.activation(kf[:, h, MPERF * b:MPERF * b + MPERF], psW[h % 2][:, MPERF * b:MPERF * b + MPERF],
                                           ACT.Exp, bias=kbias[:, h, b:b + 1])
                    e.then_inc(S["kf_exp"], 1)
                for h in range(H):
                    act.wait_ge(S["uq_max"], h + 1)
                    for b in range(PB):
                        e = act.activation(qf[:, h, MPERF * b:MPERF * b + MPERF], psW[h % 2][:, MPERF * b:MPERF * b + MPERF],
                                           ACT.Exp, bias=qbias[:, h, b:b + 1])
                    e.then_inc(S["qf_exp"], 1)
                for h in range(H):
                    act.wait_ge(S["qf_turned"], h + 1)
                    copy(qfT[:, h, :], psS[h % 2][:, :]).then_inc(S["qfT_out"], 1)
                act.wait_ge(S["at_turned"], 1)
                copy(attnT.rearrange("p k n -> p (k n)"), psW[0][:, 0:KD * NPERF]).then_inc(S["atT_out"], 1)
                act.wait_ge(S["o_full"], 1)
                copy(oT.rearrange("p k n -> p (k n)"), psW[1][:, 0:KD * NPERF]).then_inc(S["o_out"], 1)
                phase_end(act, 3)
                for f in range(KD):
                    act.wait_ge(S["conv_full"], f + 1)
                    act.activation(yT[:, f, :], psW[f % 2][:, 0:N], ACT.Relu, bias=bc_c[:, f:f + 1]).then_inc(S["conv_out"], 1)
                take_root(128, KD)
                act.wait_ge(S["y_stats"], 2)
                for f in range(KD):
                    act.activation(yT[:, f, :], yT[:, f, :], ACT.Identity, bias=shf[:, f:f + 1], scale=scl[:, f:f + 1]).then_inc(S["y_scaled"], 1)
            else:
                phase_end(act, 3)
            phase_end(act, 4)
            if layers >= 3:
                relu_norm(2)
                phase_end(act, 5)

                def rows_out(h, b):
                    act.wait_ge(S["b_turned"], h + 1)
                    copy(row_sb[:, 0, :], psS[1][0:TILES, 0:ROWS]).then_inc(S["b_rows"], 1)
                    act.wait_ge(S["b_wide"], h + 1)
                    blocks_out(copy, b_row[b][0:ROWS, :], psW[0], ROWS).then_inc(S["b_out"], 1)
                    act.wait_ge(S["uw_turned"], h + 1)
                    copy(row_sb[:, :, :].rearrange("p r c -> p (r c)"), psS[1][0:TILES, 0:2 * ROWS]).then_inc(S["uw_rows"], 1)
                    for r, dst in enumerate((u_row[b], w_row[b])):
                        act.wait_ge(S["uw_wide"], 2 * h + r + 1)
                        blocks_out(copy, dst[0:ROWS, :], psW[0], ROWS).then_inc(S["uw_out"], 1)

                def exps(h, b):
                    for t in range(TILES):
                        n = h * TILES + t
                        act.wait_ge(S["score_made"], n + 1)
                        if isinstance(h, int) and h == 0 and t < 2:
                            pass
                        else:
                            act.wait_ge(S["prob_made"], n - 1)
                        act.activation(ex2[t % 2][0:ROWS, :], score[t % 2][0:ROWS, :], ACT.Exp,
                                       bias=b02[0:ROWS, h, t:t + 1]).then_inc(S["ex_made"], 1)

                rows_out(0, 0)
                rows_out(1, 1)
                exps(0, 0)
                with act.Fori(0, H // 2 - 1) as g:
                    rows_out(2 * g + 2, 0)
                    exps(2 * g + 1, 1)
                    rows_out(2 * g + 3, 1)
                    exps(2 * g + 2, 0)
                exps(H - 1, 1)
            else:
                phase_end(act, 5)
            phase_end(act, 6)
            if layers >= 4:
                relu_norm(3)
                for n in range(2 * KD):
                    act.wait_ge(S["proj3_full"], n + 1)
                    dst, s = ((k_all, 1.0), (q_all, DH ** -0.5))[n // KD]
                    act.mul(dst[:, n % KD, :], psW[n % 2][:, 0:N], s).then_inc(S["proj3_out"], 1)
                phase_end(act, 7)

                def slots(h, b, g):
                    act.wait_ge(S["prob_used"], (H + h - 1) * TILES)
                    copy(q_slot[b][0:DH, :], q_all[DH * b:DH * b + DH, g, :])
                    copy(k_slot[b][0:DH, :], k_all[DH * b:DH * b + DH, g, :]).then_inc(S["slots_set"], 1)

                def head(h, b):
                    act.wait_ge(S["s1_full"], S3 * h + 6)
                    copy(row_sb[:, 0, :], psW[1][0:TILES, 0:ROWS]).then_inc(S["s1_free"], 1)
                    act.wait_ge(S["s0_full"], S3 * h + 6)
                    blocks_out(lambda d, s: act.mul(d, s, -1.0), q_slot[b][DH:VA, :], psW[0][DH:VA, :], 1).then_inc(S["s0_free"], 1)
                    for t in range(TILES):
                        act.wait_ge(S[f"s{t % 2}_full"], S3 * h + 7 + t // 2)
                        act.wait_ge(S["prob_made"], H * TILES + h * TILES + t - 1)
                        act.activation(ex3[t % 2][0:ROWS, :], psW[t % 2][0:ROWS, 0:N], ACT.Exp).then_inc(S[f"s{t % 2}_free"], 1)

                slots(0, 0, 0)
                slots(1, 1, 0)
                head(0, 0)
                with act.Fori(0, H // 2 - 1) as g:
                    slots(2 * g + 2, 0, g + 1)
                    head(2 * g + 1, 1)
                    slots(2 * g + 3, 1, g + 1)
                    head(2 * g + 2, 0)
                head(H - 1, 1)
            else:
                phase_end(act, 7)
            phase_end(act, 8)

        @block.vector
        def _(dve):
            done = Order(dve, S["dve_done"])
            tt, ts, stt = dve.tensor_tensor, dve.tensor_scalar, dve.scalar_tensor_tensor

            def take_wait():
                dve.sem_inc(S["waits_taken"], 1)

            dve.wait_ge(S["edges_in"], 32)
            dve.tensor_copy(e_f[0:PAIRS, :, :], e_raw[0:PAIRS, :, :]).then_inc(S["edges_f32"], 1)
            dve.wait_ge(S["edges_f32"], 1)
            dve.tensor_reduce(pair_mm[0:PAIRS, 0:1], e_f[0:PAIRS, 0, :], AX, ALU.max)
            dve.tensor_reduce(pair_mm[0:PAIRS, 1:2], e_f[0:PAIRS, 0, :], AX, ALU.min).then_inc(S["pair_bounds"], 1)
            dve.wait_ge(S["edges_turned"], 1)
            src = psS[0][0:ROWS, 0:4 * PAIRS].rearrange("e (s g p) -> e s p g", s=2, g=2)
            for s in range(2):
                c = dve.tensor_copy(e_col[0:ROWS, s, :, :], src[:, s, :, :])
            c.then_inc(S["edge_cols"], 1)
            dve.wait_ge(S["bounds_turned"], 1)
            dve.wait_ge(S["consts_set"], 1)
            done(dve.tensor_copy(pair_row, psS[1][0:1, 0:2 * PAIRS]))
            shape = [1, TILES, PAIRS]
            largest = pair_row[:, 0:PAIRS].unsqueeze(1).to_broadcast(shape)
            smallest = pair_row[:, PAIRS:2 * PAIRS].unsqueeze(1).to_broadcast(shape)
            up, down = (r.unsqueeze(1).to_broadcast(shape) for r in (up_row, down_row))
            lo, hi, tile_hi, n_pairs, incl, excl, rest = (bnd[:, i, :] for i in range(7))
            done(ts(tile_hi, tile_lo, float(ROWS), None, ALU.add))
            done(tt(flag[0], largest, tile_lo.unsqueeze(2).to_broadcast(shape), ALU.is_ge))
            done(tt(flag[1], smallest, tile_hi.unsqueeze(2).to_broadcast(shape), ALU.is_lt))
            done(tt(flag[0], flag[0], flag[1], ALU.mult))
            done(tt(flag[1], flag[0], up, ALU.mult))
            done(dve.tensor_reduce(hi, flag[1], AX, ALU.max))
            done(tt(flag[1], flag[0], down, ALU.mult))
            done(dve.tensor_reduce(rest, flag[1], AX, ALU.max))
            done(ts(lo, rest, -1.0, float(PAIRS), ALU.mult, ALU.add))
            done(ts(hi, hi, 1.0, None, ALU.max))
            done(ts(rest, hi, -1.0, None, ALU.add))
            done(tt(lo, lo, rest, ALU.min))
            done(tt(n_pairs, hi, lo, ALU.subtract))
            done(dve.tensor_copy(incl, n_pairs))
            for t in range(1, TILES):
                done(tt(incl[:, t:t + 1], incl[:, t - 1:t], n_pairs[:, t:t + 1], ALU.add))
            done(tt(excl, incl, n_pairs, ALU.subtract))
            for i, r in enumerate((lo, excl, incl)):
                c = dve.tensor_copy(bounds_i[:, i * TILES:(i + 1) * TILES], r)
            c.then_inc(S["bounds_set"], 1)
            dve.wait_ge(S["bounds_set"], 1)
            for g in range(2):
                dve.sem_inc(S[f"hot{g}_free"], 1)
            for t in range(TILES):
                first, start, end = (dve.value_load(bounds_i[0:1, i * TILES + t:i * TILES + t + 1], min_val=m,
                                                    max_val=TILES * PAIRS - (1 - m) if i else PAIRS - 1)
                                     for i, m in ((0, 0), (1, 0), (2, 1)))
                with dve.Fori(start, end) as n:
                    k = nc.s_assert_within(n - start + first, 0, PAIRS - 1,
                                           skip_runtime_bounds_check_because="first + (end - start) <= PAIRS by construction")
                    for g in range(2):
                        dve.wait_ge(S[f"hot{g}_free"], n + 1)
                        ts(hot_src[g][0:ROWS, :], iota_h[0:ROWS, :], e_col[0:ROWS, 1, k, g:g + 1], None, ALU.is_equal)
                        ts(hot_dst[g][0:ROWS, 0:ROWS], iota_h[0:ROWS, t * ROWS:(t + 1) * ROWS],
                           e_col[0:ROWS, 0, k, g:g + 1], None, ALU.is_equal).then_inc(S[f"hot{g}_made"], 1)

            roots = [0]

            def rsqrt(dst, var):
                rows, cols = dst.shape
                ts(var_eps[0:rows, 0:cols], var, EPS, None, ALU.add).then_inc(S["var_ready"], 1)
                roots[0] += 1
                dve.wait_ge(S["root_out"], roots[0])
                done(dve.reciprocal(dst, root[0:rows, 0:cols]))

            def ln_stats(l):
                if l == 0:
                    dve.wait_ge(S["x_in"], 32)
                for t in range(TILES):
                    s = dve.bn_stats(bn6[0:ROWS, t, :], x_nm[0:ROWS, t, :])
                done(s)
                for t in range(TILES):
                    s = dve.bn_aggr(mv[0:ROWS, t, :], bn6[0:ROWS, t, :])
                done(s)
                rsqrt(rstd[0:ROWS, :], mv[0:ROWS, :, 1])
                stt(nbias[0:ROWS, :], mv[0:ROWS, :, 0], -1.0, rstd[0:ROWS, :], ALU.mult, ALU.mult).then_inc(S["ln_ready"], 1)
                for k in range(KD):
                    dve.wait_ge(S["h_turned"], KD * l + k + 1)
                    blocks_out(dve.tensor_copy, hT[:, k, :], psW[k % 2], 128).then_inc(S["hT_made"], 1)

            def bn_over_nodes(src, ready, gamma, beta, s_out, b_out):
                for f in range(KD):
                    ready(f)
                    for c, (lo, hi) in enumerate(((0, 512), (512, 1024), (1024, N))):
                        s = dve.bn_stats(bns[:, f, c, :], src[:, f, lo:hi])
                done(s)
                for f in range(KD):
                    s = dve.bn_aggr(bnv[:, f, :], bns[:, f, :, :].rearrange("p c s -> p (c s)"))
                done(s)
                rsqrt(s_out[:, :], bnv[:, :, 1])
                done(tt(s_out[:, :], s_out[:, :], gamma, ALU.mult))
                done(tt(b_out[:, :], bnv[:, :, 0], s_out[:, :], ALU.mult))
                return tt(b_out[:, :], beta, b_out[:, :], ALU.subtract)

            def add_back(base):
                for t in range(TILES):
                    dve.wait_ge(S["z_turned"], base + t + 1)
                    tt(x_nm[0:ROWS, t, :], x_nm[0:ROWS, t, :], psS[t % 2][0:ROWS, :], ALU.add).then_inc(S["x_updated"], 1)

            def sums(h, b, layer, ps):
                dve.wait_ge(S["prob_used"], (layer * H + h + 1) * TILES)
                acc = acc_view(ps)
                rd = rden[0:ROWS, b, :]
                rd2 = rd.rearrange("p (u t) -> p u t", u=2)
                done(ts(rd2, acc[:, :, :, DH], TINY, None, ALU.max))
                done(dve.reciprocal(rd, rd))
                done(tt(head_sum[0:ROWS, :, :, :], acc[:, :, :, 0:DH], rd2.unsqueeze(3).to_broadcast([ROWS, 2, HEAD_HALF, DH]), ALU.mult))
                xs = x_nm[0:ROWS, :, :].rearrange("p t (h d) -> p t h d", h=H)[:, :, h, :]
                tt(xs, xs, head_sum[0:ROWS, :, :, :].rearrange("p u t d -> p (u t) d"), ALU.add).then_inc(S["acc_read"], 1)

            dve.wait_ge(S["deg_wide"], 1)
            done(blocks_out(dve.tensor_copy, pos_b, psW[0], 128))
            ts(rdeg_b, pos_b, 1.0, None, ALU.max).then_inc(S["deg_rows"], 1)
            dve.wait_ge(S["deg_rows"], 1)
            done(dve.reciprocal(rdeg_b, rdeg_b))
            done(ts(pos_b, pos_b, 1.0, None, ALU.min))
            phase_end(dve, 1)
            ln_stats(0)
            for k in range(KD):
                dve.wait_ge(S["cT_used"], TILES * (k // 2 + 1))
                tt(aggT[:, k, :], psW[k % 2][:, 0:N], rdeg_b, ALU.mult).then_inc(S["agg_read"], 1)
            dve.wait_ge(S["vec_in"], 16 * 10)
            bn_over_nodes(yT, lambda f: dve.wait_ge(S["y_out"], f + 1), ga0_c, be0_c, scl, shf).then_inc(S["y_stats"], 1)
            dve.wait_ge(S["x_plus_h"], 1)
            add_back(0)
            phase_end(dve, 2)
            if layers >= 2:
                ln_stats(1)
                bn_over_nodes(hT, lambda f: dve.wait_ge(S["hT_made"], KD + f + 1), g1_c, b1_c, scl1, shf1).then_inc(S["bn1_ready"], 1)
                done(dve.memset(v_perf[:, :, :, DH:VA], 1.0))
                dve.wait_ge(S["v_full"], 1)
                for b in range(PB):
                    c = dve.tensor_copy(v_perf[:, b, :, 0:DH], psS[b][:, :].rearrange("p (h d) -> p h d", h=H))
                c.then_inc(S["v_out"], 1)
                dve.wait_ge(S["qk_out"], 2)
                tt(sq, qkT, qkT, ALU.mult).then_inc(S["sq_made"], 1)
                dve.wait_ge(S["diag_full"], 1)
                for par in range(2):
                    for r, dst in enumerate((qdiag, kdiag)):
                        c = dve.tensor_copy(dst[:, par:H:2, :], psS[par][:, r * H:(r + 1) * H].rearrange("p (h b) -> p h b", b=PB))
                c.then_inc(S["diag_out"], 1)
                for h in range(H):
                    dve.wait_ge(S["uk_full"], h + 1)
                    dve.tensor_reduce(kmax[:, h:h + 1], psW[h % 2][:, 0:PB * MPERF], AX, ALU.max).then_inc(S["uk_max"], 1)
                dve.wait_ge(S["kmax_all"], 1)
                dve.wait_ge(S["diag_out"], 1)
                stt(kbias[:, :, :], kdiag[:, :, :], -1.0, kmaxa[:, :].unsqueeze(2).to_broadcast([128, H, PB]),
                    ALU.mult, ALU.subtract).then_inc(S["kbias_set"], 1)
                for h in range(H):
                    dve.wait_ge(S["kf_exp"], h + 1)
                    ts(kf[:, h, :], kf[:, h, :], MPERF ** -0.5, KEPS, ALU.mult, ALU.add).then_inc(S["kf_made"], 1)
                for h in range(H):
                    dve.wait_ge(S["uq_full"], h + 1)
                    done(dve.tensor_reduce(qmax[:, h, :], psW[h % 2][:, 0:PB * MPERF].rearrange("p (b m) -> p b m", b=PB), AX, ALU.max))
                    stt(qbias[:, h, :], qdiag[:, h, :], -1.0, qmax[:, h, :], ALU.mult, ALU.subtract).then_inc(S["uq_max"], 1)
                for h in range(H):
                    dve.wait_ge(S["qf_exp"], h + 1)
                    ts(qf[:, h, :], qf[:, h, :], MPERF ** -0.5, KEPS, ALU.mult, ALU.add).then_inc(S["qf_made"], 1)
                for h in range(H):
                    dve.wait_ge(S["kv_full"], h + 1)
                    dve.tensor_copy(kv_perf[:, h, :, :], psW[h % 2][:, 0:PB * VA].rearrange("p (b d) -> p b d", b=PB)).then_inc(S["kv_out"], 1)
                for h in range(H):
                    dve.wait_ge(S["at_full"], h + 1)
                    at = psW[h % 2][:, 512:512 + PB * VA].rearrange("p (b d) -> p b d", b=PB)
                    done(ts(pz[:, h, :], at[:, :, DH], KEPS, None, ALU.add))
                    done(dve.reciprocal(pz[:, h, :], pz[:, h, :]))
                    tt(attn[:, :, h * DH:(h + 1) * DH], at[:, :, 0:DH], pz[:, h, :].unsqueeze(2).to_broadcast([128, PB, DH]),
                       ALU.mult).then_inc(S["at_out"], 1)
                phase_end(dve, 3)
                for k in range(KD):
                    dve.wait_ge(S["cT_used"], 2 * TILES + TILES * (k // 2 + 1))
                    done(stt(aggT[:, k, :], psW[k % 2][:, 0:N], scl1[:, k:k + 1], rdeg_b, ALU.mult, ALU.mult))
                    stt(aggT[:, k, :], pos_b, shf1[:, k:k + 1], aggT[:, k, :], ALU.mult, ALU.add).then_inc(S["agg_read"], 1)
                for f in range(KD):
                    dve.wait_ge(S["conv_out"], f + 1)
                    done(tt(yT[:, f, :], yT[:, f, :], hT[:, f, :], ALU.add))
                    tt(yT[:, f, 0:NPERF], yT[:, f, 0:NPERF], oT[:, f, :], ALU.add)
                    done(ts(yT[:, f, NPERF:N], yT[:, f, NPERF:N], oT[:, f, NPERF - 1:NPERF], None, ALU.add))
                bn_over_nodes(yT, lambda f: None, g2_c, b2_c, scl, shf).then_inc(S["y_stats"], 1)
                add_back(TILES)
            else:
                phase_end(dve, 3)
            phase_end(dve, 4)
            if layers >= 3:
                ln_stats(2)
                dve.wait_ge(S["w_in"], 16 * (7 + KD + 3))
                for t in range(TILES):
                    dve.wait_ge(S["wx_full"], t + 1)
                    tt(v_aug[0:ROWS, t, :, 0:DH], psS[t % 2][0:ROWS, :].rearrange("p (h d) -> p h d", h=H),
                       wb_row[0:ROWS, :].rearrange("p (h d) -> p h d", h=H), ALU.add).then_inc(S["wx_out"], 1)
                    dve.wait_ge(S["wx_mul"], t + 1)
                    dve.tensor_reduce(tcol[0:ROWS, :, t], a_mul[0:ROWS, 0, :, :], AX, ALU.add)
                    dve.tensor_reduce(bcol[0:ROWS, :, t], a_mul[0:ROWS, 1, :, :], AX, ALU.add).then_inc(S["ab_cols"], 1)
                dve.wait_ge(S["ab_cols"], TILES)
                tt(tcol[0:ROWS, :, :], tcol[0:ROWS, :, :], ab_row[0:ROWS, :].unsqueeze(2).to_broadcast([ROWS, H, TILES]), ALU.add)
                ts(b08[0:ROWS, :, :], bcol[0:ROWS, :, :], 0.8, None, ALU.mult)
                ts(b02[0:ROWS, :, :], bcol[0:ROWS, :, :], 0.2, None, ALU.mult)
                done(ts(mask[0:ROWS, :, :], cnt[0:ROWS, :, :], 0.0, NEG, ALU.is_equal, ALU.mult))
                phase_end(dve, 5)

                PREP_STEPS, SUM_STEPS = 4, 3

                def prep(h, b):
                    dve.tensor_copy(bst[0:ROWS, b, :], bcol[0:ROWS, h, :]).then_inc(S["b_picked"], 1)
                    dve.wait_ge(S["b_out"], h + 1)
                    take_wait()
                    for t in range(TILES):
                        r = dve.tensor_tensor_reduce(junk[0:ROWS, t % 5, :], b_row[b][0:ROWS, :], mask[0:ROWS, t, :], 1.0, 2 * NEG,
                                                     ALU.add, ALU.max, mcol[0:ROWS, b, t:t + 1])
                        if t % 5 == 4:
                            done(r)
                            take_wait()
                    done(tt(zcol[0:ROWS, b, :], mcol[0:ROWS, b, :], tcol[0:ROWS, h, :], ALU.add))
                    done(stt(mcol[0:ROWS, b, :], zcol[0:ROWS, b, :], 0.2, zcol[0:ROWS, b, :], ALU.mult, ALU.max))
                    tt(ucol[0:ROWS, b, 0, :], tcol[0:ROWS, h, :], mcol[0:ROWS, b, :], ALU.subtract)
                    stt(ucol[0:ROWS, b, 1, :], tcol[0:ROWS, h, :], 0.2, mcol[0:ROWS, b, :], ALU.mult, ALU.subtract).then_inc(S["uw_cols"], 1)

                def tiles(h, b):
                    dve.wait_ge(S["uw_out"], 2 * h + 2)
                    for t in range(TILES + 1):
                        n = h * TILES + t
                        if t < TILES:
                            stt(score[t % 2][0:ROWS, :], u_row[b][0:ROWS, :], b08[0:ROWS, h, t:t + 1], w_row[b][0:ROWS, :],
                                ALU.add, ALU.max).then_inc(S["score_made"], 1)
                        if t >= 1:
                            m = n - 1
                            dve.wait_ge(S["ex_made"], m + 1)
                            if not (isinstance(h, int) and h == 0 and t < 3):
                                dve.wait_ge(S["prob_used"], m - 1)
                            stt(prob[(t - 1) % 2][0:ROWS, :], ex2[(t - 1) % 2][0:ROWS, :], CAP, cntT[0:ROWS, t - 1, :],
                                ALU.min, ALU.mult).then_inc(S["prob_made"], 1)

                prep(0, 0)
                prep(1, 1)
                tiles(0, 0)
                sums(0, 0, 0, psW[1])
                per, first = 2 * (PREP_STEPS + SUM_STEPS), done.n
                with dve.Fori(0, H // 2 - 1) as g:
                    done.base = g * per
                    prep(2 * g + 2, 0)
                    tiles(2 * g + 1, 1)
                    sums(2 * g + 1, 1, 0, psW[1])
                    prep(2 * g + 3, 1)
                    tiles(2 * g + 2, 0)
                    sums(2 * g + 2, 0, 0, psW[1])
                assert done.n - first == per
                done.base, done.n = 0, first + per * (H // 2 - 1)
                tiles(H - 1, 1)
                sums(H - 1, 1, 0, psW[1])
            else:
                phase_end(dve, 5)
            phase_end(dve, 6)
            if layers >= 4:
                ln_stats(3)
                for t in range(TILES):
                    dve.wait_ge(S["v3_full"], t + 1)
                    dve.tensor_copy(v_aug[0:ROWS, t, :, 0:DH], psS[t % 2][0:ROWS, :].rearrange("p (h d) -> p h d", h=H)).then_inc(S["v3_out"], 1)
                done(ts(mask[0:ROWS, :, :], cntT[0:ROWS, :, :], 0.0, NEG, ALU.is_equal, ALU.mult))
                phase_end(dve, 7)

                def head3(h, b):
                    for t in range(TILES):
                        dve.wait_ge(S[f"s{t % 2}_full"], S3 * h + t // 2 + 1)
                        take_wait()
                        dve.tensor_tensor_reduce(psW[t % 2][0:ROWS, 0:N], psW[t % 2][0:ROWS, 0:N], mask[0:ROWS, t, :], 1.0, 2 * NEG,
                                                 ALU.add, ALU.max, mcol[0:ROWS, b, t:t + 1]).then_inc(S[f"s{t % 2}_free"], 1)
                    for t in range(TILES):
                        n = (H + h) * TILES + t
                        dve.wait_ge(S[f"s{t % 2}_free"], S3 * h + 8 + t // 2)
                        dve.wait_ge(S["prob_used"], n - 1)
                        stt(prob[t % 2][0:ROWS, :], ex3[t % 2][0:ROWS, :], CAP, cnt[0:ROWS, t, :], ALU.min, ALU.mult).then_inc(S["prob_made"], 1)
                    sums(h, b, 1, small)

                with dve.Fori(0, H // 2) as g:
                    done.base = g * (2 * SUM_STEPS)
                    head3(2 * g, 0)
                    head3(2 * g + 1, 1)
                done.base = 0
            else:
                phase_end(dve, 7)
            phase_end(dve, 8)

        @block.tensor
        def _(pe):
            def turn(dst, src, k):
                return pe.transpose(dst, src, ident[0:k, 0:k])

            pe.wait_ge(S["consts_set"], 1)
            pe.wait_ge(S["edges_f32"], 1)
            for s in range(2):
                for g in range(2):
                    at = (2 * s + g) * PAIRS
                    m = turn(psS[0][0:CHUNK, at:at + PAIRS], e_f[0:PAIRS, s, g * CHUNK:(g + 1) * CHUNK], PAIRS)
            m.then_inc(S["edges_turned"], 1)
            pe.wait_ge(S["pair_bounds"], 1)
            for r in range(2):
                m = turn(psS[1][0:1, r * PAIRS:(r + 1) * PAIRS], pair_mm[0:PAIRS, r:r + 1], PAIRS)
            m.then_inc(S["bounds_turned"], 1)
            pe.wait_ge(S["bounds_set"], 1)

            def turn_counts(t):
                pe.wait_ge(S["counts_f32"], t + 1)
                for r, (lo, hi) in enumerate(((0, 4), (4, 8), (8, 10))):
                    n = 3 * t + r
                    if n >= 2:
                        pe.wait_ge(S["counts_turn_read"], n - 1)
                    if n == 2:
                        pe.wait_ge(S["edge_cols"], 1)
                    for j in range(lo, hi):
                        m = turn(psS[n % 2][0:ROWS, (j - lo) * ROWS:(j - lo + 1) * ROWS], cnt_f[t % 2][0:ROWS, j * ROWS:(j + 1) * ROWS], ROWS)
                    m.then_inc(S["counts_turning"], 1)

            def zero_matmul(ps, start, stop):
                for lo, hi in ((0, 512), (512, 1024), (1024, N)):
                    mm = pe.matmul(ps[0:ROWS, lo:hi], zero_bf[:, 0:ROWS], zero_bf[:, 0:hi - lo], start=start, stop=stop)
                return mm

            for t in range(TILES):
                start, end = (pe.value_load(bounds_i[0:1, i * TILES + t:i * TILES + t + 1], min_val=i - 1,
                                            max_val=TILES * PAIRS) for i in (1, 2))
                if t >= 2:
                    pe.wait_ge(S["counts_f32"], t - 1)
                if t == 0:
                    pe.wait_ge(S["edge_cols"], 1)
                zero_matmul(psW[t % 2], True, False)
                with pe.Fori(start, end) as n:
                    for g in range(2):
                        pe.wait_ge(S[f"hot{g}_made"], n + 1)
                        wide_matmul(pe, psW[t % 2], ROWS, hot_dst[g][0:ROWS, 0:ROWS], hot_src[g][0:ROWS, :], False, False).then_inc(S[f"hot{g}_free"], 1)
                zero_matmul(psW[t % 2], False, True).then_inc(S["tile_counted"], 1)
                if t >= 1:
                    turn_counts(t - 1)
            turn_counts(TILES - 1)
            pe.wait_ge(S["counts_turn_read"], 3 * TILES)
            turn(psS[1][0:TILES, 0:ROWS], deg_col[0:ROWS, :], ROWS).then_inc(S["deg_turned"], 1)
            pe.wait_ge(S["deg_row_out"], 1)

            def spread(ps, row, signal):
                for t in range(TILES):
                    m = pe.matmul(block_at(ps, 128, t), sel[:, t, :], row, start=True, stop=True)
                m.then_inc(signal, 1)

            spread(psW[0], row_sb[:, 0, :], S["deg_wide"])
            phase_end(pe, 1)

            def turn_h(l):
                for k in range(KD):
                    if k >= 2:
                        pe.wait_ge(S["hT_made"], KD * l + k - 1)
                    for t in range(TILES):
                        if k == 0:
                            pe.wait_ge(S["h_made"], TILES * l + t + 1)
                        m = turn(block_at(psW[k % 2], 128, t), h_nm[0:ROWS, t, 128 * k:128 * k + 128], ROWS)
                    m.then_inc(S["h_turned"], 1)

            def aggregate(base):
                for half in range(2):
                    if half == 1:
                        pe.wait_ge(S["agg_read"], (base // TILES // 2) * KD + 2)
                    for j in range(TILES):
                        n = half * TILES + j
                        pe.wait_ge(S["cT_f32"], base + n + 1)
                        for kk in range(2):
                            k = 2 * half + kk
                            m = wide_matmul(pe, psW[kk], 128, h_nm[0:ROWS, j, 128 * k:128 * k + 128], cntT_f[n % 2][0:ROWS, :],
                                            j == 0, j == TILES - 1)
                        m.then_inc(S["cT_used"], 1)

            def turn_back(base):
                for t in range(TILES):
                    if t >= 2:
                        pe.wait_ge(S["x_updated"], base + t - 1)
                    for k in range(KD):
                        m = turn(psS[t % 2][0:ROWS, 128 * k:128 * k + 128], yT[:, k, t * ROWS:(t + 1) * ROWS], 128)
                    m.then_inc(S["z_turned"], 1)

            turn_h(0)
            pe.wait_ge(S["w_in"], 32)
            for n in range(2 * KD):
                if n >= 2:
                    pe.wait_ge(S["w_turn_read"], n - 1)
                w = w_nat[n // KD]
                for o in range(KD):
                    m = turn(psS[n % 2][:, 128 * o:128 * o + 128], w[:, o, 128 * (n % KD):128 * (n % KD) + 128], 128)
                m.then_inc(S["w_turned"], 1)
            pe.wait_ge(S["hT_made"], KD)
            aggregate(0)
            pe.wait_ge(S["w_turn_read"], 2 * KD)
            pe.wait_ge(S["agg_read"], KD)
            for f in range(KD):
                if f >= 2:
                    pe.wait_ge(S["y_out"], f - 1)
                for k in range(2 * KD):
                    w, r = ((w_a, aggT), (w_b, hT))[k // KD]
                    m = wide_matmul(pe, psW[f % 2], 128, w[:, k % KD, 128 * f:128 * f + 128], r[:, k % KD, :], k == 0, k == 2 * KD - 1)
                m.then_inc(S["y_full"], 1)
            pe.wait_ge(S["y_scaled"], KD)
            turn_back(0)
            phase_end(pe, 2)
            if layers >= 2:
                turn_h(1)
                pe.wait_ge(S["w_in"], 16 * 6)
                pe.wait_ge(S["hT_made"], 2 * KD)
                for r, w in enumerate((w_a, w_b)):
                    for f in range(KD):
                        for k in range(KD):
                            m = pe.matmul(psW[r][:, NPERF * f:NPERF * f + NPERF], w[:, k, 128 * f:128 * f + 128], hT[:, k, 0:NPERF],
                                          start=(k == 0), stop=(k == KD - 1))
                    m.then_inc(S["qk_full"], 1)
                for b in range(PB):
                    for k in range(KD):
                        m = pe.matmul(psS[b][:, :], hT[:, k, 128 * b:128 * b + 128], wv[:, k, :], start=(k == 0), stop=(k == KD - 1))
                m.then_inc(S["v_full"], 1)
                for b in range(PB):
                    m = turn(psW[1][:, 1024 + 128 * b:1024 + 128 * b + 128], proj_nat[:, b, :], 128)
                m.then_inc(S["proj_turned"], 1)
                pe.wait_ge(S["v_out"], 1)
                pe.wait_ge(S["sq_made"], 1)
                for par in range(2):
                    p = slice(DH * par, DH * par + DH)
                    for r in range(2):
                        for hh in range(H // 2):
                            for b in range(PB):
                                at = r * H + hh * PB + b
                                m = pe.matmul(psS[par][:, at:at + 1], sq[p, r, NPERF * hh + 128 * b:NPERF * hh + 128 * b + 128],
                                              half_c[p, :], start=True, stop=True)
                m.then_inc(S["diag_full"], 1)
                pe.wait_ge(S["proj_out"], 1)

                def features(r, h):
                    p = slice(DH * (h % 2), DH * (h % 2) + DH)
                    for b in range(PB):
                        at = NPERF * (h // 2) + 128 * b
                        m = pe.matmul(psW[h % 2][:, MPERF * b:MPERF * b + MPERF], qkT[p, r, at:at + 128], projT[p, :], start=True, stop=True)
                    return m

                for h in range(H):
                    if h >= 2:
                        pe.wait_ge(S["uk_max"], h - 1)
                    features(1, h).then_inc(S["uk_full"], 1)
                for h in range(H):
                    pe.wait_ge(*((S["uk_max"], H) if h < 2 else (S["kf_exp"], h - 1)))
                    features(1, h).then_inc(S["uk2_full"], 1)
                for h in range(H):
                    pe.wait_ge(*((S["kf_exp"], H) if h < 2 else (S["qf_exp"], h - 1)))
                    features(0, h).then_inc(S["uq_full"], 1)
                pe.wait_ge(S["kf_made"], H)
                pe.wait_ge(S["qf_exp"], H)
                for h in range(H):
                    if h >= 2:
                        pe.wait_ge(S["kv_out"], h - 1)
                    for mb in range(PB):
                        for b in range(PB):
                            m = pe.matmul(psW[h % 2][:, VA * mb:VA * mb + VA], kf[:, h, MPERF * b + 128 * mb:MPERF * b + 128 * mb + 128],
                                          v_perf[:, b, h, :], start=(b == 0), stop=(b == PB - 1))
                    m.then_inc(S["kv_full"], 1)
                pe.wait_ge(S["diag_out"], 1)
                for h in range(H):
                    pe.wait_ge(S["qf_made"], h + 1)
                    if h >= 2:
                        pe.wait_ge(S["qfT_out"], h - 1)
                    for mb in range(PB):
                        for b in range(PB):
                            m = turn(psS[h % 2][:, NPERF * mb + 128 * b:NPERF * mb + 128 * b + 128],
                                     qf[:, h, MPERF * b + 128 * mb:MPERF * b + 128 * mb + 128], 128)
                    m.then_inc(S["qf_turned"], 1)
                pe.wait_ge(S["qfT_out"], H)
                for h in range(H):
                    pe.wait_ge(S["kv_out"], h + 1)
                    if h >= 2:
                        pe.wait_ge(S["at_out"], h - 1)
                    for b in range(PB):
                        for mb in range(PB):
                            m = pe.matmul(psW[h % 2][:, 512 + VA * b:512 + VA * b + VA], qfT[:, h, NPERF * mb + 128 * b:NPERF * mb + 128 * b + 128],
                                          kv_perf[:, h, mb, :], start=(mb == 0), stop=(mb == PB - 1))
                    m.then_inc(S["at_full"], 1)
                pe.wait_ge(S["at_out"], H)
                for k in range(KD):
                    for b in range(PB):
                        m = turn(psW[0][:, NPERF * k + 128 * b:NPERF * k + 128 * b + 128], attn[:, b, 128 * k:128 * k + 128], 128)
                m.then_inc(S["at_turned"], 1)
                pe.wait_ge(S["atT_out"], 1)
                for f in range(KD):
                    for k in range(KD):
                        m = pe.matmul(psW[1][:, NPERF * f:NPERF * f + NPERF], wo[:, k, 128 * f:128 * f + 128], attnT[:, k, :],
                                      start=(k == 0), stop=(k == KD - 1))
                m.then_inc(S["o_full"], 1)
                phase_end(pe, 3)
                aggregate(2 * TILES)
                pe.wait_ge(S["w_in"], 16 * 7)
                pe.wait_ge(S["agg_read"], 2 * KD)
                for f in range(KD):
                    if f >= 2:
                        pe.wait_ge(S["conv_out"], f - 1)
                    for k in range(KD):
                        m = wide_matmul(pe, psW[f % 2], 128, w_a[:, k, 128 * f:128 * f + 128], aggT[:, k, :], k == 0, k == KD - 1)
                    m.then_inc(S["conv_full"], 1)
                pe.wait_ge(S["y_scaled"], 2 * KD)
                turn_back(TILES)
            else:
                phase_end(pe, 3)
            phase_end(pe, 4)
            if layers >= 3:
                turn_h(2)
                pe.wait_ge(S["hT_made"], 3 * KD)
                pe.wait_ge(S["w_in"], 16 * (7 + KD + 3))
                for t in range(TILES):
                    if t >= 2:
                        pe.wait_ge(S["wx_out"], t - 1)
                    for k in range(KD):
                        m = pe.matmul(psS[t % 2][0:ROWS, :], hT[:, k, t * ROWS:(t + 1) * ROWS],
                                      w_gat[:, k, :, :].rearrange("p h d -> p (h d)"), start=(k == 0), stop=(k == KD - 1))
                    m.then_inc(S["wx_full"], 1)
                phase_end(pe, 5)

                def rows_wide(h, b):
                    pe.wait_ge(S["b_picked"], h + 1)
                    if not (isinstance(h, int) and h == 0):
                        pe.wait_ge(S["uw_out"], 2 * h)
                    turn(psS[1][0:TILES, 0:ROWS], bst[0:ROWS, b, :], ROWS).then_inc(S["b_turned"], 1)
                    pe.wait_ge(S["b_rows"], h + 1)
                    spread(psW[0], row_sb[:, 0, :], S["b_wide"])
                    pe.wait_ge(S["uw_cols"], h + 1)
                    for r in range(2):
                        m = turn(psS[1][0:TILES, r * ROWS:(r + 1) * ROWS], ucol[0:ROWS, b, r, :], ROWS)
                    m.then_inc(S["uw_turned"], 1)
                    pe.wait_ge(S["uw_rows"], h + 1)
                    pe.wait_ge(S["b_out"], h + 1)
                    for r in range(2):
                        if r == 1:
                            pe.wait_ge(S["uw_out"], 2 * h + 1)
                        spread(psW[0], row_sb[:, r, :], S["uw_wide"])

                def weigh(h, layer, t, ps):
                    pe.wait_ge(S["prob_made"], (layer * H + h) * TILES + t + 1)
                    if t == 0:
                        pe.wait_ge(S["acc_read"], layer * H + h)
                    acc = acc_view(ps)
                    for i in range(TILES):
                        m = pe.matmul(acc[:, i // HEAD_HALF, i % HEAD_HALF, :], prob[t % 2][0:ROWS, i * ROWS:(i + 1) * ROWS],
                                      v_aug[0:ROWS, t, h, :], start=(t == 0 and i % HEAD_HALF == 0), stop=(t == TILES - 1),
                                      skip_group_check=True)
                    m.then_inc(S["prob_used"], 1)

                def gat_sums(h):
                    for t in range(TILES):
                        weigh(h, 0, t, psW[1])

                rows_wide(0, 0)
                rows_wide(1, 1)
                gat_sums(0)
                with pe.Fori(0, H // 2 - 1) as g:
                    rows_wide(2 * g + 2, 0)
                    gat_sums(2 * g + 1)
                    rows_wide(2 * g + 3, 1)
                    gat_sums(2 * g + 2)
                gat_sums(H - 1)
            else:
                phase_end(pe, 5)
            phase_end(pe, 6)
            if layers >= 4:
                turn_h(3)
                pe.wait_ge(S["hT_made"], 4 * KD)
                pe.wait_ge(S["w_in"], 16 * (7 + KD + 6))
                for n in range(2 * KD):
                    if n >= 2:
                        pe.wait_ge(S["proj3_out"], n - 1)
                    w = (w_k, w_q)[n // KD]
                    for k in range(KD):
                        m = wide_matmul(pe, psW[n % 2], 128, w[:, k, 128 * (n % KD):128 * (n % KD) + 128], hT[:, k, :], k == 0, k == KD - 1)
                    m.then_inc(S["proj3_full"], 1)
                for t in range(TILES):
                    if t >= 2:
                        pe.wait_ge(S["v3_out"], t - 1)
                    for k in range(KD):
                        m = pe.matmul(psS[t % 2][0:ROWS, :], hT[:, k, t * ROWS:(t + 1) * ROWS], w_v[:, k, :], start=(k == 0), stop=(k == KD - 1))
                    m.then_inc(S["v3_full"], 1)
                phase_end(pe, 7)
                pe.wait_ge(S["ones_set"], 1)
                for i in range(2):
                    pe.sem_inc(S[f"s{i}_free"], 1)

                def head(h, b):
                    pe.wait_ge(S["slots_set"], h + 1)
                    for t in range(TILES):
                        pe.wait_ge(S[f"s{t % 2}_free"], S3 * h + t // 2 + 1)
                        wide_matmul(pe, psW[t % 2], ROWS, q_slot[b][0:DH, t * ROWS:(t + 1) * ROWS], k_slot[b][0:DH, :],
                                    True, True).then_inc(S[f"s{t % 2}_full"], 1)
                    pe.wait_ge(S["s0_free"], S3 * h + 6)
                    pe.wait_ge(S["s1_free"], S3 * h + 6)
                    turn(psW[1][0:TILES, 0:ROWS], mcol[0:ROWS, b, :], ROWS).then_inc(S["s1_full"], 1)
                    pe.wait_ge(S["s1_free"], S3 * h + 7)
                    spread(psW[0], row_sb[:, 0, :], S["s0_full"])
                    for t in range(TILES + 1):
                        if t < TILES:
                            pe.wait_ge(S[f"s{t % 2}_free"], S3 * h + 7 + t // 2)
                            wide_matmul(pe, psW[t % 2], ROWS, k_slot[b][0:VA, t * ROWS:(t + 1) * ROWS], q_slot[b][0:VA, :],
                                        True, True).then_inc(S[f"s{t % 2}_full"], 1)
                        if t >= 1:
                            weigh(h, 1, t - 1, small)

                with pe.Fori(0, H // 2) as g:
                    head(2 * g, 0)
                    head(2 * g + 1, 1)
            else:
                phase_end(pe, 7)
            phase_end(pe, 8)


INS = ["x", "src", "dst", "L0_gnn_W_l", "L0_gnn_b_l", "L0_gnn_W_r", "L0_gnn_gamma", "L0_gnn_beta", "L1_gnn_norm1_g",
       "L1_gnn_norm1_b", "L1_gnn_norm2_g", "L1_gnn_norm2_b", "L1_gnn_W_conv", "L1_gnn_b_conv", "L1_gnn_Wq", "L1_gnn_Wk",
       "L1_gnn_Wv", "L1_gnn_Wo", "L1_gnn_proj", "L2_gnn_Ws", "L2_gnn_Wb", "L2_gnn_a_w", "L2_gnn_a_b", "L3_gnn_W"]


def kernel(**inputs):
    import numpy as np
    import concourse.bacc as bacc
    from concourse.bass_utils import run_bass_kernel_spmd as run

    nc = bacc.Bacc("TRN2", target_bir_lowering=False, num_devices=1)
    arrays, aps = {}, {}
    for name in INS:
        arr = np.ascontiguousarray(inputs[name])
        arrays[f"in_{name}"] = arr
        aps[name] = nc.dram_tensor(f"in_{name}", arr.shape, mybir.dt.from_np(arr.dtype), kind="ExternalInput").ap()
    out = nc.dram_tensor("out", (N, D), F32, kind="ExternalOutput").ap()
    gnn_program(nc, aps, out)
    r = run(nc, [arrays], core_ids=[0])
    return r.results[0]["out"]
```

```python
from contextlib import ExitStack

import concourse.bass as bass
from concourse import mybir

ALU = mybir.AluOpType
ACT = mybir.ActivationFunctionType
AX = mybir.AxisListType.X
F32, BF16, F16 = mybir.dt.float32, mybir.dt.bfloat16, mybir.dt.float16
I32, I16 = mybir.dt.int32, mybir.dt.int16
RMAX = bass.bass_isa.ReduceOp.max

N, E, D = 1250, 20000, 512
TILES, ROWS = 10, 125
KD = D // 128
CHUNK = 125
PAIRS = E // (2 * CHUNK)
H, DH = 8, 64
VA = DH + 1
NPERF, MPERF = 256, 256
PB = NPERF // 128
EPS, KEPS = 1e-5, 1e-6
NEG = -1e30
CAP = 1e30
LEAD = 3
MAX_STEPS3 = ((), (), (0,), (1, 2), (3,), (4, 5), (6,), (7,), (8, 9), ())
HS = 2048.0
EXACT16 = 2048.0
TINY = 1e-30
HEAD_HALF = 5
SIZE = {F32: 4, I32: 4, BF16: 2, F16: 2, I16: 2}


def wide_matmul(pe, ps, rows, lhsT, rhs, start, stop):
    for lo, hi in ((0, 512), (512, 1024), (1024, N)):
        mm = pe.matmul(ps[0:rows, lo:hi], lhsT, rhs[:, lo:hi], start=start, stop=stop, skip_group_check=True)
    return mm


def block_at(ps, rows, t):
    at = 512 * (t // 4) + ROWS * (t % 4)
    return ps[0:rows, at:at + ROWS]


def blocks_out(copy, dst, ps, rows):
    banks = ps[0:rows, :].rearrange("p (b c) -> p b c", b=3)
    copy(dst[:, 0:1000].rearrange("p (b c) -> p b c", b=2), banks[:, 0:2, 0:500])
    return copy(dst[:, 1000:N], banks[:, 2, 0:250])


def gnn_program(nc, a, out, layers=4):
    ctx = ExitStack()
    with ctx:
        def sb(name, shape, dt=F32):
            return ctx.enter_context(nc.sbuf_tensor(name, shape, dt))

        def sem(name):
            return ctx.enter_context(nc.semaphore(name))

        x_nm = sb("x_nm", [128, TILES, D])
        cnt = sb("cnt", [128, TILES, N], I16)
        cntT = sb("cntT", [128, TILES, N], I16)
        ident = sb("ident", [128, 128])
        ident_bf = sb("ident_bf", [128, 128], BF16)
        sel = sb("sel", [3 * TILES, TILES, 128], BF16)
        b_parts = sb("b_parts", [128, H, 3, TILES], BF16)
        parts = sb("parts", [128, 2, 3, TILES], BF16)
        split_rest = sb("split_rest", [128, H, TILES])
        zero_bf = sb("zero_bf", [1, 512], BF16)
        deg_col = sb("deg_col", [128, TILES])
        row_sb = sb("row_sb", [3 * TILES, 2, ROWS], BF16)
        bn6 = sb("bn6", [128, TILES, 6])
        mv = sb("mv", [128, TILES, 2])
        rstd = sb("rstd", [128, TILES])
        nbias = sb("nbias", [128, TILES])
        vec = sb("vec", [128, 8, KD])
        bl_c, ga0_c, be0_c, g1_c, b1_c, g2_c, b2_c, bc_c = [vec[:, i, :] for i in range(8)]
        bns = sb("bns", [128, KD, 3, 6])
        bnv = sb("bnv", [128, KD, 2])
        scl = sb("scl", [128, KD])
        shf = sb("shf", [128, KD])
        scl1 = sb("scl1", [128, KD])
        shf1 = sb("shf1", [128, KD])
        bounds_i = sb("bounds_i", [1, 3 * TILES + 1], I32)
        var_eps = sb("var_eps", [128, TILES])
        root = sb("root", [128, TILES])
        half_c = sb("half_c", [128, 1])
        proj_nat = sb("proj_nat", [128, PB, 2 * DH])
        projT = sb("projT", [128, MPERF])
        qdiag = sb("qdiag", [128, H, PB])
        kdiag = sb("kdiag", [128, H, PB])
        qmax = sb("qmax", [128, H, PB])
        kmax = sb("kmax", [128, H])
        kmaxa = sb("kmaxa", [128, H])
        qbias = sb("qbias", [128, H, PB])
        kbias = sb("kbias", [128, H, PB])
        pz = sb("pz", [128, H, PB])
        tcol = sb("tcol", [128, H, TILES])
        bcol = sb("bcol", [128, H, TILES])
        t02 = sb("t02", [128, H, TILES])
        b08 = sb("b08", [128, H, TILES])
        b02 = sb("b02", [128, H, TILES])
        mcol = sb("mcol", [128, 2, TILES])
        zcol = sb("zcol", [128, 2, TILES])
        ucol = sb("ucol", [128, 2, TILES])
        rden = sb("rden", [128, 2, TILES])
        head_sum = sb("head_sum", [128, 2, HEAD_HALF, DH])
        AW = 31584
        arena = sb("arena", [128, AW])

        def region(off, shape, dt=F32):
            n = 1
            for s in shape:
                n *= s
            words = (n * SIZE[dt] + 3) // 4
            assert off + words <= AW, (off, words)
            v = arena[:, off:off + words]
            if dt != F32:
                v = v.bitcast(dt)
            if len(shape) == 2:
                v = v.rearrange("p (a b) -> p a b", a=shape[0])
            if len(shape) == 3:
                v = v.rearrange("p (a b c) -> p a b c", a=shape[0], b=shape[1])
            return v

        h_nm = region(0, [TILES, D])
        hT = region(5120, [KD, N])
        rdeg_b = region(10120, [N])
        pos_b = region(11370, [N])
        h_pair = [region(2560 * i, [TILES, D], F16) for i in range(2)]
        h32 = [region(12620 + 512 * i, [D]) for i in range(2)]
        G = 13644
        hot_src = [region(G + 625 * i, [N], BF16) for i in range(2)]
        hot_dst = [region(G + 1250 + 64 * i, [128], BF16) for i in range(2)]
        cnt_f = [region(G + 1400 + 1250 * i, [N]) for i in range(2)]
        iota_h = region(G + 3900, [N], F16)
        e_raw = region(G + 4530, [2, 2 * CHUNK], I32)
        e_f = region(G + 5030, [2, 2 * CHUNK])
        e_col = region(G + 5530, [2, PAIRS, 2])
        pair_mm = region(G + 5900, [2])
        pair_row = arena[0:1, G + 6000:G + 6160]
        tile_lo = arena[0:1, G + 6160:G + 6170]
        up_row = arena[0:1, G + 6200:G + 6280]
        down_row = arena[0:1, G + 6280:G + 6360]
        flag = [arena[0:1, G + 6400 + 800 * i:G + 7200 + 800 * i].rearrange("p (t q) -> p t q", t=TILES)
                for i in range(2)]
        bnd = arena[0:1, G + 8000:G + 8080].rearrange("p (r t) -> p r t", r=8)
        aggT = region(G, [KD, N])
        yT = region(G + 5000, [KD, N])
        w_nat = [region(G + 5000 + 2048 * i, [KD, D]) for i in range(2)]
        w_a = region(G + 10300, [KD, D])
        w_b = region(G + 12348, [KD, D])
        cntT_16 = [region(G + 14400 + 625 * i, [N], F16) for i in range(2)]
        oT = region(G + 16500, [KD, NPERF])
        wo = region(G + 14400, [KD, D])
        wv = region(G, [KD, D])
        qf = region(G, [H, PB * MPERF])
        attn = region(G, [PB, D])
        attnT = region(G + 1024, [KD, NPERF])
        sq = region(G + 4096, [2, KD * NPERF])
        kf = region(G + 4096, [H, PB * MPERF])
        qkT = region(G + 8192, [2, KD * NPERF])
        qfT = region(G + 10300, [H, PB * NPERF])
        v_perf = region(G + 16500, [PB, H, VA])
        kv_perf = region(G + 8192, [H, PB, VA])
        b_row = [region(1250 * i, [N]) for i in range(2)]
        u_row = [region(2500 + 2500 * i, [N]) for i in range(2)]
        w_row = [region(3750 + 2500 * i, [N]) for i in range(2)]
        prob = [region(7500 + 1250 * i, [N]) for i in range(2)]
        mask = region(10120, [TILES, N], BF16)
        v_aug = region(16370, [TILES, H, VA])
        score = [region(21570 + 1250 * i, [N]) for i in range(4)]
        wb_row = region(21570, [D])
        ab_row = region(22100, [H])
        ex2 = [region(26570 + 1250 * i, [N]) for i in range(2)]
        w_gat = region(27820, [KD, H, DH])
        a_mul = region(29868, [2, H, DH])
        junk = region(29070, [2, N], BF16)
        a_rows = region(25320, [H, 2 * DH])
        k_part = [region(o, [KD, N], BF16) for o in (0, 2500, 21570)]
        q_part = [region(o, [KD, N], BF16) for o in (24070, 26570, 29070)]
        q12, q13, k11, k22, k31 = [[region(5120 + 3125 * b + 625 * i, [N], BF16) for b in range(2)] for i in range(5)]
        ex3 = [region(11370 + 1250 * i, [N]) for i in range(2)]
        prob3 = [region(13870 + 1250 * i, [N]) for i in range(2)]
        mask3 = cntT[:, :, :].bitcast(BF16)
        w_k, w_q, w_v = [region(10120 + 2048 * i, [KD, D]) for i in range(3)]

        psW = [ctx.enter_context(nc.psum_tensor(f"wide{i}", [128, 1536], F32)) for i in range(2)]
        small = ctx.enter_context(nc.psum_tensor("small", [128, 1024], F32))
        psS = [small[:, 0:512], small[:, 512:1024]]

        def acc_view(ps):
            return ps[0:ROWS, 0:1024].rearrange("p (u c) -> p u c", u=2)[:, :, 0:HEAD_HALF * VA].rearrange(
                "p u (t d) -> p u t d", d=VA)

        names = """x_in edges_in vec_in w_in edges_f32 edges_turned edge_cols pair_bounds bounds_turned bounds_row
            pair_cols bounds_set consts_set hot0_made hot1_made hot0_free hot1_free tile_counted counts_f32
            counts_i16 counts_turning counts_turn_read deg_split deg_turned deg_row_out deg_wide deg_rows
            ln_ready h_made h_turned hT_made x_plus_h h1_made h_split cT_wide cT_used lo_wide lo_made lo_used agg_full agg_read w_turned w_turn_read y_full y_out
            y_stats y_scaled z_turned x_updated bn1_ready qk_full qk_out v_full v_out proj_turned proj_out sq_made
            diag_full diag_out uk_full uk_max kmax_all kbias_set uk2_full kf_exp kf_made uq_full uq_max qf_exp
            qf_made qf_turned qfT_out kv_full kv_out at_full at_out at_turned atT_out o_full o_out conv_full
            conv_out sum_made wx_full wx_out wx_mul ab_cols mask_made maxed b_parts_set b_turned b_rows b_wide b_out
            uw_cols uw_turned uw_rows uw_wide uw_out score_made ex_made prob_made prob_used acc_read
            proj3_full proj3_1 proj3_rest proj3_2 proj3_out v3_full v3_out stack0_set stack1_set s0_full s1_full s0_free s1_free
            waits_taken var_ready root_out m_made m_split dve_done stored phase_done pool_done""".split()
        S = {n: sem(n) for n in names}
        block = ctx.enter_context(nc.Block())

        class Order:

            def __init__(self, eng, semaphore):
                self.eng, self.sem, self.base, self.n = eng, semaphore, 0, 0

            def __call__(self, ins):
                self.n += 1
                ins.then_inc(self.sem, 1)
                self.eng.wait_ge(self.sem, self.base + self.n)

        def phase_end(eng, n):
            eng.drain().then_inc(S["phase_done"], 1)
            eng.wait_ge(S["phase_done"], 5 * n)

        def s0_use(h, t):
            return TILES // 2 + (TILES + 1) * h + t + 2

        def s1_use(h, t):
            return TILES * h - TILES // 2 + t + 1

        def split_cols(eng, done, dst, rest, src):
            part = [dst[:, i, :] if len(dst.shape) == 3 else dst[:, :, i, :] for i in range(3)]
            done(eng.tensor_copy(part[0], src))
            done(eng.tensor_tensor(rest, src, part[0], ALU.subtract))
            done(eng.tensor_copy(part[1], rest))
            return eng.tensor_tensor(part[2], rest, part[1], ALU.subtract)

        def h_tiles(l):
            return TILES * min(l, 2) + KD * max(l - 2, 0)

        def has_big_count(eng):
            return eng.value_load(bounds_i[0:1, 3 * TILES:3 * TILES + 1], min_val=0, max_val=1)

        @block.sync
        def _(sp):
            col = "(k p) -> p k"
            sp.dma_start(e_raw[0:PAIRS, 0, :], a["dst"].rearrange("(p e) -> p e", p=PAIRS)).then_inc(S["edges_in"], 16)
            sp.dma_start(e_raw[0:PAIRS, 1, :], a["src"].rearrange("(p e) -> p e", p=PAIRS)).then_inc(S["edges_in"], 16)
            for t in range(0, TILES, 5):
                sp.dma_start(x_nm[0:ROWS, t:t + 5, :], a["x"].rearrange("(t p) f -> p t f", p=ROWS)[:, t:t + 5, :]).then_inc(S["x_in"], 16)
            with nc.allow_non_contiguous_dma(reason="feature vectors as columns, 4 bytes a partition"):
                for i, name in enumerate(["L0_gnn_b_l", "L0_gnn_gamma", "L0_gnn_beta", "L1_gnn_norm1_g",
                                          "L1_gnn_norm1_b", "L1_gnn_norm2_g", "L1_gnn_norm2_b", "L1_gnn_b_conv"]):
                    sp.dma_start(vec[:, i, :], a[name].rearrange(col, p=128)).then_inc(S["vec_in"], 16)
            for r in range(2):
                sp.dma_start(proj_nat[:, :, DH * r:DH * r + DH],
                             a["L1_gnn_proj"].rearrange("(b m) d -> m b d", m=128)).then_inc(S["vec_in"], 16)
            rows = "(k p) n -> p k n"
            phase_end(sp, 1)
            sp.dma_start(w_nat[0], a["L0_gnn_W_l"].rearrange(rows, p=128)).then_inc(S["w_in"], 16)
            sp.dma_start(w_nat[1], a["L0_gnn_W_r"].rearrange(rows, p=128)).then_inc(S["w_in"], 16)
            phase_end(sp, 2)
            sp.dma_start(w_a, a["L1_gnn_Wq"].rearrange(rows, p=128)).then_inc(S["w_in"], 16)
            sp.dma_start(w_b, a["L1_gnn_Wk"].rearrange(rows, p=128)).then_inc(S["w_in"], 16)
            sp.dma_start(wv, a["L1_gnn_Wv"].rearrange(rows, p=128)).then_inc(S["w_in"], 16)
            sp.dma_start(wo, a["L1_gnn_Wo"].rearrange(rows, p=128)).then_inc(S["w_in"], 16)
            phase_end(sp, 3)
            sp.dma_start(w_a, a["L1_gnn_W_conv"].rearrange(rows, p=128)).then_inc(S["w_in"], 16)
            phase_end(sp, 4)
            for k in range(KD):
                sp.dma_start(w_gat[:, k, :, :], a["L2_gnn_Ws"][:, 128 * k:128 * k + 128, :].rearrange("h p d -> p h d")).then_inc(S["w_in"], 16)
            sp.dma_start(wb_row, a["L2_gnn_Wb"].rearrange("h d -> (h d)").partition_broadcast(128)).then_inc(S["w_in"], 16)
            sp.dma_start(a_rows.rearrange("p h d -> p (h d)"), a["L2_gnn_a_w"].rearrange("h d -> (h d)").partition_broadcast(128)).then_inc(S["w_in"], 16)
            sp.dma_start(ab_row, a["L2_gnn_a_b"].partition_broadcast(128)).then_inc(S["w_in"], 16)
            phase_end(sp, 5)
            phase_end(sp, 6)
            w3 = a["L3_gnn_W"].rearrange(rows, p=128)
            sp.dma_start(w_k, w3[:, :, D:2 * D]).then_inc(S["w_in"], 16)
            sp.dma_start(w_q, w3[:, :, 0:D]).then_inc(S["w_in"], 16)
            sp.dma_start(w_v, w3[:, :, 2 * D:3 * D]).then_inc(S["w_in"], 16)
            phase_end(sp, 7)

            def stack(b, g):
                own = slice(DH * b, DH * b + DH)
                for dst, (top, low) in ((q12, (q_part[0], q_part[1])), (k11, (k_part[0], k_part[0])), (k22, (k_part[1], k_part[1])),
                                        (q13, (q_part[0], q_part[2])), (k31, (k_part[2], k_part[0]))):
                    sp.dma_start(dst[b][0:DH, :], top[own, g, :]).then_inc(S[f"stack{b}_set"], 16)
                    sp.dma_start(dst[b][DH:128, :], low[own, g, :]).then_inc(S[f"stack{b}_set"], 16)

            if layers >= 4:
                stack(0, 0)
                stack(1, 0)
                with sp.Fori(0, H // 2 - 1) as g:
                    for b in range(2):
                        sp.wait_ge(S["s0_full"], s0_use(2 * g + b, TILES - 1))
                        stack(b, g + 1)
            phase_end(sp, 8)
            sp.dma_start(out.rearrange("(t p) f -> p t f", p=ROWS), x_nm[0:ROWS, :, :]).then_inc(S["stored"], 16)
            sp.wait_ge(S["stored"], 16)

        @block.gpsimd
        def _(pool):
            done = Order(pool, S["pool_done"])
            pool.memset(ident[:, :], 1.0)
            pool.memset(sel[:, :, :], 0.0)
            pool.memset(half_c[:, :], 0.5)
            done(pool.memset(zero_bf[:, :], 0.0))
            done(pool.affine_select(out=ident[:, :], in_=ident[:, :], compare_op=ALU.is_equal, fill=0.0, base=0,
                                    pattern=[[-1, 128]], channel_multiplier=1))
            for r in range(3):
                done(pool.affine_select(out=sel[:, :, :], in_=sel[:, :, :], compare_op=ALU.not_equal, fill=1.0, base=-r * TILES,
                                        pattern=[[-1, TILES], [0, 128]], channel_multiplier=1))
            pool.tensor_copy(ident_bf[:, :], ident[:, :])
            many = dict(allow_small_or_imprecise_dtypes=True, channel_multiplier=0)
            done(pool.iota(tile_lo, pattern=[[ROWS, TILES]], base=0, **many))
            done(pool.iota(up_row, pattern=[[1, PAIRS]], base=1, **many))
            done(pool.iota(down_row, pattern=[[-1, PAIRS]], base=PAIRS, **many))
            pool.iota(iota_h[:, :], pattern=[[1, N]], base=0, **many).then_inc(S["consts_set"], 1)
            for t in range(TILES):
                pool.wait_ge(S["counts_f32"], t + 1)
                pool.tensor_copy(cnt[0:ROWS, t, :], cnt_f[t % 2][0:ROWS, :]).then_inc(S["counts_i16"], 1)
            phase_end(pool, 1)

            for t in range(TILES):
                pool.wait_ge(S["h_made"], t + 1)
                pool.tensor_tensor(x_nm[0:ROWS, t, :], x_nm[0:ROWS, t, :], h32[t % 2][0:ROWS, :], ALU.add).then_inc(S["x_plus_h"], 1)
            phase_end(pool, 2)
            pool.wait_ge(S["uk_max"], H)
            pool.partition_all_reduce(kmaxa[:, :], kmax[:, :], 128, RMAX).then_inc(S["kmax_all"], 1)
            phase_end(pool, 3)
            phase_end(pool, 4)
            pool.memset(v_aug[0:ROWS, :, :, DH], 1.0)
            for t in range(TILES):
                pool.wait_ge(S["wx_out"], t + 1)
                if t >= 1:
                    pool.wait_ge(S["ab_cols"], t)
                for r in range(2):
                    m = pool.tensor_tensor(a_mul[0:ROWS, r, :, :], v_aug[0:ROWS, t, :, 0:DH],
                                           a_rows[0:ROWS, :, DH * r:DH * r + DH], ALU.mult)
                m.then_inc(S["wx_mul"], 1)
            phase_end(pool, 5)

            def target_terms(h):
                pool.wait_ge(S["maxed"], TILES * (h + 1))
                z, z02 = zcol[0:ROWS, 0, :], zcol[0:ROWS, 1, :]
                done(pool.tensor_tensor(z, mcol[0:ROWS, h % 2, :], tcol[0:ROWS, h, :], ALU.add))
                done(pool.tensor_scalar(z02, z, 0.2, None, ALU.mult))
                done(pool.tensor_scalar(z, z, 0.0, 0.8, ALU.max, ALU.mult))
                done(pool.tensor_tensor(z, z, z02, ALU.add))
                pool.tensor_tensor(ucol[0:ROWS, 0, :], tcol[0:ROWS, h, :], z, ALU.subtract)
                done(pool.tensor_tensor(ucol[0:ROWS, 1, :], t02[0:ROWS, h, :], z, ALU.subtract))
                split_cols(pool, done, parts[0:ROWS, :, :, :], split_rest[0:ROWS, 0:2, :], ucol[0:ROWS, :, :]).then_inc(S["uw_cols"], 1)

            if layers >= 3:
                for h in range(H):
                    if h >= 1:
                        pool.wait_ge(S["uw_turned"], h)
                    target_terms(h)
            phase_end(pool, 6)
            pool.memset(v_aug[0:ROWS, :, :, DH], 1.0)
            phase_end(pool, 7)

            def maxima_split(h):
                pool.wait_ge(S["m_made"], h + 1)
                done(pool.tensor_scalar(zcol[0:ROWS, 0, :], mcol[0:ROWS, 0, :], -1.0, None, ALU.mult))
                split_cols(pool, done, parts[0:ROWS, 0, :, :], split_rest[0:ROWS, 0, :], zcol[0:ROWS, 0, :]).then_inc(S["m_split"], 1)

            if layers >= 4:
                for h in range(H):
                    maxima_split(h)
            phase_end(pool, 8)

        @block.scalar
        def _(act):
            def copy(dst, src, **k):
                return act.activation(dst, src, ACT.Copy, **k)

            for t in range(TILES + 1):
                if t < TILES:
                    act.wait_ge(S["tile_counted"], t + 1)
                    if t >= 2:
                        act.wait_ge(S["counts_i16"], t - 1)
                        act.wait_ge(S["counts_turning"], 3 * (t - 1))
                    copy(cnt_f[t % 2][0:ROWS, :], psW[t % 2][0:ROWS, 0:N], accum_out=deg_col[0:ROWS, t:t + 1]).then_inc(S["counts_f32"], 1)
                if t >= 1:
                    for r, (lo, hi) in enumerate(((0, 4), (4, 8), (8, 10))):
                        n = 3 * (t - 1) + r
                        act.wait_ge(S["counts_turning"], n + 1)
                        src = psS[n % 2][0:ROWS, 0:(hi - lo) * ROWS].rearrange("p (b c) -> p b c", b=hi - lo)
                        copy(cntT[0:ROWS, lo:hi, (t - 1) * ROWS:t * ROWS], src).then_inc(S["counts_turn_read"], 1)
            act.wait_ge(S["deg_turned"], 1)
            copy(row_sb[:, 0, :], psS[1][0:3 * TILES, 0:ROWS]).then_inc(S["deg_row_out"], 1)

            roots = [0]

            def take_root(rows, cols):
                roots[0] += 1
                act.wait_ge(S["var_ready"], roots[0])
                act.activation(root[0:rows, 0:cols], var_eps[0:rows, 0:cols], ACT.Sqrt).then_inc(S["root_out"], 1)

            def upper_part(l, t):
                act.wait_ge(S["h_made"], TILES * l + t + 1)
                act.mul(h_pair[0][0:ROWS, t, :], h32[t % 2][0:ROWS, :], HS).then_inc(S["h1_made"], 1)

            def relu_norm(l):
                take_root(ROWS, TILES)
                act.wait_ge(S["ln_ready"], l + 1)
                for t in range(TILES):
                    if l < 2 and t >= 2:
                        act.wait_ge(S["h_turned"], h_tiles(l) + t - 1)
                        act.wait_ge(S["h_split"], TILES * l + t - 1)
                        if l == 0:
                            act.wait_ge(S["x_plus_h"], t - 1)
                    dst = h32[t % 2][0:ROWS, :] if l < 2 else h_nm[0:ROWS, t, :]
                    act.activation(dst, x_nm[0:ROWS, t, :], ACT.Relu, bias=nbias[0:ROWS, t:t + 1],
                                   scale=rstd[0:ROWS, t:t + 1]).then_inc(S["h_made"], 1)
                    if l < 2 and t >= 1:
                        upper_part(l, t - 1)
                if l < 2:
                    upper_part(l, TILES - 1)

            def widen(l, big):
                for half in range(2):
                    for j in range(TILES):
                        n = TILES * (2 * l + half) + j
                        if j >= 2:
                            act.wait_ge(S["cT_used"], n - 1)
                        elif n >= TILES:
                            act.wait_ge(S["agg_full"], 2 * l + half)
                        copy(cntT_16[j % 2][0:ROWS, :], cntT[0:ROWS, j, :]).then_inc(S["cT_wide"], 1)
                    with act.If(big > 0):
                        for j in range(TILES):
                            n = TILES * (2 * l + half) + j
                            if j >= 2:
                                act.wait_ge(S["lo_used"], n - 1)
                            else:
                                act.wait_ge(S["cT_used"], TILES * (2 * l + half) + TILES - 1 + j)
                            copy(cntT_16[j % 2][0:ROWS, :], cntT[0:ROWS, j, :]).then_inc(S["lo_wide"], 1)

            phase_end(act, 1)
            big = has_big_count(act)
            relu_norm(0)
            for n in range(2 * KD):
                act.wait_ge(S["w_turned"], n + 1)
                w = (w_a, w_b)[n // KD]
                copy(w[:, n % KD, :], psS[n % 2][:, :]).then_inc(S["w_turn_read"], 1)
            widen(0, big)
            for f in range(KD):
                act.wait_ge(S["y_full"], f + 1)
                act.activation(yT[:, f, :], psW[f % 2][:, 0:N], ACT.Identity, bias=bl_c[:, f:f + 1]).then_inc(S["y_out"], 1)
            take_root(128, KD)
            act.wait_ge(S["y_stats"], 1)
            for f in range(KD):
                act.activation(yT[:, f, :], yT[:, f, :], ACT.Relu, bias=shf[:, f:f + 1], scale=scl[:, f:f + 1]).then_inc(S["y_scaled"], 1)
            phase_end(act, 2)
            if layers >= 2:
                relu_norm(1)
                take_root(128, KD)
                for r in range(2):
                    act.wait_ge(S["qk_full"], r + 1)
                    act.mul(qkT[:, r, :], psW[r][:, 0:KD * NPERF], DH ** -0.25).then_inc(S["qk_out"], 1)
                act.wait_ge(S["proj_turned"], 1)
                copy(projT[:, :], psW[1][:, 1024:1024 + MPERF]).then_inc(S["proj_out"], 1)
                act.wait_ge(S["kbias_set"], 1)
                for h in range(H):
                    act.wait_ge(S["uk2_full"], h + 1)
                    for b in range(PB):
                        e = act.activation(kf[:, h, MPERF * b:MPERF * b + MPERF], psW[h % 2][:, MPERF * b:MPERF * b + MPERF],
                                           ACT.Exp, bias=kbias[:, h, b:b + 1])
                    e.then_inc(S["kf_exp"], 1)
                for h in range(H):
                    act.wait_ge(S["uq_max"], h + 1)
                    for b in range(PB):
                        e = act.activation(qf[:, h, MPERF * b:MPERF * b + MPERF], psW[h % 2][:, MPERF * b:MPERF * b + MPERF],
                                           ACT.Exp, bias=qbias[:, h, b:b + 1])
                    e.then_inc(S["qf_exp"], 1)
                for h in range(H):
                    act.wait_ge(S["qf_turned"], h + 1)
                    copy(qfT[:, h, :], psS[h % 2][:, :]).then_inc(S["qfT_out"], 1)
                act.wait_ge(S["at_turned"], 1)
                copy(attnT.rearrange("p k n -> p (k n)"), psW[0][:, 0:KD * NPERF]).then_inc(S["atT_out"], 1)
                act.wait_ge(S["o_full"], 1)
                copy(oT.rearrange("p k n -> p (k n)"), psW[1][:, 0:KD * NPERF]).then_inc(S["o_out"], 1)
                phase_end(act, 3)
                widen(1, big)
                for f in range(KD):
                    act.wait_ge(S["conv_full"], f + 1)
                    act.activation(yT[:, f, :], psW[f % 2][:, 0:N], ACT.Relu, bias=bc_c[:, f:f + 1]).then_inc(S["conv_out"], 1)
                take_root(128, KD)
                act.wait_ge(S["y_stats"], 2)
                for f in range(KD):
                    act.activation(yT[:, f, :], yT[:, f, :], ACT.Identity, bias=shf[:, f:f + 1], scale=scl[:, f:f + 1]).then_inc(S["y_scaled"], 1)
            else:
                phase_end(act, 3)
            phase_end(act, 4)
            if layers >= 3:
                relu_norm(2)
                phase_end(act, 5)

                def b_row_in(h):
                    act.wait_ge(S["b_turned"], h + 1)
                    copy(row_sb[:, 0, :], psS[1][0:3 * TILES, 0:ROWS]).then_inc(S["b_rows"], 1)

                def b_out(h, b):
                    act.wait_ge(S["b_wide"], h + 1)
                    blocks_out(copy, b_row[b][0:ROWS, :], psW[0], ROWS).then_inc(S["b_out"], 1)

                def uw_row_in(h):
                    act.wait_ge(S["uw_turned"], h + 1)
                    copy(row_sb[:, :, :].rearrange("p r c -> p (r c)"), psS[1][0:3 * TILES, 0:2 * ROWS]).then_inc(S["uw_rows"], 1)

                def uw_out(h, b, r):
                    act.wait_ge(S["uw_wide"], 2 * h + r + 1)
                    blocks_out(copy, (u_row, w_row)[r][b][0:ROWS, :], psW[0], ROWS).then_inc(S["uw_out"], 1)

                def head(h, b):
                    first, last, before = (isinstance(h, int) and h == k for k in (0, H - 1, H - 2))
                    for t in range(TILES):
                        n = h * TILES + t
                        act.wait_ge(S["score_made"], n + 1)
                        if not (first and t < 2):
                            act.wait_ge(S["prob_made"], n - 1)
                        act.activation(ex2[t % 2][0:ROWS, :], score[(b * TILES + t) % 4][0:ROWS, :], ACT.Exp,
                                       bias=b02[0:ROWS, h, t:t + 1]).then_inc(S["ex_made"], 1)
                        if t in (0, 2) and not (last or before):
                            b_row_in(h + 2) if t == 0 else b_out(h + 2, b)
                        if t == 6 and not last:
                            uw_row_in(h + 1)
                        if t in (7, 8) and not last:
                            uw_out(h + 1, 1 - b, t - 7)

                for h in range(2):
                    b_row_in(h)
                    b_out(h, h)
                uw_row_in(0)
                for r in range(2):
                    uw_out(0, 0, r)
                head(0, 0)
                with act.Fori(0, 2) as g:
                    head(2 * g + 1, 1)
                    head(2 * g + 2, 0)
                for h in (5, 6, 7):
                    head(h, h % 2)
            else:
                phase_end(act, 5)
            phase_end(act, 6)
            if layers >= 4:
                relu_norm(3)
                for n in range(2 * KD):
                    part, scale = ((k_part, 1.0), (q_part, DH ** -0.5))[n // KD]
                    act.wait_ge(S["proj3_full"], n + 1)
                    act.mul(part[0][:, n % KD, :], psW[n % 2][:, 0:N], scale).then_inc(S["proj3_1"], 1)
                    act.wait_ge(S["proj3_rest"], n + 1)
                    copy(part[1][:, n % KD, :], psW[n % 2][:, 0:N]).then_inc(S["proj3_2"], 1)
                phase_end(act, 7)

                def head(h):
                    act.wait_ge(S["s0_full"], s0_use(h, -1))
                    copy(row_sb[:, 0, :], psW[0][0:3 * TILES, 0:ROWS]).then_inc(S["s0_free"], 1)
                    for t in range(TILES):
                        act.wait_ge(S["s0_full"], s0_use(h, t))
                        act.wait_ge(S["prob_made"], H * TILES + h * TILES + t - 1)
                        act.activation(ex3[t % 2][0:ROWS, :], psW[0][0:ROWS, 0:N], ACT.Exp).then_inc(S["s0_free"], 1)

                with act.Fori(0, H) as h:
                    head(h)
            else:
                phase_end(act, 7)
            phase_end(act, 8)

        @block.vector
        def _(dve):
            done = Order(dve, S["dve_done"])
            tt, ts, stt = dve.tensor_tensor, dve.tensor_scalar, dve.scalar_tensor_tensor

            def take_wait():
                dve.sem_inc(S["waits_taken"], 1)

            dve.wait_ge(S["edges_in"], 32)
            dve.tensor_copy(e_f[0:PAIRS, :, :], e_raw[0:PAIRS, :, :]).then_inc(S["edges_f32"], 1)
            dve.wait_ge(S["edges_f32"], 1)
            dve.tensor_reduce(pair_mm[0:PAIRS, 0:1], e_f[0:PAIRS, 0, :], AX, ALU.max)
            dve.tensor_reduce(pair_mm[0:PAIRS, 1:2], e_f[0:PAIRS, 0, :], AX, ALU.min).then_inc(S["pair_bounds"], 1)
            dve.wait_ge(S["edges_turned"], 1)
            src = psS[0][0:ROWS, 0:4 * PAIRS].rearrange("e (s g p) -> e s p g", s=2, g=2)
            for s in range(2):
                c = dve.tensor_copy(e_col[0:ROWS, s, :, :], src[:, s, :, :])
            c.then_inc(S["edge_cols"], 1)
            dve.wait_ge(S["bounds_turned"], 1)
            dve.wait_ge(S["consts_set"], 1)
            done(dve.tensor_copy(pair_row, psS[1][0:1, 0:2 * PAIRS]))
            shape = [1, TILES, PAIRS]
            largest = pair_row[:, 0:PAIRS].unsqueeze(1).to_broadcast(shape)
            smallest = pair_row[:, PAIRS:2 * PAIRS].unsqueeze(1).to_broadcast(shape)
            up, down = (r.unsqueeze(1).to_broadcast(shape) for r in (up_row, down_row))
            lo, hi, tile_hi, n_pairs, incl, excl, rest = (bnd[:, i, :] for i in range(7))
            done(ts(tile_hi, tile_lo, float(ROWS), None, ALU.add))
            done(tt(flag[0], largest, tile_lo.unsqueeze(2).to_broadcast(shape), ALU.is_ge))
            done(tt(flag[1], smallest, tile_hi.unsqueeze(2).to_broadcast(shape), ALU.is_lt))
            done(tt(flag[0], flag[0], flag[1], ALU.mult))
            done(tt(flag[1], flag[0], up, ALU.mult))
            done(dve.tensor_reduce(hi, flag[1], AX, ALU.max))
            done(tt(flag[1], flag[0], down, ALU.mult))
            done(dve.tensor_reduce(rest, flag[1], AX, ALU.max))
            done(ts(lo, rest, -1.0, float(PAIRS), ALU.mult, ALU.add))
            done(ts(hi, hi, 1.0, None, ALU.max))
            done(ts(rest, hi, -1.0, None, ALU.add))
            done(tt(lo, lo, rest, ALU.min))
            done(tt(n_pairs, hi, lo, ALU.subtract))
            done(dve.tensor_copy(incl, n_pairs))
            for t in range(1, TILES):
                done(tt(incl[:, t:t + 1], incl[:, t - 1:t], n_pairs[:, t:t + 1], ALU.add))
            done(tt(excl, incl, n_pairs, ALU.subtract))
            for i, r in enumerate((lo, excl, incl)):
                c = dve.tensor_copy(bounds_i[:, i * TILES:(i + 1) * TILES], r)
            c.then_inc(S["bounds_set"], 1)
            dve.wait_ge(S["bounds_set"], 1)
            for g in range(2):
                dve.sem_inc(S[f"hot{g}_free"], 1)
            for t in range(TILES):
                first, start, end = (dve.value_load(bounds_i[0:1, i * TILES + t:i * TILES + t + 1], min_val=m,
                                                    max_val=TILES * PAIRS - (1 - m) if i else PAIRS - 1)
                                     for i, m in ((0, 0), (1, 0), (2, 1)))
                with dve.Fori(start, end) as n:
                    k = nc.s_assert_within(n - start + first, 0, PAIRS - 1,
                                           skip_runtime_bounds_check_because="first + (end - start) <= PAIRS by construction")
                    for g in range(2):
                        dve.wait_ge(S[f"hot{g}_free"], n + 1)
                        ts(hot_src[g][0:ROWS, :], iota_h[0:ROWS, :], e_col[0:ROWS, 1, k, g:g + 1], None, ALU.is_equal)
                        ts(hot_dst[g][0:ROWS, 0:ROWS], iota_h[0:ROWS, t * ROWS:(t + 1) * ROWS],
                           e_col[0:ROWS, 0, k, g:g + 1], None, ALU.is_equal).then_inc(S[f"hot{g}_made"], 1)

            roots = [0]

            def rsqrt(dst, var):
                rows, cols = dst.shape
                ts(var_eps[0:rows, 0:cols], var, EPS, None, ALU.add).then_inc(S["var_ready"], 1)
                roots[0] += 1
                dve.wait_ge(S["root_out"], roots[0])
                done(dve.reciprocal(dst, root[0:rows, 0:cols]))

            def ln_stats(l):
                if l == 0:
                    dve.wait_ge(S["x_in"], 32)
                for t in range(TILES):
                    s = dve.bn_stats(bn6[0:ROWS, t, :], x_nm[0:ROWS, t, :])
                done(s)
                for t in range(TILES):
                    s = dve.bn_aggr(mv[0:ROWS, t, :], bn6[0:ROWS, t, :])
                done(s)
                rsqrt(rstd[0:ROWS, :], mv[0:ROWS, :, 1])
                stt(nbias[0:ROWS, :], mv[0:ROWS, :, 0], -1.0, rstd[0:ROWS, :], ALU.mult, ALU.mult).then_inc(S["ln_ready"], 1)
                if l < 2:
                    for t in range(TILES):
                        dve.wait_ge(S["h_turned"], h_tiles(l) + t + 1)
                        dve.tensor_copy(hT[:, :, t * ROWS:(t + 1) * ROWS], psS[t % 2][:, 0:KD * ROWS].rearrange("p (k c) -> p k c", k=KD)).then_inc(S["hT_made"], 1)
                        dve.wait_ge(S["h1_made"], TILES * l + t + 1)
                        stt(h_pair[1][0:ROWS, t, :], h32[t % 2][0:ROWS, :], HS, h_pair[0][0:ROWS, t, :], ALU.mult, ALU.subtract).then_inc(S["h_split"], 1)
                    return
                for k in range(KD):
                    dve.wait_ge(S["h_turned"], h_tiles(l) + k + 1)
                    blocks_out(dve.tensor_copy, hT[:, k, :], psW[k % 2], 128).then_inc(S["hT_made"], 1)

            def low_counts(l, half, big):
                with dve.If(big > 0):
                    for j in range(TILES):
                        dve.wait_ge(S["lo_wide"], TILES * (2 * l + half) + j + 1)
                        tt(cntT_16[j % 2][0:ROWS, :], cntT[0:ROWS, j, :], cntT_16[j % 2][0:ROWS, :], ALU.subtract).then_inc(S["lo_made"], 1)

            def bn_over_nodes(src, ready, gamma, beta, s_out, b_out):
                for f in range(KD):
                    ready(f)
                    for c, (lo, hi) in enumerate(((0, 512), (512, 1024), (1024, N))):
                        s = dve.bn_stats(bns[:, f, c, :], src[:, f, lo:hi])
                done(s)
                for f in range(KD):
                    s = dve.bn_aggr(bnv[:, f, :], bns[:, f, :, :].rearrange("p c s -> p (c s)"))
                done(s)
                rsqrt(s_out[:, :], bnv[:, :, 1])
                done(tt(s_out[:, :], s_out[:, :], gamma, ALU.mult))
                done(tt(b_out[:, :], bnv[:, :, 0], s_out[:, :], ALU.mult))
                return tt(b_out[:, :], beta, b_out[:, :], ALU.subtract)

            def add_back(base):
                for t in range(TILES):
                    dve.wait_ge(S["z_turned"], base + t + 1)
                    tt(x_nm[0:ROWS, t, :], x_nm[0:ROWS, t, :], psS[t % 2][0:ROWS, :], ALU.add).then_inc(S["x_updated"], 1)

            def sums(h, b, layer, ps):
                dve.wait_ge(S["prob_used"], (layer * H + h + 1) * TILES)
                acc = acc_view(ps)
                rd = rden[0:ROWS, b, :]
                rd2 = rd.rearrange("p (u t) -> p u t", u=2)
                done(ts(rd2, acc[:, :, :, DH], TINY, None, ALU.max))
                done(dve.reciprocal(rd, rd))
                done(tt(head_sum[0:ROWS, :, :, :], acc[:, :, :, 0:DH], rd2.unsqueeze(3).to_broadcast([ROWS, 2, HEAD_HALF, DH]), ALU.mult))
                xs = x_nm[0:ROWS, :, :].rearrange("p t (h d) -> p t h d", h=H)[:, :, h, :]
                tt(xs, xs, head_sum[0:ROWS, :, :, :].rearrange("p u t d -> p (u t) d"), ALU.add).then_inc(S["acc_read"], 1)

            dve.wait_ge(S["counts_f32"], TILES)
            split_cols(dve, done, parts[0:ROWS, 0, :, :], split_rest[0:ROWS, 0, :], deg_col[0:ROWS, :]).then_inc(S["deg_split"], 1)
            dve.wait_ge(S["deg_wide"], 1)
            done(blocks_out(dve.tensor_copy, pos_b, psW[0], 128))
            ts(rdeg_b, pos_b, 1.0, None, ALU.max).then_inc(S["deg_rows"], 1)
            dve.wait_ge(S["deg_rows"], 1)
            done(dve.reciprocal(rdeg_b, rdeg_b))
            done(ts(rdeg_b, rdeg_b, 1.0 / HS, None, ALU.mult))
            done(dve.tensor_reduce(bnd[:, 0, 0:1], pos_b[0:1, :], AX, ALU.max))
            done(ts(bnd[:, 0, 0:1], bnd[:, 0, 0:1], EXACT16, None, ALU.is_gt))
            done(dve.tensor_copy(bounds_i[:, 3 * TILES:3 * TILES + 1], bnd[:, 0, 0:1]))
            done(ts(pos_b, pos_b, 1.0, None, ALU.min))
            phase_end(dve, 1)
            big = has_big_count(dve)
            ln_stats(0)
            for k in range(KD):
                if k % 2 == 0:
                    low_counts(0, k // 2, big)
                    dve.wait_ge(S["agg_full"], k // 2 + 1)
                tt(aggT[:, k, :], psW[k % 2][:, 0:N], rdeg_b, ALU.mult).then_inc(S["agg_read"], 1)
            dve.wait_ge(S["vec_in"], 16 * 10)
            bn_over_nodes(yT, lambda f: dve.wait_ge(S["y_out"], f + 1), ga0_c, be0_c, scl, shf).then_inc(S["y_stats"], 1)
            dve.wait_ge(S["x_plus_h"], TILES)
            add_back(0)
            phase_end(dve, 2)
            if layers >= 2:
                ln_stats(1)
                bn_over_nodes(hT, lambda f: dve.wait_ge(S["hT_made"], h_tiles(2)), g1_c, b1_c, scl1, shf1).then_inc(S["bn1_ready"], 1)
                done(dve.memset(v_perf[:, :, :, DH:VA], 1.0))
                dve.wait_ge(S["v_full"], 1)
                for b in range(PB):
                    c = dve.tensor_copy(v_perf[:, b, :, 0:DH], psS[b][:, :].rearrange("p (h d) -> p h d", h=H))
                c.then_inc(S["v_out"], 1)
                dve.wait_ge(S["qk_out"], 2)
                tt(sq, qkT, qkT, ALU.mult).then_inc(S["sq_made"], 1)
                dve.wait_ge(S["diag_full"], 1)
                for par in range(2):
                    for r, dst in enumerate((qdiag, kdiag)):
                        c = dve.tensor_copy(dst[:, par:H:2, :], psS[par][:, r * H:(r + 1) * H].rearrange("p (h b) -> p h b", b=PB))
                c.then_inc(S["diag_out"], 1)
                for h in range(H):
                    dve.wait_ge(S["uk_full"], h + 1)
                    dve.tensor_reduce(kmax[:, h:h + 1], psW[h % 2][:, 0:PB * MPERF], AX, ALU.max).then_inc(S["uk_max"], 1)
                dve.wait_ge(S["kmax_all"], 1)
                dve.wait_ge(S["diag_out"], 1)
                stt(kbias[:, :, :], kdiag[:, :, :], -1.0, kmaxa[:, :].unsqueeze(2).to_broadcast([128, H, PB]),
                    ALU.mult, ALU.subtract).then_inc(S["kbias_set"], 1)
                for h in range(H):
                    dve.wait_ge(S["kf_exp"], h + 1)
                    ts(kf[:, h, :], kf[:, h, :], MPERF ** -0.5, KEPS, ALU.mult, ALU.add).then_inc(S["kf_made"], 1)
                for h in range(H):
                    dve.wait_ge(S["uq_full"], h + 1)
                    done(dve.tensor_reduce(qmax[:, h, :], psW[h % 2][:, 0:PB * MPERF].rearrange("p (b m) -> p b m", b=PB), AX, ALU.max))
                    stt(qbias[:, h, :], qdiag[:, h, :], -1.0, qmax[:, h, :], ALU.mult, ALU.subtract).then_inc(S["uq_max"], 1)
                for h in range(H):
                    dve.wait_ge(S["qf_exp"], h + 1)
                    ts(qf[:, h, :], qf[:, h, :], MPERF ** -0.5, KEPS, ALU.mult, ALU.add).then_inc(S["qf_made"], 1)
                for h in range(H):
                    dve.wait_ge(S["kv_full"], h + 1)
                    dve.tensor_copy(kv_perf[:, h, :, :], psW[h % 2][:, 0:PB * VA].rearrange("p (b d) -> p b d", b=PB)).then_inc(S["kv_out"], 1)
                for h in range(H):
                    dve.wait_ge(S["at_full"], h + 1)
                    at = psW[h % 2][:, 512:512 + PB * VA].rearrange("p (b d) -> p b d", b=PB)
                    done(ts(pz[:, h, :], at[:, :, DH], KEPS, None, ALU.add))
                    done(dve.reciprocal(pz[:, h, :], pz[:, h, :]))
                    tt(attn[:, :, h * DH:(h + 1) * DH], at[:, :, 0:DH], pz[:, h, :].unsqueeze(2).to_broadcast([128, PB, DH]),
                       ALU.mult).then_inc(S["at_out"], 1)
                phase_end(dve, 3)
                for k in range(KD):
                    if k % 2 == 0:
                        low_counts(1, k // 2, big)
                        dve.wait_ge(S["agg_full"], 2 + k // 2 + 1)
                    done(stt(aggT[:, k, :], psW[k % 2][:, 0:N], scl1[:, k:k + 1], rdeg_b, ALU.mult, ALU.mult))
                    stt(aggT[:, k, :], pos_b, shf1[:, k:k + 1], aggT[:, k, :], ALU.mult, ALU.add).then_inc(S["agg_read"], 1)
                for f in range(KD):
                    dve.wait_ge(S["conv_out"], f + 1)
                    done(tt(yT[:, f, :], yT[:, f, :], hT[:, f, :], ALU.add))
                    tt(yT[:, f, 0:NPERF], yT[:, f, 0:NPERF], oT[:, f, :], ALU.add)
                    done(ts(yT[:, f, NPERF:N], yT[:, f, NPERF:N], oT[:, f, NPERF - 1:NPERF], None, ALU.add))
                bn_over_nodes(yT, lambda f: None, g2_c, b2_c, scl, shf).then_inc(S["y_stats"], 1)
                add_back(TILES)
            else:
                phase_end(dve, 3)
            phase_end(dve, 4)
            if layers >= 3:
                ln_stats(2)
                dve.wait_ge(S["w_in"], 16 * (7 + KD + 3))
                for t in range(TILES):
                    dve.wait_ge(S["wx_full"], t + 1)
                    tt(v_aug[0:ROWS, t, :, 0:DH], psS[t % 2][0:ROWS, :].rearrange("p (h d) -> p h d", h=H),
                       wb_row[0:ROWS, :].rearrange("p (h d) -> p h d", h=H), ALU.add).then_inc(S["wx_out"], 1)
                    dve.wait_ge(S["wx_mul"], t + 1)
                    dve.tensor_reduce(tcol[0:ROWS, :, t], a_mul[0:ROWS, 0, :, :], AX, ALU.add)
                    dve.tensor_reduce(bcol[0:ROWS, :, t], a_mul[0:ROWS, 1, :, :], AX, ALU.add).then_inc(S["ab_cols"], 1)
                dve.wait_ge(S["ab_cols"], TILES)
                split_cols(dve, done, b_parts[0:ROWS, :, :, :], split_rest[0:ROWS, :, :], bcol[0:ROWS, :, :]).then_inc(S["b_parts_set"], 1)
                done(tt(tcol[0:ROWS, :, :], tcol[0:ROWS, :, :], ab_row[0:ROWS, :].unsqueeze(2).to_broadcast([ROWS, H, TILES]), ALU.add))
                ts(t02[0:ROWS, :, :], tcol[0:ROWS, :, :], 0.2, None, ALU.mult)
                ts(b08[0:ROWS, :, :], bcol[0:ROWS, :, :], 0.8, None, ALU.mult)
                ts(b02[0:ROWS, :, :], bcol[0:ROWS, :, :], 0.2, None, ALU.mult)
                done(ts(mask[0:ROWS, :, :], cnt[0:ROWS, :, :], 0.0, NEG, ALU.is_equal, ALU.mult))
                phase_end(dve, 5)

                def largest(h, b, k):
                    if not (isinstance(h, int) and h == 0 and k < 2):
                        dve.wait_ge(S["maxed"], h * TILES + k - 1)
                    take_wait()
                    dve.tensor_tensor_reduce(junk[0:ROWS, k % 2, :], b_row[b][0:ROWS, :], mask[0:ROWS, k, :], 1.0, 2 * NEG,
                                             ALU.add, ALU.max, mcol[0:ROWS, b, k:k + 1]).then_inc(S["maxed"], 1)

                def make_prob(n, k, ordered=True):
                    dve.wait_ge(S["ex_made"], n + 1)
                    if ordered:
                        dve.wait_ge(S["prob_used"], n - 1)
                    stt(prob[k % 2][0:ROWS, :], ex2[k % 2][0:ROWS, :], CAP, cntT[0:ROWS, k, :],
                        ALU.min, ALU.mult).then_inc(S["prob_made"], 1)

                def head(h, b):
                    first, last, before = (isinstance(h, int) and h == k for k in (0, H - 1, H - 2))
                    dve.wait_ge(S["uw_out"], 2 * h + 2)
                    for t in range(TILES):
                        n = h * TILES + t
                        stt(score[(b * TILES + t) % 4][0:ROWS, :], u_row[b][0:ROWS, :], b08[0:ROWS, h, t:t + 1], w_row[b][0:ROWS, :],
                            ALU.add, ALU.max).then_inc(S["score_made"], 1)
                        if t < TILES - LEAD and not last:
                            largest(h + 1, 1 - b, t + LEAD)
                        if t >= TILES - LEAD and not (last or before):
                            if t == TILES - LEAD:
                                dve.wait_ge(S["b_out"], h + 3)
                            largest(h + 2, b, t + LEAD - TILES)
                        if t == 3 and not first:
                            sums(h - 1, 0, 0, psW[1])
                        if not (first and t < 2):
                            make_prob(n - 2, (t - 2) % TILES, not (first and t < 4))

                SUM_STEPS = 3
                dve.wait_ge(S["b_out"], 1)
                for k in range(TILES):
                    largest(0, 0, k)
                dve.wait_ge(S["b_out"], 2)
                for k in range(LEAD):
                    largest(1, 1, k)
                head(0, 0)
                first = done.n
                with dve.Fori(0, 2) as g:
                    done.base = g * 2 * SUM_STEPS
                    head(2 * g + 1, 1)
                    head(2 * g + 2, 0)
                assert done.n - first == 2 * SUM_STEPS
                done.base, done.n = 0, first + 4 * SUM_STEPS
                for h in (5, 6, 7):
                    head(h, h % 2)
                for t in (TILES - 2, TILES - 1):
                    make_prob((H - 1) * TILES + t, t)
                sums(H - 1, 0, 0, psW[1])
            else:
                phase_end(dve, 5)
            phase_end(dve, 6)
            if layers >= 4:
                ln_stats(3)
                for n in range(2 * KD):
                    part, scale = ((k_part, 1.0), (q_part, DH ** -0.5))[n // KD]
                    ps = psW[n % 2][:, 0:N]
                    dve.wait_ge(S["proj3_1"], n + 1)
                    stt(ps, ps, scale, part[0][:, n % KD, :], ALU.mult, ALU.subtract).then_inc(S["proj3_rest"], 1)
                    dve.wait_ge(S["proj3_2"], n + 1)
                    tt(part[2][:, n % KD, :], ps, part[1][:, n % KD, :], ALU.subtract).then_inc(S["proj3_out"], 1)
                for t in range(TILES):
                    dve.wait_ge(S["v3_full"], t + 1)
                    dve.tensor_copy(v_aug[0:ROWS, t, :, 0:DH], psS[t % 2][0:ROWS, :].rearrange("p (h d) -> p h d", h=H)).then_inc(S["v3_out"], 1)
                done(ts(mask3[0:ROWS, :, :], cntT[0:ROWS, :, :], 0.0, NEG, ALU.is_equal, ALU.mult))
                phase_end(dve, 7)

                def maximum(t, i, use):
                    dve.wait_ge(S[f"s{i}_full"], use)
                    take_wait()
                    return dve.tensor_tensor_reduce(psW[i][0:ROWS, 0:N], psW[i][0:ROWS, 0:N], mask3[0:ROWS, t, :], 1.0, 2 * NEG,
                                                    ALU.add, ALU.max, mcol[0:ROWS, 0, t:t + 1])

                def head3(h, more, last):
                    for t in range(TILES):
                        steps = MAX_STEPS3[t] if more else ()
                        for k in steps[0:1]:
                            maximum(k, 1, s1_use(h + 1, k)).then_inc(S["s1_free"], 1)
                        if last is not None and t == 1:
                            sums(last, 0, 1, small)
                        if more and t == TILES - 1:
                            dve.drain().then_inc(S["m_made"], 1)
                        n = (H + h) * TILES + t
                        dve.wait_ge(S["s0_free"], s0_use(h, t) + 1)
                        dve.wait_ge(S["prob_used"], n - 1)
                        stt(prob3[t % 2][0:ROWS, :], ex3[t % 2][0:ROWS, :], CAP, cnt[0:ROWS, t, :], ALU.min, ALU.mult).then_inc(S["prob_made"], 1)
                        for k in steps[1:2]:
                            maximum(k, 1, s1_use(h + 1, k)).then_inc(S["s1_free"], 1)

                for t in range(TILES):
                    maximum(t, t % 2, t // 2 + 1).then_inc(S[f"s{t % 2}_free"], 1)
                dve.drain().then_inc(S["m_made"], 1)
                head3(0, True, None)
                per, first = SUM_STEPS, done.n
                with dve.Fori(0, H - 2) as h:
                    done.base = h * per
                    head3(h + 1, True, h)
                assert done.n - first == per
                done.base, done.n = 0, first + per * (H - 2)
                head3(H - 1, False, H - 2)
                sums(H - 1, 0, 1, small)
            else:
                phase_end(dve, 7)
            phase_end(dve, 8)

        @block.tensor
        def _(pe):
            def turn(dst, src, k):
                return pe.transpose(dst, src, ident[0:k, 0:k])

            def turn_parts(ps, src):
                return pe.matmul(ps[0:3 * TILES, 0:ROWS], src.rearrange("p r t -> p (r t)"), ident_bf[0:ROWS, 0:ROWS], start=True, stop=True)

            pe.wait_ge(S["consts_set"], 1)
            pe.wait_ge(S["edges_f32"], 1)
            for s in range(2):
                for g in range(2):
                    at = (2 * s + g) * PAIRS
                    m = turn(psS[0][0:CHUNK, at:at + PAIRS], e_f[0:PAIRS, s, g * CHUNK:(g + 1) * CHUNK], PAIRS)
            m.then_inc(S["edges_turned"], 1)
            pe.wait_ge(S["pair_bounds"], 1)
            for r in range(2):
                m = turn(psS[1][0:1, r * PAIRS:(r + 1) * PAIRS], pair_mm[0:PAIRS, r:r + 1], PAIRS)
            m.then_inc(S["bounds_turned"], 1)
            pe.wait_ge(S["bounds_set"], 1)

            def turn_counts(t):
                pe.wait_ge(S["counts_f32"], t + 1)
                for r, (lo, hi) in enumerate(((0, 4), (4, 8), (8, 10))):
                    n = 3 * t + r
                    if n >= 2:
                        pe.wait_ge(S["counts_turn_read"], n - 1)
                    if n == 2:
                        pe.wait_ge(S["edge_cols"], 1)
                    for j in range(lo, hi):
                        m = turn(psS[n % 2][0:ROWS, (j - lo) * ROWS:(j - lo + 1) * ROWS], cnt_f[t % 2][0:ROWS, j * ROWS:(j + 1) * ROWS], ROWS)
                    m.then_inc(S["counts_turning"], 1)

            def zero_matmul(ps, start, stop):
                for lo, hi in ((0, 512), (512, 1024), (1024, N)):
                    mm = pe.matmul(ps[0:ROWS, lo:hi], zero_bf[:, 0:ROWS], zero_bf[:, 0:hi - lo], start=start, stop=stop)
                return mm

            for t in range(TILES):
                start, end = (pe.value_load(bounds_i[0:1, i * TILES + t:i * TILES + t + 1], min_val=i - 1,
                                            max_val=TILES * PAIRS) for i in (1, 2))
                if t >= 2:
                    pe.wait_ge(S["counts_f32"], t - 1)
                if t == 0:
                    pe.wait_ge(S["edge_cols"], 1)
                zero_matmul(psW[t % 2], True, False)
                with pe.Fori(start, end) as n:
                    for g in range(2):
                        pe.wait_ge(S[f"hot{g}_made"], n + 1)
                        wide_matmul(pe, psW[t % 2], ROWS, hot_dst[g][0:ROWS, 0:ROWS], hot_src[g][0:ROWS, :], False, False).then_inc(S[f"hot{g}_free"], 1)
                zero_matmul(psW[t % 2], False, True).then_inc(S["tile_counted"], 1)
                if t >= 1:
                    turn_counts(t - 1)
            turn_counts(TILES - 1)
            pe.wait_ge(S["counts_turn_read"], 3 * TILES)
            pe.wait_ge(S["deg_split"], 1)
            turn_parts(psS[1], parts[0:ROWS, 0, :, :]).then_inc(S["deg_turned"], 1)
            pe.wait_ge(S["deg_row_out"], 1)

            def spread(ps, row, signal):
                for t in range(TILES):
                    m = pe.matmul(block_at(ps, 128, t), sel[:, t, :], row, start=True, stop=True)
                m.then_inc(signal, 1)

            spread(psW[0], row_sb[:, 0, :], S["deg_wide"])
            phase_end(pe, 1)

            def turn_h(l):
                if l < 2:
                    for t in range(TILES):
                        pe.wait_ge(S["h_made"], TILES * l + t + 1)
                        if t >= 2:
                            pe.wait_ge(S["hT_made"], h_tiles(l) + t - 1)
                        for k in range(KD):
                            m = turn(psS[t % 2][:, k * ROWS:(k + 1) * ROWS], h32[t % 2][0:ROWS, 128 * k:128 * k + 128], ROWS)
                        m.then_inc(S["h_turned"], 1)
                    return
                for k in range(KD):
                    if k >= 2:
                        pe.wait_ge(S["hT_made"], h_tiles(l) + k - 1)
                    for t in range(TILES):
                        if k == 0:
                            pe.wait_ge(S["h_made"], TILES * l + t + 1)
                        m = turn(block_at(psW[k % 2], 128, t), h_nm[0:ROWS, t, 128 * k:128 * k + 128], ROWS)
                    m.then_inc(S["h_turned"], 1)

            def zero_all(ps, start, stop):
                for lo, hi in ((0, 512), (512, 1024), (1024, N)):
                    mm = pe.matmul(ps[:, lo:hi], zero_bf[:, 0:128], zero_bf[:, 0:hi - lo], start=start, stop=stop, skip_group_check=True)
                return mm

            def aggregate(l, big):
                def tile(half, j, start):
                    for kk in range(2):
                        k = 2 * half + kk
                        for part in h_pair:
                            m = wide_matmul(pe, psW[kk], 128, part[0:ROWS, j, 128 * k:128 * k + 128], cntT_16[j % 2][0:ROWS, :],
                                            start and part is h_pair[0], False)
                    return m

                pe.wait_ge(S["h_split"], TILES * (l + 1))
                for half in range(2):
                    if half == 1:
                        pe.wait_ge(S["agg_read"], l * KD + 2)
                    first = TILES * (2 * l + half)
                    for j in range(TILES):
                        pe.wait_ge(S["cT_wide"], first + j + 1)
                        tile(half, j, j == 0).then_inc(S["cT_used"], 1)
                    with pe.If(big > 0):
                        for j in range(TILES):
                            pe.wait_ge(S["lo_made"], first + j + 1)
                            tile(half, j, False).then_inc(S["lo_used"], 1)
                    for kk in range(2):
                        m = zero_all(psW[kk], False, True)
                    m.then_inc(S["agg_full"], 1)

            def turn_back(base):
                for t in range(TILES):
                    if t >= 2:
                        pe.wait_ge(S["x_updated"], base + t - 1)
                    for k in range(KD):
                        m = turn(psS[t % 2][0:ROWS, 128 * k:128 * k + 128], yT[:, k, t * ROWS:(t + 1) * ROWS], 128)
                    m.then_inc(S["z_turned"], 1)

            big = has_big_count(pe)
            turn_h(0)
            pe.wait_ge(S["w_in"], 32)
            pe.wait_ge(S["hT_made"], TILES)
            for n in range(2 * KD):
                if n >= 2:
                    pe.wait_ge(S["w_turn_read"], n - 1)
                w = w_nat[n // KD]
                for o in range(KD):
                    m = turn(psS[n % 2][:, 128 * o:128 * o + 128], w[:, o, 128 * (n % KD):128 * (n % KD) + 128], 128)
                m.then_inc(S["w_turned"], 1)
            aggregate(0, big)
            pe.wait_ge(S["w_turn_read"], 2 * KD)
            pe.wait_ge(S["agg_read"], KD)
            for f in range(KD):
                if f >= 2:
                    pe.wait_ge(S["y_out"], f - 1)
                for k in range(2 * KD):
                    w, r = ((w_a, aggT), (w_b, hT))[k // KD]
                    m = wide_matmul(pe, psW[f % 2], 128, w[:, k % KD, 128 * f:128 * f + 128], r[:, k % KD, :], k == 0, k == 2 * KD - 1)
                m.then_inc(S["y_full"], 1)
            pe.wait_ge(S["y_scaled"], KD)
            turn_back(0)
            phase_end(pe, 2)
            if layers >= 2:
                turn_h(1)
                pe.wait_ge(S["w_in"], 16 * 6)
                pe.wait_ge(S["hT_made"], h_tiles(2))
                for r, w in enumerate((w_a, w_b)):
                    for f in range(KD):
                        for k in range(KD):
                            m = pe.matmul(psW[r][:, NPERF * f:NPERF * f + NPERF], w[:, k, 128 * f:128 * f + 128], hT[:, k, 0:NPERF],
                                          start=(k == 0), stop=(k == KD - 1))
                    m.then_inc(S["qk_full"], 1)
                for b in range(PB):
                    for k in range(KD):
                        m = pe.matmul(psS[b][:, :], hT[:, k, 128 * b:128 * b + 128], wv[:, k, :], start=(k == 0), stop=(k == KD - 1))
                m.then_inc(S["v_full"], 1)
                for b in range(PB):
                    m = turn(psW[1][:, 1024 + 128 * b:1024 + 128 * b + 128], proj_nat[:, b, :], 128)
                m.then_inc(S["proj_turned"], 1)
                pe.wait_ge(S["v_out"], 1)
                pe.wait_ge(S["sq_made"], 1)
                for par in range(2):
                    p = slice(DH * par, DH * par + DH)
                    for r in range(2):
                        for hh in range(H // 2):
                            for b in range(PB):
                                at = r * H + hh * PB + b
                                m = pe.matmul(psS[par][:, at:at + 1], sq[p, r, NPERF * hh + 128 * b:NPERF * hh + 128 * b + 128],
                                              half_c[p, :], start=True, stop=True)
                m.then_inc(S["diag_full"], 1)
                pe.wait_ge(S["proj_out"], 1)

                def features(r, h):
                    p = slice(DH * (h % 2), DH * (h % 2) + DH)
                    for b in range(PB):
                        at = NPERF * (h // 2) + 128 * b
                        m = pe.matmul(psW[h % 2][:, MPERF * b:MPERF * b + MPERF], qkT[p, r, at:at + 128], projT[p, :], start=True, stop=True)
                    return m

                for h in range(H):
                    if h >= 2:
                        pe.wait_ge(S["uk_max"], h - 1)
                    features(1, h).then_inc(S["uk_full"], 1)
                for h in range(H):
                    pe.wait_ge(*((S["uk_max"], H) if h < 2 else (S["kf_exp"], h - 1)))
                    features(1, h).then_inc(S["uk2_full"], 1)
                for h in range(H):
                    pe.wait_ge(*((S["kf_exp"], H) if h < 2 else (S["qf_exp"], h - 1)))
                    features(0, h).then_inc(S["uq_full"], 1)
                pe.wait_ge(S["kf_made"], H)
                pe.wait_ge(S["qf_exp"], H)
                for h in range(H):
                    if h >= 2:
                        pe.wait_ge(S["kv_out"], h - 1)
                    for mb in range(PB):
                        for b in range(PB):
                            m = pe.matmul(psW[h % 2][:, VA * mb:VA * mb + VA], kf[:, h, MPERF * b + 128 * mb:MPERF * b + 128 * mb + 128],
                                          v_perf[:, b, h, :], start=(b == 0), stop=(b == PB - 1))
                    m.then_inc(S["kv_full"], 1)
                pe.wait_ge(S["diag_out"], 1)
                for h in range(H):
                    pe.wait_ge(S["qf_made"], h + 1)
                    if h >= 2:
                        pe.wait_ge(S["qfT_out"], h - 1)
                    for mb in range(PB):
                        for b in range(PB):
                            m = turn(psS[h % 2][:, NPERF * mb + 128 * b:NPERF * mb + 128 * b + 128],
                                     qf[:, h, MPERF * b + 128 * mb:MPERF * b + 128 * mb + 128], 128)
                    m.then_inc(S["qf_turned"], 1)
                pe.wait_ge(S["qfT_out"], H)
                for h in range(H):
                    pe.wait_ge(S["kv_out"], h + 1)
                    if h >= 2:
                        pe.wait_ge(S["at_out"], h - 1)
                    for b in range(PB):
                        for mb in range(PB):
                            m = pe.matmul(psW[h % 2][:, 512 + VA * b:512 + VA * b + VA], qfT[:, h, NPERF * mb + 128 * b:NPERF * mb + 128 * b + 128],
                                          kv_perf[:, h, mb, :], start=(mb == 0), stop=(mb == PB - 1))
                    m.then_inc(S["at_full"], 1)
                pe.wait_ge(S["at_out"], H)
                for k in range(KD):
                    for b in range(PB):
                        m = turn(psW[0][:, NPERF * k + 128 * b:NPERF * k + 128 * b + 128], attn[:, b, 128 * k:128 * k + 128], 128)
                m.then_inc(S["at_turned"], 1)
                pe.wait_ge(S["atT_out"], 1)
                for f in range(KD):
                    for k in range(KD):
                        m = pe.matmul(psW[1][:, NPERF * f:NPERF * f + NPERF], wo[:, k, 128 * f:128 * f + 128], attnT[:, k, :],
                                      start=(k == 0), stop=(k == KD - 1))
                m.then_inc(S["o_full"], 1)
                phase_end(pe, 3)
                aggregate(1, big)
                pe.wait_ge(S["w_in"], 16 * 7)
                pe.wait_ge(S["agg_read"], 2 * KD)
                for f in range(KD):
                    if f >= 2:
                        pe.wait_ge(S["conv_out"], f - 1)
                    for k in range(KD):
                        m = wide_matmul(pe, psW[f % 2], 128, w_a[:, k, 128 * f:128 * f + 128], aggT[:, k, :], k == 0, k == KD - 1)
                    m.then_inc(S["conv_full"], 1)
                pe.wait_ge(S["y_scaled"], 2 * KD)
                turn_back(TILES)
            else:
                phase_end(pe, 3)
            phase_end(pe, 4)
            if layers >= 3:
                turn_h(2)
                pe.wait_ge(S["hT_made"], h_tiles(3))
                pe.wait_ge(S["w_in"], 16 * (7 + KD + 3))
                for t in range(TILES):
                    if t >= 2:
                        pe.wait_ge(S["wx_out"], t - 1)
                    for k in range(KD):
                        m = pe.matmul(psS[t % 2][0:ROWS, :], hT[:, k, t * ROWS:(t + 1) * ROWS],
                                      w_gat[:, k, :, :].rearrange("p h d -> p (h d)"), start=(k == 0), stop=(k == KD - 1))
                    m.then_inc(S["wx_full"], 1)
                phase_end(pe, 5)

                def b_turn(h):
                    turn_parts(psS[1], b_parts[0:ROWS, h, :, :]).then_inc(S["b_turned"], 1)

                def b_spread(h):
                    pe.wait_ge(S["b_rows"], h + 1)
                    if not isinstance(h, int) or h >= 2:
                        pe.wait_ge(S["uw_out"], 2 * h - 2)
                    elif h == 1:
                        pe.wait_ge(S["b_out"], 1)
                    spread(psW[0], row_sb[:, 0, :], S["b_wide"])

                def uw_turn(h):
                    pe.wait_ge(S["uw_cols"], h + 1)
                    for r in range(2):
                        m = turn_parts(psS[1][:, r * ROWS:(r + 1) * ROWS], parts[0:ROWS, r, :, :])
                    m.then_inc(S["uw_turned"], 1)

                def uw_spread(h, r):
                    if r == 0:
                        pe.wait_ge(S["uw_rows"], h + 1)
                        if not isinstance(h, int) or h < H - 1:
                            pe.wait_ge(S["b_out"], h + 2)
                    else:
                        pe.wait_ge(S["uw_out"], 2 * h + 1)
                    spread(psW[0], row_sb[:, r, :], S["uw_wide"])

                def weigh(h, layer, t, ps, prob):
                    pe.wait_ge(S["prob_made"], (layer * H + h) * TILES + t + 1)
                    if t == 0:
                        pe.wait_ge(S["acc_read"], layer * H + h)
                    acc = acc_view(ps)
                    for i in range(TILES):
                        m = pe.matmul(acc[:, i // HEAD_HALF, i % HEAD_HALF, :], prob[t % 2][0:ROWS, i * ROWS:(i + 1) * ROWS],
                                      v_aug[0:ROWS, t, h, :], start=(t == 0 and i % HEAD_HALF == 0), stop=(t == TILES - 1),
                                      skip_group_check=True)
                    m.then_inc(S["prob_used"], 1)

                def head(h):
                    first, last, before = (isinstance(h, int) and h == k for k in (0, H - 1, H - 2))
                    for t in range(TILES):
                        if t in (7, 8) and not last:
                            uw_spread(h + 1, t - 7)
                        if t >= 2:
                            weigh(h, 0, t - 2, psW[1], prob)
                        elif not first:
                            weigh(h - 1, 0, TILES - 2 + t, psW[1], prob)
                        if t in (0, 1) and not (last or before):
                            b_turn(h + 2) if t == 0 else b_spread(h + 2)
                        if t == 6 and not last:
                            uw_turn(h + 1)

                pe.wait_ge(S["b_parts_set"], 1)
                for h in range(2):
                    if h == 1:
                        pe.wait_ge(S["b_rows"], 1)
                    b_turn(h)
                    b_spread(h)
                uw_turn(0)
                for r in range(2):
                    uw_spread(0, r)
                head(0)
                with pe.Fori(0, 2) as g:
                    head(2 * g + 1)
                    head(2 * g + 2)
                for h in (5, 6, 7):
                    head(h)
                for t in (TILES - 2, TILES - 1):
                    weigh(H - 1, 0, t, psW[1], prob)
            else:
                phase_end(pe, 5)
            phase_end(pe, 6)
            if layers >= 4:
                turn_h(3)
                pe.wait_ge(S["hT_made"], h_tiles(4))
                pe.wait_ge(S["w_in"], 16 * (7 + KD + 6))
                for n in range(2 * KD):
                    if n >= 2:
                        pe.wait_ge(S["proj3_out"], n - 1)
                    w = (w_k, w_q)[n // KD]
                    for k in range(KD):
                        m = wide_matmul(pe, psW[n % 2], 128, w[:, k, 128 * (n % KD):128 * (n % KD) + 128], hT[:, k, :], k == 0, k == KD - 1)
                    m.then_inc(S["proj3_full"], 1)
                for t in range(TILES):
                    if t >= 2:
                        pe.wait_ge(S["v3_out"], t - 1)
                    for k in range(KD):
                        m = pe.matmul(psS[t % 2][0:ROWS, :], hT[:, k, t * ROWS:(t + 1) * ROWS], w_v[:, k, :], start=(k == 0), stop=(k == KD - 1))
                    m.then_inc(S["v3_full"], 1)
                phase_end(pe, 7)
                for i in range(2):
                    pe.sem_inc(S[f"s{i}_free"], 1)

                cuts = sorted({512, 1024, *range(0, N + 1, ROWS)})
                pieces = list(zip(cuts, cuts[1:]))

                def score_for_max(b, t, i, use):
                    pe.wait_ge(S[f"s{i}_free"], use)
                    own = slice(t * ROWS, (t + 1) * ROWS)
                    wide_matmul(pe, psW[i], ROWS, q12[b][:, own], k11[b], True, False)
                    wide_matmul(pe, psW[i], ROWS, q12[b][:, own], k22[b], False, True).then_inc(S[f"s{i}_full"], 1)

                def maxima_row(h):
                    pe.wait_ge(S["m_split"], h + 1)
                    pe.wait_ge(S["s0_free"], s0_use(h, -1))
                    turn_parts(psW[0], parts[0:ROWS, 0, :, :]).then_inc(S["s0_full"], 1)

                def head(h, b, g_next, last):
                    for t in range(TILES):
                        pe.wait_ge(S["s0_free"], s0_use(h, t))
                        own = slice(t * ROWS, (t + 1) * ROWS)
                        for lo, hi in pieces:
                            j = lo // ROWS
                            pe.matmul(psW[0][0:ROWS, lo:hi], sel[:, j, 0:ROWS], row_sb[:, 0, lo - j * ROWS:hi - j * ROWS],
                                      start=lo in (0, 512, 1024), stop=False, skip_group_check=True)
                        for keys, queries in ((k11, q12), (k22, q12), (k31, q13)):
                            m = wide_matmul(pe, psW[0], ROWS, keys[b][:, own], queries[b], False, keys is k31)
                        m.then_inc(S["s0_full"], 1)
                        steps = MAX_STEPS3[t] if g_next is not None else ()
                        for k in steps[0:1]:
                            if k == 0:
                                pe.wait_ge(S[f"stack{1 - b}_set"], 160 * (g_next + 1))
                            score_for_max(1 - b, k, 1, s1_use(h + 1, k))
                        if t >= 2:
                            weigh(h, 1, t - 2, small, prob3)
                        elif last is not None:
                            weigh(last, 1, TILES - 2 + t, small, prob3)
                        for k in steps[1:2]:
                            score_for_max(1 - b, k, 1, s1_use(h + 1, k))
                    if g_next is not None:
                        maxima_row(h + 1)

                pe.wait_ge(S["stack0_set"], 160)
                for t in range(TILES):
                    score_for_max(0, t, t % 2, t // 2 + 1)
                maxima_row(0)
                head(0, 0, 0, None)
                with pe.Fori(0, H // 2 - 1) as g:
                    head(2 * g + 1, 1, g + 1, 2 * g)
                    head(2 * g + 2, 0, g + 1, 2 * g + 1)
                head(H - 1, 1, None, H - 2)
                for t in (TILES - 2, TILES - 1):
                    weigh(H - 1, 1, t, small, prob3)
            else:
                phase_end(pe, 7)
            phase_end(pe, 8)


INS = ["x", "src", "dst", "L0_gnn_W_l", "L0_gnn_b_l", "L0_gnn_W_r", "L0_gnn_gamma", "L0_gnn_beta", "L1_gnn_norm1_g",
       "L1_gnn_norm1_b", "L1_gnn_norm2_g", "L1_gnn_norm2_b", "L1_gnn_W_conv", "L1_gnn_b_conv", "L1_gnn_Wq", "L1_gnn_Wk",
       "L1_gnn_Wv", "L1_gnn_Wo", "L1_gnn_proj", "L2_gnn_Ws", "L2_gnn_Wb", "L2_gnn_a_w", "L2_gnn_a_b", "L3_gnn_W"]


def kernel(**inputs):
    import numpy as np
    import concourse.bacc as bacc
    from concourse.bass_utils import run_bass_kernel_spmd as run

    nc = bacc.Bacc("TRN2", target_bir_lowering=False, num_devices=1)
    arrays, aps = {}, {}
    for name in INS:
        arr = np.ascontiguousarray(inputs[name])
        arrays[f"in_{name}"] = arr
        aps[name] = nc.dram_tensor(f"in_{name}", arr.shape, mybir.dt.from_np(arr.dtype), kind="ExternalInput").ap()
    out = nc.dram_tensor("out", (N, D), F32, kind="ExternalOutput").ap()
    gnn_program(nc, aps, out)
    r = run(nc, [arrays], core_ids=[0])
    return r.results[0]["out"]
```

```python
from contextlib import ExitStack

import concourse.bass as bass
from concourse import mybir

ALU = mybir.AluOpType
ACT = mybir.ActivationFunctionType
AX = mybir.AxisListType.X
F32, BF16, F16 = mybir.dt.float32, mybir.dt.bfloat16, mybir.dt.float16
I32, I16 = mybir.dt.int32, mybir.dt.int16
RMAX = bass.bass_isa.ReduceOp.max

N, E, D = 1250, 20000, 512
TILES, ROWS = 10, 125
KD = D // 128
CHUNK = 125
CHUNKS = 4
GROUPS = E // (CHUNKS * CHUNK)
H, DH = 8, 64
VA = DH + 1
NPERF, MPERF = 256, 256
PB = NPERF // 128
EPS, KEPS = 1e-5, 1e-6
NEG = -1e30
HS = 2048.0
EXACT16 = 2048.0
RING = 4
TINY = 1e-30
HEAD_HALF = 5
SIZE = {F32: 4, I32: 4, BF16: 2, F16: 2, I16: 2}


def wide_matmul(pe, ps, rows, lhsT, rhs, start, stop):
    for lo, hi in ((0, 512), (512, 1024), (1024, N)):
        mm = pe.matmul(ps[0:rows, lo:hi], lhsT, rhs[:, lo:hi], start=start, stop=stop, skip_group_check=True)
    return mm


def block_at(ps, rows, t):
    at = 512 * (t // 4) + ROWS * (t % 4)
    return ps[0:rows, at:at + ROWS]


def blocks_out(copy, dst, ps, rows):
    banks = ps[0:rows, :].rearrange("p (b c) -> p b c", b=3)
    copy(dst[:, 0:1000].rearrange("p (b c) -> p b c", b=2), banks[:, 0:2, 0:500])
    return copy(dst[:, 1000:N], banks[:, 2, 0:250])


def gnn_program(nc, a, out, layers=4):
    ctx = ExitStack()
    with ctx:
        def sb(name, shape, dt=F32):
            return ctx.enter_context(nc.sbuf_tensor(name, shape, dt))

        def sem(name):
            return ctx.enter_context(nc.semaphore(name))

        x_nm = sb("x_nm", [128, TILES, D])
        cnt = sb("cnt", [128, TILES, N], I16)
        cntT = sb("cntT", [128, TILES, N], I16)
        ident = sb("ident", [128, 128])
        ident_bf = sb("ident_bf", [128, 128], BF16)
        sel = sb("sel", [3 * TILES, TILES, 128], BF16)
        b_parts = sb("b_parts", [128, 2, H, 3, TILES], BF16)
        parts = sb("parts", [128, 3, TILES], BF16)
        split_rest = sb("split_rest", [128, H, TILES])
        zero_bf = sb("zero_bf", [1, 512], BF16)
        deg_col = sb("deg_col", [128, TILES])
        row_sb = sb("row_sb", [3 * TILES, 2, 2, ROWS], BF16)
        bn6 = sb("bn6", [128, TILES, 6])
        mv = sb("mv", [128, TILES, 2])
        rstd = sb("rstd", [128, TILES])
        nbias = sb("nbias", [128, TILES])
        vec = sb("vec", [128, 8, KD])
        bl_c, ga0_c, be0_c, g1_c, b1_c, g2_c, b2_c, bc_c = [vec[:, i, :] for i in range(8)]
        bns = sb("bns", [128, KD, 3, 6])
        bnv = sb("bnv", [128, KD, 2])
        scl = sb("scl", [128, KD])
        shf = sb("shf", [128, KD])
        scl1 = sb("scl1", [128, KD])
        shf1 = sb("shf1", [128, KD])
        bounds_i = sb("bounds_i", [1, 3 * TILES + 1], I32)
        var_eps = sb("var_eps", [128, TILES])
        root = sb("root", [128, TILES])
        half_c = sb("half_c", [128, 1])
        proj_nat = sb("proj_nat", [128, PB, 2 * DH])
        projT = sb("projT", [128, MPERF])
        qdiag = sb("qdiag", [128, H, PB])
        kdiag = sb("kdiag", [128, H, PB])
        qmax = sb("qmax", [128, H, PB])
        kmax = sb("kmax", [128, H])
        kmaxa = sb("kmaxa", [128, H])
        qbias = sb("qbias", [128, H, PB])
        kbias = sb("kbias", [128, H, PB])
        pz = sb("pz", [128, H, PB])
        tcol = sb("tcol", [128, H, TILES])
        bcol = sb("bcol", [128, H, TILES])
        t08 = sb("t08", [128, H, TILES])
        b02 = sb("b02", [128, H, TILES])
        neg_max = sb("neg_max", [128, TILES])
        mcol = sb("mcol", [128, TILES])
        rden = sb("rden", [128, TILES])
        head_sum = sb("head_sum", [128, 2, HEAD_HALF, DH])
        AW = 31584
        arena = sb("arena", [128, AW])

        def region(off, shape, dt=F32):
            n = 1
            for s in shape:
                n *= s
            words = (n * SIZE[dt] + 3) // 4
            assert off + words <= AW, (off, words)
            v = arena[:, off:off + words]
            if dt != F32:
                v = v.bitcast(dt)
            if len(shape) == 2:
                v = v.rearrange("p (a b) -> p a b", a=shape[0])
            if len(shape) == 3:
                v = v.rearrange("p (a b c) -> p a b c", a=shape[0], b=shape[1])
            return v

        h_nm = region(0, [TILES, D])
        hT = region(5120, [KD, N])
        rdeg_b = region(10120, [N])
        pos_b = region(11370, [N])
        h_pair = [region(2560 * i, [TILES, D], F16) for i in range(2)]
        G = 13644
        h32 = [region(G + 5000 + 512 * i, [D]) for i in range(RING)]
        hot_src = region(0, [2, CHUNKS, N], BF16)
        hot_dst = region(G, [2, CHUNKS, 128], BF16)
        cnt_f = [region(G + 1400 + 1250 * i, [N]) for i in range(2)]
        iota_h = region(G + 3900, [N], F16)
        e_raw = region(10120, [2, CHUNKS * CHUNK], I32)
        e_f = region(11120, [2, CHUNKS * CHUNK])
        e_col = region(G + 5530, [2, GROUPS, CHUNKS])
        group_mm = region(G + 5900, [2])
        group_row = arena[0:1, G + 6000:G + 6000 + 2 * GROUPS]
        tile_lo = arena[0:1, G + 6160:G + 6170]
        up_row = arena[0:1, G + 6200:G + 6200 + GROUPS]
        down_row = arena[0:1, G + 6280:G + 6280 + GROUPS]
        flag = [arena[0:1, G + 6400 + 800 * i:G + 6400 + 800 * i + TILES * GROUPS].rearrange("p (t q) -> p t q", t=TILES)
                for i in range(2)]
        bnd = arena[0:1, G + 8000:G + 8080].rearrange("p (r t) -> p r t", r=8)
        aggT = region(G, [KD, N])
        yT = region(G + 5000, [KD, N])
        w_nat = [region(G + 8100 + 7600 * i, [KD, D]) for i in range(2)]
        w_a = region(G + 10300, [KD, D])
        w_b = region(G + 12348, [KD, D])
        cntT_16 = [region(G + 14400 + 625 * i, [N], F16) for i in range(2)]
        oT = region(G + 16500, [KD, NPERF])
        wo = region(G + 14400, [KD, D])
        wv = region(G, [KD, D])
        qf = region(G, [H, PB * MPERF])
        attn = region(G, [PB, D])
        attnT = region(G + 1024, [KD, NPERF])
        sq = region(G + 4096, [2, KD * NPERF])
        kf = region(G + 4096, [H, PB * MPERF])
        qkT = region(G + 8192, [2, KD * NPERF])
        qfT = region(G + 10300, [H, PB * NPERF])
        v_perf = region(G + 16500, [PB, H, VA])
        kv_perf = region(G + 8192, [H, PB, VA])
        b_row = [region(1250 * i, [N]) for i in range(2)]
        b02_row = [region(2500 + 1250 * i, [N]) for i in range(2)]
        row2 = [region(5000 + 1250 * i, [N]) for i in range(4)]
        probT2 = [region(21570 + 1250 * i, [N]) for i in range(2)]
        mask = region(10120, [TILES, N], BF16)
        v_aug = region(16370, [TILES, H, VA])
        wb_row = region(21570, [D])
        ab_row = region(22100, [H])
        w_gat = region(G + 12348, [KD, H, DH])
        a_mul = [[region(1024 * i + 512 * r, [H, DH]) for r in range(2)] for i in range(2)]
        a_rows = region(G + 14400, [H, 2 * DH])
        k_part = [region(o, [KD, N], BF16) for o in (0, 2500, 21570)]
        q_part = [region(o, [KD, N], BF16) for o in (24070, 26570, 29070)]
        q12, q13, k11, k22, k31 = [[region(10120 + 3125 * b + 625 * i, [N], BF16) for b in range(2)] for i in range(5)]
        row3 = [region(5120 + 1250 * i, [N]) for i in range(2)]
        probT3 = [region(7620 + 1250 * i, [N]) for i in range(2)]
        mask3 = cnt[:, :, :].bitcast(BF16)
        w_k, w_q, w_v = [region(10120 + 2048 * i, [KD, D]) for i in range(3)]

        psW = [ctx.enter_context(nc.psum_tensor(f"wide{i}", [128, 1536], F32)) for i in range(2)]
        small = ctx.enter_context(nc.psum_tensor("small", [128, 1024], F32))
        psS = [small[:, 0:512], small[:, 512:1024]]

        def acc_view(ps):
            return ps[0:ROWS, 0:1024].rearrange("p (u c) -> p u c", u=2)[:, :, 0:HEAD_HALF * VA].rearrange(
                "p u (t d) -> p u t d", d=VA)

        names = """ident_set w_gat_in sel_set x_in edges_in vec_in w_in wv_in wo_in edges_f32 edges_turned
            edge_cols group_bounds bounds_turned bounds_set consts_set hot0_made hot1_made hot2_made hot3_made
            hot0_free hot1_free hot2_free hot3_free tile_counted counts_f32 counts_i16 counts_turning
            counts_turn_read deg_split deg_turned deg_row_out deg_wide ln_ready h_made h_turned hT_made
            x_plus_h h1_made h_split cT_wide cT_used lo_wide lo_made lo_used agg_full agg_read w_turned
            w_turn_read y_full y_out y_stats y_scaled z_turned x_updated bn1_ready qk_full qk_out v_full v_out
            proj_turned proj_out sq_made diag_full diag_out uk_full uk_max kmax_all kbias_set uk2_full kf_exp
            kf_made uq_full uq_max qf_exp qf_made qf_turned qfT_out kv_full kv_out at_full at_out at_turned
            atT_out o_full o_out conv_full conv_out wx_full wx_out wx_mul wx_mul2 ab_cols b_turned b_rows
            b_wide b_out acc_read score2_full relu2_made line2_made score2_read max2_made exp2_made prob2_made
            turned2 turned2_out used2 proj3_full proj3_1 proj3_rest proj3_2 proj3_out v3_full v3_out
            stack0_set stack1_set score3_full score3_read max3_made exp3_made prob3_made turned3 turned3_out
            used3 waits_taken var_ready root_out dve_done stored phase_done pool_done""".split()
        S = {n: sem(n) for n in names}
        block = ctx.enter_context(nc.Block())

        class Order:

            def __init__(self, eng, semaphore):
                self.eng, self.sem, self.base, self.n = eng, semaphore, 0, 0

            def __call__(self, ins):
                self.n += 1
                ins.then_inc(self.sem, 1)
                self.eng.wait_ge(self.sem, self.base + self.n)

        def phase_end(eng, n):
            eng.drain().then_inc(S["phase_done"], 1)
            eng.wait_ge(S["phase_done"], 5 * n)

        def after(eng, signal, count):
            if not isinstance(count, int) or count > 0:
                eng.wait_ge(S[signal], count)

        def split_cols(eng, done, dst, rest, src):
            part = [dst[:, i, :] if len(dst.shape) == 3 else dst[:, :, i, :] for i in range(3)]
            done(eng.tensor_copy(part[0], src))
            done(eng.tensor_tensor(rest, src, part[0], ALU.subtract))
            done(eng.tensor_copy(part[1], rest))
            return eng.tensor_tensor(part[2], rest, part[1], ALU.subtract)

        def has_big_count(eng):
            return eng.value_load(bounds_i[0:1, 3 * TILES:3 * TILES + 1], min_val=0, max_val=1)

        @block.sync
        def _(sp):
            col = "(k p) -> p k"
            sp.dma_start(e_raw[0:GROUPS, 0, :], a["dst"].rearrange("(p e) -> p e", p=GROUPS)).then_inc(S["edges_in"], 16)
            sp.dma_start(e_raw[0:GROUPS, 1, :], a["src"].rearrange("(p e) -> p e", p=GROUPS)).then_inc(S["edges_in"], 16)
            rows = "(k p) n -> p k n"
            sp.dma_start(w_nat[0], a["L0_gnn_W_l"].rearrange(rows, p=128)).then_inc(S["w_in"], 16)
            sp.dma_start(w_nat[1], a["L0_gnn_W_r"].rearrange(rows, p=128)).then_inc(S["w_in"], 16)
            for t in range(0, TILES, 5):
                sp.dma_start(x_nm[0:ROWS, t:t + 5, :], a["x"].rearrange("(t p) f -> p t f", p=ROWS)[:, t:t + 5, :]).then_inc(S["x_in"], 16)
            with nc.allow_non_contiguous_dma(reason="feature vectors as columns, 4 bytes a partition"):
                for i, name in enumerate(["L0_gnn_b_l", "L0_gnn_gamma", "L0_gnn_beta", "L1_gnn_norm1_g",
                                          "L1_gnn_norm1_b", "L1_gnn_norm2_g", "L1_gnn_norm2_b", "L1_gnn_b_conv"]):
                    sp.dma_start(vec[:, i, :], a[name].rearrange(col, p=128)).then_inc(S["vec_in"], 16)
            for r in range(2):
                sp.dma_start(proj_nat[:, :, DH * r:DH * r + DH],
                             a["L1_gnn_proj"].rearrange("(b m) d -> m b d", m=128)).then_inc(S["vec_in"], 16)
            phase_end(sp, 1)
            phase_end(sp, 2)
            sp.dma_start(w_a, a["L1_gnn_Wq"].rearrange(rows, p=128)).then_inc(S["w_in"], 16)
            sp.dma_start(w_b, a["L1_gnn_Wk"].rearrange(rows, p=128)).then_inc(S["w_in"], 16)
            sp.dma_start(wv, a["L1_gnn_Wv"].rearrange(rows, p=128)).then_inc(S["wv_in"], 16)
            sp.dma_start(wo, a["L1_gnn_Wo"].rearrange(rows, p=128)).then_inc(S["wo_in"], 16)
            phase_end(sp, 3)
            sp.dma_start(w_a, a["L1_gnn_W_conv"].rearrange(rows, p=128)).then_inc(S["w_in"], 16)
            for k in range(KD):
                sp.dma_start(w_gat[:, k, :, :], a["L2_gnn_Ws"][:, 128 * k:128 * k + 128, :].rearrange("h p d -> p h d")).then_inc(S["w_gat_in"], 16)
            phase_end(sp, 4)
            sp.dma_start(wb_row, a["L2_gnn_Wb"].rearrange("h d -> (h d)").partition_broadcast(128)).then_inc(S["w_in"], 16)
            sp.dma_start(a_rows.rearrange("p h d -> p (h d)"), a["L2_gnn_a_w"].rearrange("h d -> (h d)").partition_broadcast(128)).then_inc(S["w_in"], 16)
            sp.dma_start(ab_row, a["L2_gnn_a_b"].partition_broadcast(128)).then_inc(S["w_in"], 16)
            phase_end(sp, 5)
            phase_end(sp, 6)
            w3 = a["L3_gnn_W"].rearrange(rows, p=128)
            sp.dma_start(w_k, w3[:, :, D:2 * D]).then_inc(S["w_in"], 16)
            sp.dma_start(w_q, w3[:, :, 0:D]).then_inc(S["w_in"], 16)
            sp.dma_start(w_v, w3[:, :, 2 * D:3 * D]).then_inc(S["w_in"], 16)
            def stack(b, g):
                own = slice(DH * b, DH * b + DH)
                for dst, (top, low) in ((q12, (q_part[0], q_part[1])), (k11, (k_part[0], k_part[0])), (k22, (k_part[1], k_part[1])),
                                        (q13, (q_part[0], q_part[2])), (k31, (k_part[2], k_part[0]))):
                    sp.dma_start(dst[b][0:DH, :], top[own, g, :]).then_inc(S[f"stack{b}_set"], 16)
                    sp.dma_start(dst[b][DH:128, :], low[own, g, :]).then_inc(S[f"stack{b}_set"], 16)

            if layers >= 4:
                sp.wait_ge(S["proj3_out"], 2 * KD)
                stack(0, 0)
            phase_end(sp, 7)
            if layers >= 4:
                stack(1, 0)
                with sp.Fori(0, H // 2 - 1) as g:
                    for b in range(2):
                        sp.wait_ge(S["score3_full"], TILES * (2 * g + b + 1))
                        stack(b, g + 1)
            rows_out = out.rearrange("(t p) f -> p t f", p=ROWS)
            for n, part in ((2 * H - 1, slice(0, D - DH)), (2 * H, slice(D - DH, D))):
                if layers >= 4:
                    sp.wait_ge(S["acc_read"], n)
                sp.dma_start(rows_out[:, :, part], x_nm[0:ROWS, :, part]).then_inc(S["stored"], 16)
            phase_end(sp, 8)
            sp.wait_ge(S["stored"], 32)

        @block.gpsimd
        def _(pool):
            done = Order(pool, S["pool_done"])
            many = dict(allow_small_or_imprecise_dtypes=True, channel_multiplier=0)
            done(pool.memset(ident[:, :], 1.0))
            pool.affine_select(out=ident[:, :], in_=ident[:, :], compare_op=ALU.is_equal, fill=0.0, base=0,
                               pattern=[[-1, 128]], channel_multiplier=1).then_inc(S["ident_set"], 1)
            pool.iota(tile_lo, pattern=[[ROWS, TILES]], base=0, **many)
            pool.iota(up_row, pattern=[[1, GROUPS]], base=1, **many)
            done(pool.iota(down_row, pattern=[[-1, GROUPS]], base=GROUPS, **many))
            done(pool.memset(zero_bf[:, :], 0.0))
            pool.iota(iota_h[:, :], pattern=[[1, N]], base=0, **many).then_inc(S["consts_set"], 1)
            pool.memset(half_c[:, :], 0.5)
            done(pool.memset(sel[:, :, :], 0.0))
            for r in range(3):
                done(pool.affine_select(out=sel[:, :, :], in_=sel[:, :, :], compare_op=ALU.not_equal, fill=1.0, base=-r * TILES,
                                        pattern=[[-1, TILES], [0, 128]], channel_multiplier=1))
            pool.wait_ge(S["ident_set"], 1)
            pool.tensor_copy(ident_bf[:, :], ident[:, :]).then_inc(S["sel_set"], 1)
            for t in range(TILES):
                pool.wait_ge(S["counts_f32"], t + 1)
                pool.tensor_copy(cnt[0:ROWS, t, :], cnt_f[t % 2][0:ROWS, :]).then_inc(S["counts_i16"], 1)
            phase_end(pool, 1)

            for t in range(TILES):
                pool.wait_ge(S["h_made"], t + 1)
                pool.tensor_tensor(x_nm[0:ROWS, t, :], x_nm[0:ROWS, t, :], h32[t % RING][0:ROWS, :], ALU.add).then_inc(S["x_plus_h"], 1)
            phase_end(pool, 2)
            pool.wait_ge(S["uk_max"], H)
            pool.partition_all_reduce(kmaxa[:, :], kmax[:, :], 128, RMAX).then_inc(S["kmax_all"], 1)
            phase_end(pool, 3)
            phase_end(pool, 4)
            pool.memset(v_aug[0:ROWS, :, :, DH], 1.0)
            for t in range(TILES):
                pool.wait_ge(S["wx_out"], t + 1)
                if t >= 2:
                    pool.wait_ge(S["ab_cols"], t - 1)
                pool.tensor_tensor(a_mul[t % 2][0][0:ROWS, :, :], v_aug[0:ROWS, t, :, 0:DH], a_rows[0:ROWS, :, 0:DH],
                                   ALU.mult).then_inc(S["wx_mul"], 1)
            phase_end(pool, 5)

            phase_end(pool, 6)
            pool.memset(v_aug[0:ROWS, :, :, DH], 1.0)
            phase_end(pool, 7)

            phase_end(pool, 8)

        @block.scalar
        def _(act):
            def copy(dst, src, **k):
                return act.activation(dst, src, ACT.Copy, **k)

            for n in range(2 * KD):
                act.wait_ge(S["w_turned"], n + 1)
                w = (w_a, w_b)[n // KD]
                copy(w[:, n % KD, :], psW[n % 2][:, 512 * (n // 2 % 3):512 * (n // 2 % 3) + 512]).then_inc(S["w_turn_read"], 1)

            for t in range(TILES + 1):
                if t >= 1:
                    for r, (lo, hi) in enumerate(((0, 4), (4, 8), (8, 10))):
                        n = 3 * (t - 1) + r
                        act.wait_ge(S["counts_turning"], n + 1)
                        src = psS[n % 2][0:ROWS, 0:(hi - lo) * ROWS].rearrange("p (b c) -> p b c", b=hi - lo)
                        copy(cntT[0:ROWS, lo:hi, (t - 1) * ROWS:t * ROWS], src).then_inc(S["counts_turn_read"], 1)
                if t < TILES:
                    act.wait_ge(S["tile_counted"], t + 1)
                    if t >= 2:
                        act.wait_ge(S["counts_i16"], t - 1)
                        act.wait_ge(S["counts_turning"], 3 * (t - 1))
                    copy(cnt_f[t % 2][0:ROWS, :], psW[t % 2][0:ROWS, 0:N], accum_out=deg_col[0:ROWS, t:t + 1]).then_inc(S["counts_f32"], 1)
            act.wait_ge(S["deg_turned"], 1)
            copy(row_sb[:, 0, 0, :], psS[1][0:3 * TILES, 0:ROWS]).then_inc(S["deg_row_out"], 1)

            roots = [0]

            def take_root(rows, cols):
                roots[0] += 1
                act.wait_ge(S["var_ready"], roots[0])
                act.activation(root[0:rows, 0:cols], var_eps[0:rows, 0:cols], ACT.Sqrt).then_inc(S["root_out"], 1)

            def scale_y(func):
                for half in range(2):
                    nodes = slice(half * HEAD_HALF * ROWS, (half + 1) * HEAD_HALF * ROWS)
                    for f in range(KD):
                        act.activation(yT[:, f, nodes], yT[:, f, nodes], func, bias=shf[:, f:f + 1],
                                       scale=scl[:, f:f + 1]).then_inc(S["y_scaled"], 1)

            def upper_part(l, t):
                act.wait_ge(S["h_made"], TILES * l + t + 1)
                act.mul(h_pair[0][0:ROWS, t, :], h32[t % RING][0:ROWS, :], HS).then_inc(S["h1_made"], 1)

            def relu_norm(l):
                take_root(ROWS, TILES)
                act.wait_ge(S["ln_ready"], l + 1)
                for t in range(TILES):
                    if l < 2 and t >= RING:
                        act.wait_ge(S["h_turned"], TILES * l + t - RING + 1)
                        act.wait_ge(S["h_split"], TILES * l + t - RING + 1)
                        if l == 0:
                            act.wait_ge(S["x_plus_h"], t - RING + 1)
                    dst = h32[t % RING][0:ROWS, :] if l < 2 else h_nm[0:ROWS, t, :]
                    act.activation(dst, x_nm[0:ROWS, t, :], ACT.Relu, bias=nbias[0:ROWS, t:t + 1],
                                   scale=rstd[0:ROWS, t:t + 1]).then_inc(S["h_made"], 1)
                    if l < 2 and t >= 1:
                        upper_part(l, t - 1)
                if l < 2:
                    upper_part(l, TILES - 1)

            def widen(l, big):
                for half in range(2):
                    for j in range(TILES):
                        n = TILES * (2 * l + half) + j
                        if j >= 2:
                            act.wait_ge(S["cT_used"], n - 1)
                        elif n >= TILES:
                            act.wait_ge(S["agg_full"], 2 * l + half)
                        copy(cntT_16[j % 2][0:ROWS, :], cntT[0:ROWS, j, :]).then_inc(S["cT_wide"], 1)
                    with act.If(big > 0):
                        for j in range(TILES):
                            n = TILES * (2 * l + half) + j
                            if j >= 2:
                                act.wait_ge(S["lo_used"], n - 1)
                            else:
                                act.wait_ge(S["cT_used"], TILES * (2 * l + half) + TILES - 1 + j)
                            copy(cntT_16[j % 2][0:ROWS, :], cntT[0:ROWS, j, :]).then_inc(S["lo_wide"], 1)

            phase_end(act, 1)
            big = has_big_count(act)
            relu_norm(0)
            widen(0, big)
            act.wait_ge(S["vec_in"], 16 * 10)
            act.wait_ge(S["x_plus_h"], TILES)
            for f in range(KD):
                act.wait_ge(S["y_full"], f + 1)
                act.activation(yT[:, f, :], psW[f % 2][:, 0:N], ACT.Identity, bias=bl_c[:, f:f + 1]).then_inc(S["y_out"], 1)
            take_root(128, KD)
            act.wait_ge(S["y_stats"], 1)
            scale_y(ACT.Relu)
            phase_end(act, 2)
            if layers >= 2:
                relu_norm(1)
                take_root(128, KD)
                for r in range(2):
                    act.wait_ge(S["qk_full"], r + 1)
                    act.mul(qkT[:, r, :], psW[r][:, 0:KD * NPERF], DH ** -0.25).then_inc(S["qk_out"], 1)
                act.wait_ge(S["proj_turned"], 1)
                copy(projT[:, :], psW[1][:, 1024:1024 + MPERF]).then_inc(S["proj_out"], 1)
                act.wait_ge(S["kbias_set"], 1)
                for h in range(H):
                    act.wait_ge(S["uk2_full"], h + 1)
                    for b in range(PB):
                        e = act.activation(kf[:, h, MPERF * b:MPERF * b + MPERF], psW[h % 2][:, MPERF * b:MPERF * b + MPERF],
                                           ACT.Exp, bias=kbias[:, h, b:b + 1])
                    e.then_inc(S["kf_exp"], 1)
                for h in range(H):
                    act.wait_ge(S["uq_max"], h + 1)
                    for b in range(PB):
                        e = act.activation(qf[:, h, MPERF * b:MPERF * b + MPERF], psW[h % 2][:, MPERF * b:MPERF * b + MPERF],
                                           ACT.Exp, bias=qbias[:, h, b:b + 1])
                    e.then_inc(S["qf_exp"], 1)
                for h in range(H):
                    act.wait_ge(S["qf_turned"], h + 1)
                    copy(qfT[:, h, :], psS[h % 2][:, :]).then_inc(S["qfT_out"], 1)
                act.wait_ge(S["at_turned"], 1)
                copy(attnT.rearrange("p k n -> p (k n)"), psW[0][:, 0:KD * NPERF]).then_inc(S["atT_out"], 1)
                act.wait_ge(S["o_full"], 1)
                copy(oT.rearrange("p k n -> p (k n)"), psW[1][:, 0:KD * NPERF]).then_inc(S["o_out"], 1)
                phase_end(act, 3)
                widen(1, big)
                for f in range(KD):
                    act.wait_ge(S["conv_full"], f + 1)
                    act.activation(yT[:, f, :], psW[f % 2][:, 0:N], ACT.Relu, bias=bc_c[:, f:f + 1]).then_inc(S["conv_out"], 1)
                take_root(128, KD)
                act.wait_ge(S["y_stats"], 2)
                scale_y(ACT.Identity)
            else:
                phase_end(act, 3)
            phase_end(act, 4)
            if layers >= 3:
                relu_norm(2)
                phase_end(act, 5)

                def tables_in(h, b):
                    act.wait_ge(S["b_turned"], h + 1)
                    copy(row_sb[:, b, :, :].rearrange("p r c -> p (r c)"), psW[0][0:3 * TILES, 0:2 * ROWS]).then_inc(S["b_rows"], 1)

                def b_out(h, b):
                    act.wait_ge(S["b_wide"], h + 1)
                    blocks_out(copy, b_row[b][0:ROWS, :], psW[0], ROWS)
                    blocks_out(lambda d, s: act.mul(d, s, 0.2), b02_row[b][0:ROWS, :], psW[0], ROWS).then_inc(S["b_out"], 1)

                def positive_part(h, b, t):
                    act.activation(row2[(b * TILES + t) % 4][0:ROWS, :], b_row[b][0:ROWS, :], ACT.Relu, scale=0.8,
                                   bias=t08[0:ROWS, h, t:t + 1]).then_inc(S["relu2_made"], 1)

                def turned_out(layer, n, k, dst):
                    act.wait_ge(S[f"turned{layer}"], n + 1)
                    after(act, f"used{layer}", n - 1)
                    blocks_out(copy, dst[k % 2][0:ROWS, :], psW[1], ROWS).then_inc(S[f"turned{layer}_out"], 1)

                def head(h, b, first, last):
                    for t in range(TILES):
                        n, row = h * TILES + t, row2[(b * TILES + t) % 4][0:ROWS, :]
                        if t == 3 and not last:
                            tables_in(h + 1, 1 - b)
                        if t == 5 and not last:
                            b_out(h + 1, 1 - b)
                        if t % 2 == 1 and t < TILES - 1:
                            positive_part(h, b, t + 1)
                        elif t % 2 == 1 and not last:
                            positive_part(h + 1, 1 - b, 0)
                        if not (first and t < 2):
                            turned_out(2, n - 2, t, probT2)
                        act.wait_ge(S["max2_made"], n + 1)
                        act.activation(row, row, ACT.Exp, bias=neg_max[0:ROWS, t:t + 1]).then_inc(S["exp2_made"], 1)

                tables_in(0, 0)
                b_out(0, 0)
                act.wait_ge(S["b_out"], 1)
                positive_part(0, 0, 0)
                head(0, 0, True, False)
                with act.Fori(0, H // 2 - 1) as g:
                    head(2 * g + 1, 1, False, False)
                    head(2 * g + 2, 0, False, False)
                head(H - 1, 1, False, True)
                for t in range(2):
                    turned_out(2, H * TILES - 2 + t, t, probT2)
            else:
                phase_end(act, 5)
            phase_end(act, 6)
            if layers >= 4:
                relu_norm(3)
                for n in range(2 * KD):
                    part, scale = ((k_part, 1.0), (q_part, DH ** -0.5))[n // KD]
                    act.wait_ge(S["proj3_full"], n + 1)
                    act.mul(part[0][:, n % KD, :], psW[n % 2][:, 0:N], scale).then_inc(S["proj3_1"], 1)
                    act.wait_ge(S["proj3_rest"], n + 1)
                    copy(part[1][:, n % KD, :], psW[n % 2][:, 0:N]).then_inc(S["proj3_2"], 1)
                phase_end(act, 7)

                def head(h, first):
                    for t in range(TILES):
                        n = h * TILES + t
                        if not (first and t < 2):
                            turned_out(3, n - 2, t, probT3)
                        act.wait_ge(S["max3_made"], n + 1)
                        act.activation(row3[t % 2][0:ROWS, :], row3[t % 2][0:ROWS, :], ACT.Exp,
                                       bias=neg_max[0:ROWS, t:t + 1]).then_inc(S["exp3_made"], 1)

                head(0, True)
                with act.Fori(0, H - 1) as g:
                    head(g + 1, False)
                for t in range(2):
                    turned_out(3, H * TILES - 2 + t, t, probT3)
            else:
                phase_end(act, 7)
            phase_end(act, 8)

        @block.vector
        def _(dve):
            done = Order(dve, S["dve_done"])
            tt, ts, stt = dve.tensor_tensor, dve.tensor_scalar, dve.scalar_tensor_tensor

            def take_wait():
                dve.sem_inc(S["waits_taken"], 1)

            def x_stats(t):
                return dve.bn_stats(bn6[0:ROWS, t, :], x_nm[0:ROWS, t, :])

            dve.wait_ge(S["edges_in"], 32)
            dve.tensor_copy(e_f[0:GROUPS, :, :], e_raw[0:GROUPS, :, :]).then_inc(S["edges_f32"], 1)
            dve.wait_ge(S["edges_f32"], 1)
            dve.tensor_reduce(group_mm[0:GROUPS, 0:1], e_f[0:GROUPS, 0, :], AX, ALU.max)
            dve.tensor_reduce(group_mm[0:GROUPS, 1:2], e_f[0:GROUPS, 0, :], AX, ALU.min).then_inc(S["group_bounds"], 1)
            dve.wait_ge(S["edges_turned"], 1)
            src = psS[0][0:ROWS, 0:2 * CHUNKS * GROUPS].rearrange("e (s g p) -> e s p g", s=2, g=CHUNKS)
            for s in range(2):
                c = dve.tensor_copy(e_col[0:ROWS, s, :, :], src[:, s, :, :])
            c.then_inc(S["edge_cols"], 1)
            dve.wait_ge(S["bounds_turned"], 1)
            dve.wait_ge(S["consts_set"], 1)
            done(dve.tensor_copy(group_row, psS[1][0:1, 0:2 * GROUPS]))
            shape = [1, TILES, GROUPS]
            largest = group_row[:, 0:GROUPS].unsqueeze(1).to_broadcast(shape)
            smallest = group_row[:, GROUPS:2 * GROUPS].unsqueeze(1).to_broadcast(shape)
            up, down = (r.unsqueeze(1).to_broadcast(shape) for r in (up_row, down_row))
            lo, hi, tile_hi, n_groups, incl, excl, rest = (bnd[:, i, :] for i in range(7))
            done(ts(tile_hi, tile_lo, float(ROWS), None, ALU.add))
            done(tt(flag[0], largest, tile_lo.unsqueeze(2).to_broadcast(shape), ALU.is_ge))
            done(tt(flag[1], smallest, tile_hi.unsqueeze(2).to_broadcast(shape), ALU.is_lt))
            done(tt(flag[0], flag[0], flag[1], ALU.mult))
            done(tt(flag[1], flag[0], up, ALU.mult))
            done(dve.tensor_reduce(hi, flag[1], AX, ALU.max))
            done(tt(flag[1], flag[0], down, ALU.mult))
            done(dve.tensor_reduce(rest, flag[1], AX, ALU.max))
            done(ts(lo, rest, -1.0, float(GROUPS), ALU.mult, ALU.add))
            done(ts(hi, hi, 1.0, None, ALU.max))
            done(ts(rest, hi, -1.0, None, ALU.add))
            done(tt(lo, lo, rest, ALU.min))
            done(tt(n_groups, hi, lo, ALU.subtract))
            done(dve.tensor_copy(incl, n_groups))
            for t in range(1, TILES):
                done(tt(incl[:, t:t + 1], incl[:, t - 1:t], n_groups[:, t:t + 1], ALU.add))
            done(tt(excl, incl, n_groups, ALU.subtract))
            for i, r in enumerate((lo, excl, incl)):
                c = dve.tensor_copy(bounds_i[:, i * TILES:(i + 1) * TILES], r)
            c.then_inc(S["bounds_set"], 1)
            dve.wait_ge(S["bounds_set"], 1)
            for g in range(CHUNKS):
                dve.sem_inc(S[f"hot{g}_free"], 2)
            for t in range(TILES):
                if t == 1:
                    dve.wait_ge(S["x_in"], 32)
                if t >= 1:
                    x_stats(t - 1)
                first, start, end = (dve.value_load(bounds_i[0:1, i * TILES + t:i * TILES + t + 1], min_val=m,
                                                    max_val=TILES * GROUPS - (1 - m) if i else GROUPS - 1)
                                     for i, m in ((0, 0), (1, 0), (2, 1)))
                with dve.Fori(start, end) as n:
                    k = nc.s_assert_within(n - start + first, 0, GROUPS - 1,
                                           skip_runtime_bounds_check_because="first + (end - start) <= GROUPS by construction")
                    for g in range(CHUNKS):
                        dve.wait_ge(S[f"hot{g}_free"], n + 1)
                        ts(hot_src[0:ROWS, n % 2, g, :], iota_h[0:ROWS, :], e_col[0:ROWS, 1, k, g:g + 1], None, ALU.is_equal)
                        ts(hot_dst[0:ROWS, n % 2, g, 0:ROWS], iota_h[0:ROWS, t * ROWS:(t + 1) * ROWS],
                           e_col[0:ROWS, 0, k, g:g + 1], None, ALU.is_equal).then_inc(S[f"hot{g}_made"], 1)

            roots = [0]

            def rsqrt(dst, var):
                rows, cols = dst.shape
                ts(var_eps[0:rows, 0:cols], var, EPS, None, ALU.add).then_inc(S["var_ready"], 1)
                roots[0] += 1
                dve.wait_ge(S["root_out"], roots[0])
                done(dve.reciprocal(dst, root[0:rows, 0:cols]))

            def ln_stats(l):
                for t in range(0 if l == 3 else TILES - 1, TILES):
                    s = x_stats(t)
                done(s)
                for t in range(TILES):
                    s = dve.bn_aggr(mv[0:ROWS, t, :], bn6[0:ROWS, t, :])
                done(s)
                rsqrt(rstd[0:ROWS, :], mv[0:ROWS, :, 1])
                stt(nbias[0:ROWS, :], mv[0:ROWS, :, 0], -1.0, rstd[0:ROWS, :], ALU.mult, ALU.mult).then_inc(S["ln_ready"], 1)
                for t in range(TILES):
                    dve.wait_ge(S["h_turned"], TILES * l + t + 1)
                    dve.tensor_copy(hT[:, :, t * ROWS:(t + 1) * ROWS], psS[t % 2][:, 0:KD * ROWS].rearrange("p (k c) -> p k c", k=KD)).then_inc(S["hT_made"], 1)
                    if l < 2:
                        dve.wait_ge(S["h1_made"], TILES * l + t + 1)
                        stt(h_pair[1][0:ROWS, t, :], h32[t % RING][0:ROWS, :], HS, h_pair[0][0:ROWS, t, :], ALU.mult, ALU.subtract).then_inc(S["h_split"], 1)
                if l >= 2:
                    to, counts = ((mask, cnt), (mask3, cntT))[l - 2]
                    done(ts(to[0:ROWS, :, :], counts[0:ROWS, :, :], 0.0, NEG, ALU.is_equal, ALU.mult))

            def low_counts(l, half, big):
                with dve.If(big > 0):
                    for j in range(TILES):
                        dve.wait_ge(S["lo_wide"], TILES * (2 * l + half) + j + 1)
                        tt(cntT_16[j % 2][0:ROWS, :], cntT[0:ROWS, j, :], cntT_16[j % 2][0:ROWS, :], ALU.subtract).then_inc(S["lo_made"], 1)

            def bn_over_nodes(src, ready, gamma, beta, s_out, b_out):
                for f in range(KD):
                    ready(f)
                    for c, (lo, hi) in enumerate(((0, 512), (512, 1024), (1024, N))):
                        s = dve.bn_stats(bns[:, f, c, :], src[:, f, lo:hi])
                done(s)
                for f in range(KD):
                    s = dve.bn_aggr(bnv[:, f, :], bns[:, f, :, :].rearrange("p c s -> p (c s)"))
                done(s)
                rsqrt(s_out[:, :], bnv[:, :, 1])
                done(tt(s_out[:, :], s_out[:, :], gamma, ALU.mult))
                done(tt(b_out[:, :], bnv[:, :, 0], s_out[:, :], ALU.mult))
                return tt(b_out[:, :], beta, b_out[:, :], ALU.subtract)

            def add_back(base):
                for t in range(TILES):
                    dve.wait_ge(S["z_turned"], base + t + 1)
                    tt(x_nm[0:ROWS, t, :], x_nm[0:ROWS, t, :], psS[t % 2][0:ROWS, :], ALU.add).then_inc(S["x_updated"], 1)
                    if t >= 1:
                        dve.wait_ge(S["x_updated"], base + t)
                        x_stats(t - 1)
                dve.wait_ge(S["x_updated"], base + TILES)

            def sums(h, layer, steps):
                dve.wait_ge(S[f"used{layer + 2}"], steps)
                acc = acc_view(small)
                rd = rden[0:ROWS, :]
                rd2 = rd.rearrange("p (u t) -> p u t", u=2)
                done(ts(rd2, acc[:, :, :, DH], TINY, None, ALU.max))
                done(dve.reciprocal(rd, rd))
                done(tt(head_sum[0:ROWS, :, :, :], acc[:, :, :, 0:DH], rd2.unsqueeze(3).to_broadcast([ROWS, 2, HEAD_HALF, DH]), ALU.mult))
                xs = x_nm[0:ROWS, :, :].rearrange("p t (h d) -> p t h d", h=H)[:, :, h, :]
                tt(xs, xs, head_sum[0:ROWS, :, :, :].rearrange("p u t d -> p (u t) d"), ALU.add).then_inc(S["acc_read"], 1)

            dve.wait_ge(S["counts_f32"], TILES)
            split_cols(dve, done, parts[0:ROWS, :, :], split_rest[0:ROWS, 0, :], deg_col[0:ROWS, :]).then_inc(S["deg_split"], 1)
            dve.wait_ge(S["deg_wide"], 1)
            done(blocks_out(dve.tensor_copy, pos_b, psW[0], 128))
            done(dve.tensor_reduce(bnd[:, 0, 0:1], pos_b[0:1, :], AX, ALU.max))
            done(ts(bnd[:, 0, 0:1], bnd[:, 0, 0:1], EXACT16, None, ALU.is_gt))
            done(dve.tensor_copy(bounds_i[:, 3 * TILES:3 * TILES + 1], bnd[:, 0, 0:1]))
            phase_end(dve, 1)
            big = has_big_count(dve)
            ln_stats(0)
            done(ts(rdeg_b, pos_b, 1.0, None, ALU.max))
            done(dve.reciprocal(rdeg_b, rdeg_b))
            done(ts(rdeg_b, rdeg_b, 1.0 / HS, None, ALU.mult))
            done(ts(pos_b, pos_b, 1.0, None, ALU.min))
            for k in range(KD):
                if k % 2 == 0:
                    low_counts(0, k // 2, big)
                    dve.wait_ge(S["agg_full"], k // 2 + 1)
                tt(aggT[:, k, :], psW[k % 2][:, 0:N], rdeg_b, ALU.mult).then_inc(S["agg_read"], 1)
            dve.wait_ge(S["vec_in"], 16 * 10)
            bn_over_nodes(yT, lambda f: dve.wait_ge(S["y_out"], f + 1), ga0_c, be0_c, scl, shf).then_inc(S["y_stats"], 1)
            dve.wait_ge(S["x_plus_h"], TILES)
            add_back(0)
            phase_end(dve, 2)
            if layers >= 2:
                ln_stats(1)
                bn_over_nodes(hT, lambda f: dve.wait_ge(S["hT_made"], TILES * 2), g1_c, b1_c, scl1, shf1).then_inc(S["bn1_ready"], 1)
                done(dve.memset(v_perf[:, :, :, DH:VA], 1.0))
                dve.wait_ge(S["v_full"], 1)
                for b in range(PB):
                    c = dve.tensor_copy(v_perf[:, b, :, 0:DH], psS[b][:, :].rearrange("p (h d) -> p h d", h=H))
                c.then_inc(S["v_out"], 1)
                dve.wait_ge(S["qk_out"], 2)
                tt(sq, qkT, qkT, ALU.mult).then_inc(S["sq_made"], 1)
                dve.wait_ge(S["diag_full"], 1)
                for par in range(2):
                    for r, dst in enumerate((qdiag, kdiag)):
                        c = dve.tensor_copy(dst[:, par:H:2, :], psS[par][:, r * H:(r + 1) * H].rearrange("p (h b) -> p h b", b=PB))
                c.then_inc(S["diag_out"], 1)
                for h in range(H):
                    dve.wait_ge(S["uk_full"], h + 1)
                    dve.tensor_reduce(kmax[:, h:h + 1], psW[h % 2][:, 0:PB * MPERF], AX, ALU.max).then_inc(S["uk_max"], 1)
                dve.wait_ge(S["kmax_all"], 1)
                dve.wait_ge(S["diag_out"], 1)
                stt(kbias[:, :, :], kdiag[:, :, :], -1.0, kmaxa[:, :].unsqueeze(2).to_broadcast([128, H, PB]),
                    ALU.mult, ALU.subtract).then_inc(S["kbias_set"], 1)
                for h in range(H):
                    dve.wait_ge(S["kf_exp"], h + 1)
                    ts(kf[:, h, :], kf[:, h, :], MPERF ** -0.5, KEPS, ALU.mult, ALU.add).then_inc(S["kf_made"], 1)
                for h in range(H):
                    dve.wait_ge(S["uq_full"], h + 1)
                    done(dve.tensor_reduce(qmax[:, h, :], psW[h % 2][:, 0:PB * MPERF].rearrange("p (b m) -> p b m", b=PB), AX, ALU.max))
                    stt(qbias[:, h, :], qdiag[:, h, :], -1.0, qmax[:, h, :], ALU.mult, ALU.subtract).then_inc(S["uq_max"], 1)
                for h in range(H):
                    dve.wait_ge(S["qf_exp"], h + 1)
                    ts(qf[:, h, :], qf[:, h, :], MPERF ** -0.5, KEPS, ALU.mult, ALU.add).then_inc(S["qf_made"], 1)
                for h in range(H):
                    dve.wait_ge(S["kv_full"], h + 1)
                    dve.tensor_copy(kv_perf[:, h, :, :], psW[h % 2][:, 0:PB * VA].rearrange("p (b d) -> p b d", b=PB)).then_inc(S["kv_out"], 1)
                for h in range(H):
                    dve.wait_ge(S["at_full"], h + 1)
                    at = psW[h % 2][:, 512:512 + PB * VA].rearrange("p (b d) -> p b d", b=PB)
                    done(ts(pz[:, h, :], at[:, :, DH], KEPS, None, ALU.add))
                    done(dve.reciprocal(pz[:, h, :], pz[:, h, :]))
                    tt(attn[:, :, h * DH:(h + 1) * DH], at[:, :, 0:DH], pz[:, h, :].unsqueeze(2).to_broadcast([128, PB, DH]),
                       ALU.mult).then_inc(S["at_out"], 1)
                phase_end(dve, 3)
                for k in range(KD):
                    if k % 2 == 0:
                        low_counts(1, k // 2, big)
                        dve.wait_ge(S["agg_full"], 2 + k // 2 + 1)
                    done(stt(aggT[:, k, :], psW[k % 2][:, 0:N], scl1[:, k:k + 1], rdeg_b, ALU.mult, ALU.mult))
                    stt(aggT[:, k, :], pos_b, shf1[:, k:k + 1], aggT[:, k, :], ALU.mult, ALU.add).then_inc(S["agg_read"], 1)
                for f in range(KD):
                    tt(hT[:, f, 0:NPERF], hT[:, f, 0:NPERF], oT[:, f, :], ALU.add)
                    done(ts(hT[:, f, NPERF:N], hT[:, f, NPERF:N], oT[:, f, NPERF - 1:NPERF], None, ALU.add))

                def add_conv(f):
                    dve.wait_ge(S["conv_out"], f + 1)
                    done(tt(yT[:, f, :], yT[:, f, :], hT[:, f, :], ALU.add))

                bn_over_nodes(yT, add_conv, g2_c, b2_c, scl, shf).then_inc(S["y_stats"], 1)
                add_back(TILES)
            else:
                phase_end(dve, 3)
            phase_end(dve, 4)
            if layers >= 3:
                ln_stats(2)
                dve.wait_ge(S["w_in"], 16 * (5 + 3))

                def score_terms(t):
                    dve.wait_ge(S["wx_mul"], t + 1)
                    dve.tensor_reduce(tcol[0:ROWS, :, t], a_mul[t % 2][0][0:ROWS, :, :], AX, ALU.add)
                    dve.wait_ge(S["wx_mul2"], t + 1)
                    dve.tensor_reduce(bcol[0:ROWS, :, t], a_mul[t % 2][1][0:ROWS, :, :], AX, ALU.add).then_inc(S["ab_cols"], 1)

                for t in range(TILES):
                    dve.wait_ge(S["wx_full"], t + 1)
                    tt(v_aug[0:ROWS, t, :, 0:DH], psS[t % 2][0:ROWS, :].rearrange("p (h d) -> p h d", h=H),
                       wb_row[0:ROWS, :].rearrange("p (h d) -> p h d", h=H), ALU.add).then_inc(S["wx_out"], 1)
                    dve.wait_ge(S["wx_out"], t + 1)
                    tt(a_mul[t % 2][1][0:ROWS, :, :], v_aug[0:ROWS, t, :, 0:DH], a_rows[0:ROWS, :, DH:2 * DH], ALU.mult).then_inc(S["wx_mul2"], 1)
                    if t >= 1:
                        score_terms(t - 1)
                score_terms(TILES - 1)
                dve.wait_ge(S["ab_cols"], TILES)
                ts(b02[0:ROWS, :, :], bcol[0:ROWS, :, :], 0.2, None, ALU.mult)
                done(tt(tcol[0:ROWS, :, :], tcol[0:ROWS, :, :], ab_row[0:ROWS, :].unsqueeze(2).to_broadcast([ROWS, H, TILES]), ALU.add))
                done(ts(t08[0:ROWS, :, :], tcol[0:ROWS, :, :], 0.8, None, ALU.mult))
                for r, src in enumerate((bcol, b02)):
                    done(split_cols(dve, done, b_parts[0:ROWS, r, :, :, :], split_rest[0:ROWS, :, :], src[0:ROWS, :, :]))
                phase_end(dve, 5)

                def line(h, b, t):
                    n = h * TILES + t
                    after(dve, "turned2", n - 3)
                    stt(row2[(b * TILES + t) % 4][0:ROWS, :], b_row[b][0:ROWS, :], t08[0:ROWS, h, t:t + 1], b02_row[b][0:ROWS, :],
                        ALU.add, ALU.max).then_inc(S["line2_made"], 1)

                def probs(n, k, at):
                    dve.wait_ge(S["exp2_made"], n + 1)
                    tt(row2[at % 4][0:ROWS, :], row2[at % 4][0:ROWS, :], cnt[0:ROWS, k, :], ALU.mult).then_inc(S["prob2_made"], 1)

                def head(h, b, first):
                    for t in range(TILES):
                        n, row = h * TILES + t, row2[(b * TILES + t) % 4][0:ROWS, :]
                        if t % 2 == 0:
                            dve.wait_ge(S["relu2_made"], h * (TILES // 2) + t // 2 + 1)
                            dve.wait_ge(S["score2_full"], h * (TILES // 2) + t // 2 + 1)
                            terms = psW[0][0:ROWS, 0:N], row
                        else:
                            dve.wait_ge(S["line2_made"], h * (TILES // 2) + t // 2 + 1)
                            terms = row, mask[0:ROWS, t, :]
                        take_wait()
                        dve.tensor_tensor_reduce(row, *terms, 1.0, 2 * NEG, ALU.add, ALU.max,
                                                 mcol[0:ROWS, t:t + 1]).then_inc(S["score2_read"], 1)
                        dve.wait_ge(S["score2_read"], n + 1)
                        ts(neg_max[0:ROWS, t:t + 1], mcol[0:ROWS, t:t + 1], -1.0, None, ALU.mult).then_inc(S["max2_made"], 1)
                        if t % 2 == 0:
                            if t == 0:
                                dve.wait_ge(S["b_out"], h + 1)
                            line(h, b, t + 1)
                        if not (first and t == 0):
                            probs(n - 1, (t - 1) % TILES, b * TILES + t - 1)
                        if t == 2 and not first:
                            sums(h - 1, 0, n - 2)

                SUM_STEPS = 3
                head(0, 0, True)
                first = done.n
                with dve.Fori(0, H // 2 - 1) as g:
                    done.base = g * 2 * SUM_STEPS
                    head(2 * g + 1, 1, False)
                    head(2 * g + 2, 0, False)
                assert done.n - first == 2 * SUM_STEPS
                done.base, done.n = 0, first + 2 * SUM_STEPS * (H // 2 - 1)
                head(H - 1, 1, False)
                probs(H * TILES - 1, TILES - 1, 2 * TILES - 1)
                sums(H - 1, 0, H * TILES)
            else:
                phase_end(dve, 5)
            phase_end(dve, 6)
            if layers >= 4:
                ln_stats(3)
                for n in range(2 * KD):
                    part, scale = ((k_part, 1.0), (q_part, DH ** -0.5))[n // KD]
                    ps = psW[n % 2][:, 0:N]
                    dve.wait_ge(S["proj3_1"], n + 1)
                    stt(ps, ps, scale, part[0][:, n % KD, :], ALU.mult, ALU.subtract).then_inc(S["proj3_rest"], 1)
                    dve.wait_ge(S["proj3_2"], n + 1)
                    tt(part[2][:, n % KD, :], ps, part[1][:, n % KD, :], ALU.subtract).then_inc(S["proj3_out"], 1)
                for t in range(TILES):
                    dve.wait_ge(S["v3_full"], t + 1)
                    dve.tensor_copy(v_aug[0:ROWS, t, :, 0:DH], psS[t % 2][0:ROWS, :].rearrange("p (h d) -> p h d", h=H)).then_inc(S["v3_out"], 1)
                phase_end(dve, 7)

                def head3(h, first):
                    for t in range(TILES):
                        n, row = h * TILES + t, row3[t % 2][0:ROWS, :]
                        dve.wait_ge(S["score3_full"], n + 1)
                        take_wait()
                        dve.tensor_tensor_reduce(row, psW[0][0:ROWS, 0:N], mask3[0:ROWS, t, :], 1.0, 2 * NEG,
                                                 ALU.add, ALU.max, mcol[0:ROWS, t:t + 1]).then_inc(S["score3_read"], 1)
                        dve.wait_ge(S["score3_read"], n + 1)
                        ts(neg_max[0:ROWS, t:t + 1], mcol[0:ROWS, t:t + 1], -1.0, None, ALU.mult).then_inc(S["max3_made"], 1)
                        if t == 2 and not first:
                            sums(h - 1, 1, n - 2)
                        dve.wait_ge(S["exp3_made"], n + 1)
                        tt(row, row, cntT[0:ROWS, t, :], ALU.mult).then_inc(S["prob3_made"], 1)

                head3(0, True)
                first = done.n
                with dve.Fori(0, H - 1) as g:
                    done.base = g * SUM_STEPS
                    head3(g + 1, False)
                assert done.n - first == SUM_STEPS
                done.base, done.n = 0, first + SUM_STEPS * (H - 1)
                sums(H - 1, 1, H * TILES)
            else:
                phase_end(dve, 7)
            phase_end(dve, 8)

        @block.tensor
        def _(pe):
            def turn(dst, src, k):
                return pe.transpose(dst, src, ident[0:k, 0:k])

            def turn_parts(ps, src):
                return pe.matmul(ps[0:3 * TILES, 0:ROWS], src.rearrange("p r t -> p (r t)"), ident_bf[0:ROWS, 0:ROWS], start=True, stop=True)

            pe.wait_ge(S["ident_set"], 1)
            pe.wait_ge(S["edges_f32"], 1)
            for s in range(2):
                for g in range(CHUNKS):
                    at = (CHUNKS * s + g) * GROUPS
                    m = turn(psS[0][0:CHUNK, at:at + GROUPS], e_f[0:GROUPS, s, g * CHUNK:(g + 1) * CHUNK], GROUPS)
            m.then_inc(S["edges_turned"], 1)
            pe.wait_ge(S["group_bounds"], 1)
            for r in range(2):
                m = turn(psS[1][0:1, r * GROUPS:(r + 1) * GROUPS], group_mm[0:GROUPS, r:r + 1], GROUPS)
            m.then_inc(S["bounds_turned"], 1)
            pe.wait_ge(S["w_in"], 32)
            for n in range(2 * KD):
                if n >= 6:
                    pe.wait_ge(S["w_turn_read"], n - 5)
                w = w_nat[n // KD]
                for o in range(KD):
                    at = 512 * (n // 2 % 3) + 128 * o
                    m = turn(psW[n % 2][:, at:at + 128], w[:, o, 128 * (n % KD):128 * (n % KD) + 128], 128)
                m.then_inc(S["w_turned"], 1)
            pe.wait_ge(S["w_turn_read"], 2 * KD)
            pe.wait_ge(S["consts_set"], 1)
            pe.wait_ge(S["bounds_set"], 1)

            def turn_counts(t):
                pe.wait_ge(S["counts_f32"], t + 1)
                for r, (lo, hi) in enumerate(((0, 4), (4, 8), (8, 10))):
                    n = 3 * t + r
                    if n >= 2:
                        pe.wait_ge(S["counts_turn_read"], n - 1)
                    if n == 2:
                        pe.wait_ge(S["edge_cols"], 1)
                    for j in range(lo, hi):
                        m = turn(psS[n % 2][0:ROWS, (j - lo) * ROWS:(j - lo + 1) * ROWS], cnt_f[t % 2][0:ROWS, j * ROWS:(j + 1) * ROWS], ROWS)
                    m.then_inc(S["counts_turning"], 1)

            def zero_matmul(ps, start, stop):
                for lo, hi in ((0, 512), (512, 1024), (1024, N)):
                    mm = pe.matmul(ps[0:ROWS, lo:hi], zero_bf[:, 0:ROWS], zero_bf[:, 0:hi - lo], start=start, stop=stop)
                return mm

            for t in range(TILES):
                start, end = (pe.value_load(bounds_i[0:1, i * TILES + t:i * TILES + t + 1], min_val=i - 1,
                                            max_val=TILES * GROUPS) for i in (1, 2))
                if t >= 2:
                    pe.wait_ge(S["counts_f32"], t - 1)
                if t == 0:
                    pe.wait_ge(S["edge_cols"], 1)
                zero_matmul(psW[t % 2], True, False)
                with pe.Fori(start, end) as n:
                    for g in range(CHUNKS):
                        pe.wait_ge(S[f"hot{g}_made"], n + 1)
                        wide_matmul(pe, psW[t % 2], ROWS, hot_dst[0:ROWS, n % 2, g, 0:ROWS], hot_src[0:ROWS, n % 2, g, :], False, False).then_inc(S[f"hot{g}_free"], 1)
                zero_matmul(psW[t % 2], False, True).then_inc(S["tile_counted"], 1)
                if t >= 1:
                    turn_counts(t - 1)
            turn_counts(TILES - 1)
            pe.wait_ge(S["counts_turn_read"], 3 * TILES)
            pe.wait_ge(S["sel_set"], 1)
            pe.wait_ge(S["deg_split"], 1)
            turn_parts(psS[1], parts[0:ROWS, :, :]).then_inc(S["deg_turned"], 1)
            pe.wait_ge(S["deg_row_out"], 1)

            def spread(ps, row, signal):
                for t in range(TILES):
                    m = pe.matmul(block_at(ps, 128, t), sel[:, t, :], row, start=True, stop=True)
                m.then_inc(signal, 1)

            spread(psW[0], row_sb[:, 0, 0, :], S["deg_wide"])
            phase_end(pe, 1)

            def turn_h(l):
                for t in range(TILES):
                    pe.wait_ge(S["h_made"], TILES * l + t + 1)
                    if t >= 2:
                        pe.wait_ge(S["hT_made"], TILES * l + t - 1)
                    src = h32[t % RING] if l < 2 else h_nm[:, t, :]
                    for k in range(KD):
                        m = turn(psS[t % 2][:, k * ROWS:(k + 1) * ROWS], src[0:ROWS, 128 * k:128 * k + 128], ROWS)
                    m.then_inc(S["h_turned"], 1)

            def zero_all(ps, start, stop):
                for lo, hi in ((0, 512), (512, 1024), (1024, N)):
                    mm = pe.matmul(ps[:, lo:hi], zero_bf[:, 0:128], zero_bf[:, 0:hi - lo], start=start, stop=stop, skip_group_check=True)
                return mm

            def aggregate(l, big):
                def tile(half, j, start):
                    for kk in range(2):
                        k = 2 * half + kk
                        if start and half == 1:
                            pe.wait_ge(S["agg_read"], l * KD + kk + 1)
                        for part in h_pair:
                            m = wide_matmul(pe, psW[kk], 128, part[0:ROWS, j, 128 * k:128 * k + 128], cntT_16[j % 2][0:ROWS, :],
                                            start and part is h_pair[0], False)
                    return m

                pe.wait_ge(S["h_split"], TILES * (l + 1))
                for half in range(2):
                    first = TILES * (2 * l + half)
                    for j in range(TILES):
                        pe.wait_ge(S["cT_wide"], first + j + 1)
                        tile(half, j, j == 0).then_inc(S["cT_used"], 1)
                    with pe.If(big > 0):
                        for j in range(TILES):
                            pe.wait_ge(S["lo_made"], first + j + 1)
                            tile(half, j, False).then_inc(S["lo_used"], 1)
                    for kk in range(2):
                        m = zero_all(psW[kk], False, True)
                    m.then_inc(S["agg_full"], 1)

            def turn_back(base):
                for t in range(TILES):
                    if t % HEAD_HALF == 0:
                        pe.wait_ge(S["y_scaled"], KD * (2 * (base // TILES) + t // HEAD_HALF + 1))
                    if t >= 2:
                        pe.wait_ge(S["x_updated"], base + t - 1)
                    for k in range(KD):
                        m = turn(psS[t % 2][0:ROWS, 128 * k:128 * k + 128], yT[:, k, t * ROWS:(t + 1) * ROWS], 128)
                    m.then_inc(S["z_turned"], 1)

            big = has_big_count(pe)
            turn_h(0)
            aggregate(0, big)
            for f in range(KD):
                pe.wait_ge(*((S["y_out"], f - 1) if f >= 2 else (S["agg_read"], KD - 1 + f)))
                for k in range(2 * KD):
                    w, r = ((w_b, hT), (w_a, aggT))[k // KD]
                    if f == 0 and k == KD:
                        pe.wait_ge(S["agg_read"], KD)
                    m = wide_matmul(pe, psW[f % 2], 128, w[:, k % KD, 128 * f:128 * f + 128], r[:, k % KD, :], k == 0, k == 2 * KD - 1)
                m.then_inc(S["y_full"], 1)
            turn_back(0)
            phase_end(pe, 2)
            if layers >= 2:
                turn_h(1)
                pe.wait_ge(S["w_in"], 16 * 4)
                pe.wait_ge(S["hT_made"], TILES * 2)
                for r, w in enumerate((w_a, w_b)):
                    for f in range(KD):
                        for k in range(KD):
                            m = pe.matmul(psW[r][:, NPERF * f:NPERF * f + NPERF], w[:, k, 128 * f:128 * f + 128], hT[:, k, 0:NPERF],
                                          start=(k == 0), stop=(k == KD - 1))
                    m.then_inc(S["qk_full"], 1)
                pe.wait_ge(S["wv_in"], 16)
                for b in range(PB):
                    for k in range(KD):
                        m = pe.matmul(psS[b][:, :], hT[:, k, 128 * b:128 * b + 128], wv[:, k, :], start=(k == 0), stop=(k == KD - 1))
                m.then_inc(S["v_full"], 1)
                for b in range(PB):
                    m = turn(psW[1][:, 1024 + 128 * b:1024 + 128 * b + 128], proj_nat[:, b, :], 128)
                m.then_inc(S["proj_turned"], 1)
                pe.wait_ge(S["v_out"], 1)
                pe.wait_ge(S["sq_made"], 1)
                for par in range(2):
                    p = slice(DH * par, DH * par + DH)
                    for r in range(2):
                        for hh in range(H // 2):
                            for b in range(PB):
                                at = r * H + hh * PB + b
                                m = pe.matmul(psS[par][:, at:at + 1], sq[p, r, NPERF * hh + 128 * b:NPERF * hh + 128 * b + 128],
                                              half_c[p, :], start=True, stop=True)
                m.then_inc(S["diag_full"], 1)
                pe.wait_ge(S["proj_out"], 1)

                def features(r, h):
                    p = slice(DH * (h % 2), DH * (h % 2) + DH)
                    for b in range(PB):
                        at = NPERF * (h // 2) + 128 * b
                        m = pe.matmul(psW[h % 2][:, MPERF * b:MPERF * b + MPERF], qkT[p, r, at:at + 128], projT[p, :], start=True, stop=True)
                    return m

                for h in range(H):
                    if h >= 2:
                        pe.wait_ge(S["uk_max"], h - 1)
                    features(1, h).then_inc(S["uk_full"], 1)
                for h in range(H):
                    pe.wait_ge(*((S["uk_max"], H) if h < 2 else (S["kf_exp"], h - 1)))
                    features(1, h).then_inc(S["uk2_full"], 1)
                for h in range(H):
                    pe.wait_ge(*((S["kf_exp"], H) if h < 2 else (S["qf_exp"], h - 1)))
                    features(0, h).then_inc(S["uq_full"], 1)
                pe.wait_ge(S["kf_made"], H)
                pe.wait_ge(S["qf_exp"], H)
                for h in range(H):
                    if h >= 2:
                        pe.wait_ge(S["kv_out"], h - 1)
                    for mb in range(PB):
                        for b in range(PB):
                            m = pe.matmul(psW[h % 2][:, VA * mb:VA * mb + VA], kf[:, h, MPERF * b + 128 * mb:MPERF * b + 128 * mb + 128],
                                          v_perf[:, b, h, :], start=(b == 0), stop=(b == PB - 1))
                    m.then_inc(S["kv_full"], 1)
                pe.wait_ge(S["diag_out"], 1)
                for h in range(H):
                    pe.wait_ge(S["qf_made"], h + 1)
                    if h >= 2:
                        pe.wait_ge(S["qfT_out"], h - 1)
                    for mb in range(PB):
                        for b in range(PB):
                            m = turn(psS[h % 2][:, NPERF * mb + 128 * b:NPERF * mb + 128 * b + 128],
                                     qf[:, h, MPERF * b + 128 * mb:MPERF * b + 128 * mb + 128], 128)
                    m.then_inc(S["qf_turned"], 1)
                pe.wait_ge(S["qfT_out"], H)
                for h in range(H):
                    pe.wait_ge(S["kv_out"], h + 1)
                    if h >= 2:
                        pe.wait_ge(S["at_out"], h - 1)
                    for b in range(PB):
                        for mb in range(PB):
                            m = pe.matmul(psW[h % 2][:, 512 + VA * b:512 + VA * b + VA], qfT[:, h, NPERF * mb + 128 * b:NPERF * mb + 128 * b + 128],
                                          kv_perf[:, h, mb, :], start=(mb == 0), stop=(mb == PB - 1))
                    m.then_inc(S["at_full"], 1)
                pe.wait_ge(S["at_out"], H)
                for k in range(KD):
                    for b in range(PB):
                        m = turn(psW[0][:, NPERF * k + 128 * b:NPERF * k + 128 * b + 128], attn[:, b, 128 * k:128 * k + 128], 128)
                m.then_inc(S["at_turned"], 1)
                pe.wait_ge(S["atT_out"], 1)
                pe.wait_ge(S["wo_in"], 16)
                for f in range(KD):
                    for k in range(KD):
                        m = pe.matmul(psW[1][:, NPERF * f:NPERF * f + NPERF], wo[:, k, 128 * f:128 * f + 128], attnT[:, k, :],
                                      start=(k == 0), stop=(k == KD - 1))
                m.then_inc(S["o_full"], 1)
                phase_end(pe, 3)
                aggregate(1, big)
                pe.wait_ge(S["w_in"], 16 * 5)
                for f in range(KD):
                    if f >= 2:
                        pe.wait_ge(S["conv_out"], f - 1)
                    if f == 0:
                        pe.wait_ge(S["agg_read"], 2 * KD - 1)
                    for k in range(KD):
                        if f == 0 and k == KD - 1:
                            pe.wait_ge(S["agg_read"], 2 * KD)
                        m = wide_matmul(pe, psW[f % 2], 128, w_a[:, k, 128 * f:128 * f + 128], aggT[:, k, :], k == 0, k == KD - 1)
                    m.then_inc(S["conv_full"], 1)
                turn_back(TILES)
            else:
                phase_end(pe, 3)
            phase_end(pe, 4)
            if layers >= 3:
                turn_h(2)
                pe.wait_ge(S["hT_made"], TILES * 3)
                pe.wait_ge(S["w_gat_in"], 16 * KD)
                for t in range(TILES):
                    if t >= 2:
                        pe.wait_ge(S["wx_out"], t - 1)
                    for k in range(KD):
                        m = pe.matmul(psS[t % 2][0:ROWS, :], hT[:, k, t * ROWS:(t + 1) * ROWS],
                                      w_gat[:, k, :, :].rearrange("p h d -> p (h d)"), start=(k == 0), stop=(k == KD - 1))
                    m.then_inc(S["wx_full"], 1)
                phase_end(pe, 5)

                def tables(h):
                    for r in range(2):
                        m = turn_parts(psW[0][:, r * ROWS:(r + 1) * ROWS], b_parts[0:ROWS, r, h, :, :])
                    m.then_inc(S["b_turned"], 1)

                def b_spread(h, b):
                    pe.wait_ge(S["b_rows"], h + 1)
                    spread(psW[0], row_sb[:, b, 0, :], S["b_wide"])

                def score(b, t):
                    for lo, hi in pieces:
                        j = lo // ROWS
                        pe.matmul(psW[0][0:ROWS, lo:hi], sel[:, j, 0:ROWS], row_sb[:, b, 1, lo - j * ROWS:hi - j * ROWS],
                                  start=lo in (0, 512, 1024), stop=False, skip_group_check=True)
                    wide_matmul(pe, psW[0], ROWS, ident_bf[0:ROWS, 0:ROWS], mask[0:ROWS, t, :], False, True).then_inc(S["score2_full"], 1)

                def turn_probs(layer, n, row):
                    pe.wait_ge(S[f"prob{layer}_made"], n + 1)
                    after(pe, f"turned{layer}_out", n)
                    for j in range(TILES):
                        m = turn(block_at(psW[1], ROWS, j), row[0:ROWS, j * ROWS:(j + 1) * ROWS], ROWS)
                    m.then_inc(S[f"turned{layer}"], 1)

                def weigh(layer, h, n, k, probT):
                    pe.wait_ge(S[f"turned{layer}_out"], n + 1)
                    if k == 0:
                        after(pe, "acc_read", H * (layer - 2) + h)
                    for j in range(TILES):
                        m = pe.matmul(acc_view(small)[:, k // HEAD_HALF, k % HEAD_HALF, :], probT[k % 2][0:ROWS, j * ROWS:(j + 1) * ROWS],
                                      v_aug[0:ROWS, j, h, :], start=(j == 0), stop=(j == TILES - 1))
                    m.then_inc(S[f"used{layer}"], 1)

                def head(h, b, first, last):
                    for t in range(TILES):
                        n = h * TILES + t
                        if not (first and t < 2):
                            turn_probs(2, n - 2, row2[(b * TILES + t - 2) % 4])
                        if t % 2 == 1 and not (last and t == TILES - 1):
                            if t in (3, 5) and not last:
                                pe.wait_ge(S["b_rows" if t == 3 else "b_out"], h + 2)
                            else:
                                pe.wait_ge(S["score2_read"], n)
                            score(b if t < TILES - 1 else 1 - b, (t + 1) % TILES)
                        if not (first and t < 3):
                            weigh(2, h if t >= 3 else h - 1, n - 3, (t - 3) % TILES, probT2)
                        if t in (2, 4) and not last:
                            pe.wait_ge(S["score2_read"], n + 1)
                            tables(h + 1) if t == 2 else b_spread(h + 1, 1 - b)

                cuts = sorted({512, 1024, *range(0, N + 1, ROWS)})
                pieces = list(zip(cuts, cuts[1:]))
                tables(0)
                b_spread(0, 0)
                pe.wait_ge(S["b_out"], 1)
                score(0, 0)
                head(0, 0, True, False)
                with pe.Fori(0, H // 2 - 1) as g:
                    head(2 * g + 1, 1, False, False)
                    head(2 * g + 2, 0, False, False)
                head(H - 1, 1, False, True)
                for n in range(H * TILES, H * TILES + 3):
                    if n < H * TILES + 2:
                        turn_probs(2, n - 2, row2[(n - 2) % 4])
                    weigh(2, H - 1, n - 3, n - 3 - (H - 1) * TILES, probT2)
            else:
                phase_end(pe, 5)
            phase_end(pe, 6)
            if layers >= 4:
                turn_h(3)
                pe.wait_ge(S["hT_made"], TILES * 4)
                pe.wait_ge(S["w_in"], 16 * (5 + 6))
                for n in range(2 * KD):
                    if n >= 2:
                        pe.wait_ge(S["proj3_out"], n - 1)
                    w = (w_k, w_q)[n // KD]
                    for k in range(KD):
                        m = wide_matmul(pe, psW[n % 2], 128, w[:, k, 128 * (n % KD):128 * (n % KD) + 128], hT[:, k, :], k == 0, k == KD - 1)
                    m.then_inc(S["proj3_full"], 1)
                for t in range(TILES):
                    if t >= 2:
                        pe.wait_ge(S["v3_out"], t - 1)
                    for k in range(KD):
                        m = pe.matmul(psS[t % 2][0:ROWS, :], hT[:, k, t * ROWS:(t + 1) * ROWS], w_v[:, k, :], start=(k == 0), stop=(k == KD - 1))
                    m.then_inc(S["v3_full"], 1)
                phase_end(pe, 7)
                def head(h, b, g, first):
                    pe.wait_ge(S[f"stack{b}_set"], 160 * (g + 1))
                    for t in range(TILES):
                        n = h * TILES + t
                        if not (first and t < 2):
                            turn_probs(3, n - 2, row3[t % 2])
                        after(pe, "score3_read", n)
                        own = slice(t * ROWS, (t + 1) * ROWS)
                        for queries, keys in ((q12, k11), (q12, k22), (q13, k31)):
                            m = wide_matmul(pe, psW[0], ROWS, queries[b][:, own], keys[b], keys is k11, keys is k31)
                        m.then_inc(S["score3_full"], 1)
                        if not (first and t < 3):
                            weigh(3, h if t >= 3 else h - 1, n - 3, (t - 3) % TILES, probT3)

                head(0, 0, 0, True)
                with pe.Fori(0, H // 2 - 1) as g:
                    head(2 * g + 1, 1, g, False)
                    head(2 * g + 2, 0, g + 1, False)
                head(H - 1, 1, H // 2 - 1, False)
                for n in range(H * TILES, H * TILES + 3):
                    if n < H * TILES + 2:
                        turn_probs(3, n - 2, row3[n % 2])
                    weigh(3, H - 1, n - 3, n - 3 - (H - 1) * TILES, probT3)
            else:
                phase_end(pe, 7)
            phase_end(pe, 8)


INS = ["x", "src", "dst", "L0_gnn_W_l", "L0_gnn_b_l", "L0_gnn_W_r", "L0_gnn_gamma", "L0_gnn_beta", "L1_gnn_norm1_g",
       "L1_gnn_norm1_b", "L1_gnn_norm2_g", "L1_gnn_norm2_b", "L1_gnn_W_conv", "L1_gnn_b_conv", "L1_gnn_Wq", "L1_gnn_Wk",
       "L1_gnn_Wv", "L1_gnn_Wo", "L1_gnn_proj", "L2_gnn_Ws", "L2_gnn_Wb", "L2_gnn_a_w", "L2_gnn_a_b", "L3_gnn_W"]


def kernel(**inputs):
    import numpy as np
    import concourse.bacc as bacc
    from concourse.bass_utils import run_bass_kernel_spmd as run

    nc = bacc.Bacc("TRN2", target_bir_lowering=False, num_devices=1)
    arrays, aps = {}, {}
    for name in INS:
        arr = np.ascontiguousarray(inputs[name])
        arrays[f"in_{name}"] = arr
        aps[name] = nc.dram_tensor(f"in_{name}", arr.shape, mybir.dt.from_np(arr.dtype), kind="ExternalInput").ap()
    out = nc.dram_tensor("out", (N, D), F32, kind="ExternalOutput").ap()
    gnn_program(nc, aps, out)
    r = run(nc, [arrays], core_ids=[0])
    return r.results[0]["out"]
```
